# Optimizing a Trainium2 kernel written in Bass

```python
import numpy as np
import jax
import jax.numpy as jnp

def _softmax(x, axis=-1):
    return jax.nn.softmax(x, axis=axis)

def _gelu(x):
    return jax.nn.gelu(x, approximate=True)

def _silu(x):
    return jax.nn.silu(x)

def _sigmoid(x):
    return jax.nn.sigmoid(x)

def _layernorm(x, axis=-1, eps=1e-05):
    m = jnp.mean(x, axis=axis, keepdims=True)
    v = jnp.var(x, axis=axis, keepdims=True)
    return (x - m) / jnp.sqrt(v + eps)

def _scatter_add(tgt, idx, src, axis=0):
    return tgt.at[idx].add(src)

def _segment_sum(src, seg, n):
    return jax.ops.segment_sum(src, seg, n)
kernel_name = 'mk_gnn_preln_d4_gnn_r32_eeee7d'

def setup_inputs(seed: int=0):
    np.random.seed(seed)
    _w = jnp.asarray

    def _rec_inputs():
        import jax
        import jax.numpy as jnp
        _gk = jax.random.key(seed)
        x = -0.0009044 + 1 * jax.random.normal(jax.random.fold_in(_gk, 1), (3125, 32), jnp.float32)
        src = jax.random.randint(jax.random.fold_in(_gk, 2), (100000,), 0, 3125, jnp.int32)
        dst = jax.random.randint(jax.random.fold_in(_gk, 3), (100000,), 0, 3125, jnp.int32)
        _o = jnp.argsort(dst, stable=True)
        src = src[_o]
        dst = dst[_o]
        edge_attr_3 = jax.random.uniform(jax.random.fold_in(_gk, 11), (100000, 3), jnp.float32, 0.0, 1)
        return (x, src, dst, edge_attr_3)
    x, src, dst, edge_attr_3 = _rec_inputs()

    def _L0_gnn_setup():
        import jax, jax.numpy as jnp
        import numpy as np
        N_NODES = 50000
        DEG = 16
        N_HEAD = 4
        F_IN = 32
        F_OUT = 32
        key = jax.random.key(seed)
        k_h, k_w, k_fw, k_fb = jax.random.split(key, 4)
        h = jax.random.normal(k_h, (N_NODES, F_IN), dtype=jnp.float32)
        src = jnp.repeat(jnp.arange(N_NODES, dtype=jnp.int64), DEG)
        offs = (jnp.arange(DEG, dtype=jnp.int64) + 1) * 97
        dst = (src.reshape(N_NODES, DEG) + offs[None, :]).reshape(-1) % N_NODES
        edge_index = jnp.stack([src, dst], axis=0)
        gain = 1.414
        bound_w = gain * np.sqrt(6.0 / (F_IN + F_OUT))
        w = jax.random.uniform(k_w, (N_HEAD, F_IN, F_OUT), jnp.float32, -bound_w, bound_w)
        bound_fc = np.sqrt(1.0 / (2 * F_OUT))
        fc_w = jax.random.uniform(k_fw, (1, 2 * F_OUT), jnp.float32, -bound_fc, bound_fc)
        fc_b = jax.random.uniform(k_fb, (1,), jnp.float32, -bound_fc, bound_fc)
        bias = jnp.zeros((F_OUT,), jnp.float32)
        return {'h': h, 'edge_index': edge_index, 'w': w, 'fc_w': fc_w, 'fc_b': fc_b, 'bias': bias}
    _L0_gnn_all = _L0_gnn_setup()
    _L0_gnn_in = {k: v for k, v in _L0_gnn_all.items() if k in ('w', 'fc_w', 'fc_b', 'bias')}
    del _L0_gnn_all

    def _L1_gnn_setup():
        import jax, jax.numpy as jnp
        import numpy as np
        N_NODES = 3125
        N_EDGES = 100000
        D_IN = 32
        N_HEADS = 4
        D_HEAD = 8
        key = jax.random.key(seed)
        k1, k2, k3, k4, k5, k6, k7 = jax.random.split(key, 7)
        scale = 1.0 / np.sqrt(D_IN)
        x = jax.random.normal(k1, (N_NODES, D_IN), dtype=jnp.float32)
        Wq = jax.random.normal(k2, (D_IN, N_HEADS * D_HEAD), dtype=jnp.float32) * scale
        Wk = jax.random.normal(k3, (D_IN, N_HEADS * D_HEAD), dtype=jnp.float32) * scale
        Wv = jax.random.normal(k4, (D_IN, N_HEADS * D_HEAD), dtype=jnp.float32) * scale
        Wo = jax.random.normal(k5, (N_HEADS * D_HEAD, D_IN), dtype=jnp.float32) * scale
        src = jax.random.randint(k6, (N_EDGES,), 0, N_NODES)
        dst = jax.random.randint(k7, (N_EDGES,), 0, N_NODES)
        edge_index = jnp.stack([src, dst], axis=0).astype(jnp.int64)
        return {'x': x, 'Wq': Wq, 'Wk': Wk, 'Wv': Wv, 'Wo': Wo, 'edge_index': edge_index}
    _L1_gnn_all = _L1_gnn_setup()
    _L1_gnn_in = {k: v for k, v in _L1_gnn_all.items() if k in ('Wq', 'Wk', 'Wv', 'Wo')}
    del _L1_gnn_all

    def _L2_gnn_setup():
        import jax, jax.numpy as jnp
        import numpy as np
        N = 50000
        E = 50000
        C = 32
        KS = 4
        DIM = 3
        K3 = KS ** DIM
        NEG = 0.01
        EPS = 1e-05
        _BITS = np.array([[s >> d & 1 for d in range(DIM)] for s in range(2 ** DIM)], dtype=np.int32)

        def _basis(edge_attr):
            v = edge_attr * (KS - 1)
            lo = jnp.floor(v)
            f = v - lo
            lo = lo.astype(jnp.int32)
            bits = jnp.asarray(_BITS)
            idx = jnp.clip(lo[:, None, :] + bits[None], 0, KS - 1)
            w = jnp.where(bits[None] == 1, f[:, None, :], 1.0 - f[:, None, :])
            basis = jnp.prod(w, axis=-1)
            wi = idx[..., 0] + KS * idx[..., 1] + KS * KS * idx[..., 2]
            return (basis, wi)

        def _sconv(x, src, dst, basis, wi, W, R, b):
            n = x.shape[0]
            z = jnp.einsum('nc,kco->nko', x, W)
            msg = jnp.zeros((src.shape[0], W.shape[2]), x.dtype)
            for s in range(basis.shape[1]):
                msg = msg + basis[:, s, None] * z[src, wi[:, s]]
            agg = jax.ops.segment_sum(msg, dst, num_segments=n)
            cnt = jax.ops.segment_sum(jnp.ones((dst.shape[0],), x.dtype), dst, num_segments=n)
            agg = agg / jnp.clip(cnt, 1.0)[:, None]
            return agg + x @ R + b

        def _bn(x, g, be):
            mu = x.mean(0)
            var = x.var(0)
            return (x - mu) * jax.lax.rsqrt(var + EPS) * g + be

        def _leaky(x):
            return jnp.where(x >= 0, x, NEG * x)
        key = jax.random.key(seed)
        ks = jax.random.split(key, 32)
        inp = {'patch_embs': jax.random.normal(ks[0], (N, C), jnp.float32), 'edge_index': jax.random.randint(ks[1], (2, E), 0, N, jnp.int32), 'edge_attr': jax.random.uniform(ks[2], (E, DIM), jnp.float32)}
        i = 3
        for l in (1, 2, 3):
            inp[f'W{l}'] = jax.random.normal(ks[i], (K3, C, C), jnp.float32) * 0.05
            i += 1
            inp[f'R{l}'] = jax.random.normal(ks[i], (C, C), jnp.float32) * 0.1
            i += 1
            inp[f'b{l}'] = jnp.zeros((C,), jnp.float32)
            inp[f'g{l}'] = jnp.ones((C,), jnp.float32)
            inp[f'be{l}'] = jnp.zeros((C,), jnp.float32)
        return inp
    _L2_gnn_all = _L2_gnn_setup()
    _L2_gnn_in = {k: v for k, v in _L2_gnn_all.items() if k in ('W1', 'R1', 'b1', 'g1', 'be1', 'W2', 'R2', 'b2', 'g2', 'be2', 'W3', 'R3', 'b3', 'g3', 'be3')}
    del _L2_gnn_all

    def _L3_gnn_setup():
        import jax, jax.numpy as jnp
        import numpy as np
        N_NODES = 50000
        N_EDGES = 25000
        FEAT = 32
        HEADS = 4
        key = jax.random.key(seed)
        ks = jax.random.split(key, 6)
        s = 1.0 / np.sqrt(FEAT)
        x = jax.random.normal(ks[0], (N_NODES, FEAT), dtype=jnp.float32)
        edge_index = jax.random.randint(ks[1], (2, N_EDGES), 0, N_NODES, dtype=jnp.int32)
        Wq = jax.random.normal(ks[2], (HEADS, FEAT, FEAT), dtype=jnp.float32) * s
        Wk = jax.random.normal(ks[3], (HEADS, FEAT, FEAT), dtype=jnp.float32) * s
        Wv = jax.random.normal(ks[4], (HEADS, FEAT, FEAT), dtype=jnp.float32) * s
        Wout = jax.random.normal(ks[5], (FEAT, FEAT), dtype=jnp.float32) * s
        return {'x': x, 'edge_index': edge_index, 'Wq': Wq, 'Wk': Wk, 'Wv': Wv, 'Wout': Wout}
    _L3_gnn_all = _L3_gnn_setup()
    _L3_gnn_in = {k: v for k, v in _L3_gnn_all.items() if k in ('Wq', 'Wk', 'Wv', 'Wout')}
    del _L3_gnn_all
    return {'x': x, 'src': src, 'dst': dst, 'edge_attr_3': edge_attr_3, 'L0_gnn_w': _L0_gnn_in['w'], 'L0_gnn_fc_w': _L0_gnn_in['fc_w'], 'L0_gnn_fc_b': _L0_gnn_in['fc_b'], 'L0_gnn_bias': _L0_gnn_in['bias'], 'L1_gnn_Wq': _L1_gnn_in['Wq'], 'L1_gnn_Wk': _L1_gnn_in['Wk'], 'L1_gnn_Wv': _L1_gnn_in['Wv'], 'L1_gnn_Wo': _L1_gnn_in['Wo'], 'L2_gnn_W1': _L2_gnn_in['W1'], 'L2_gnn_R1': _L2_gnn_in['R1'], 'L2_gnn_b1': _L2_gnn_in['b1'], 'L2_gnn_g1': _L2_gnn_in['g1'], 'L2_gnn_be1': _L2_gnn_in['be1'], 'L2_gnn_W2': _L2_gnn_in['W2'], 'L2_gnn_R2': _L2_gnn_in['R2'], 'L2_gnn_b2': _L2_gnn_in['b2'], 'L2_gnn_g2': _L2_gnn_in['g2'], 'L2_gnn_be2': _L2_gnn_in['be2'], 'L2_gnn_W3': _L2_gnn_in['W3'], 'L2_gnn_R3': _L2_gnn_in['R3'], 'L2_gnn_b3': _L2_gnn_in['b3'], 'L2_gnn_g3': _L2_gnn_in['g3'], 'L2_gnn_be3': _L2_gnn_in['be3'], 'L3_gnn_Wq': _L3_gnn_in['Wq'], 'L3_gnn_Wk': _L3_gnn_in['Wk'], 'L3_gnn_Wv': _L3_gnn_in['Wv'], 'L3_gnn_Wout': _L3_gnn_in['Wout']}

def reference(x, src, dst, edge_attr_3, L0_gnn_w, L0_gnn_fc_w, L0_gnn_fc_b, L0_gnn_bias, L1_gnn_Wq, L1_gnn_Wk, L1_gnn_Wv, L1_gnn_Wo, L2_gnn_W1, L2_gnn_R1, L2_gnn_b1, L2_gnn_g1, L2_gnn_be1, L2_gnn_W2, L2_gnn_R2, L2_gnn_b2, L2_gnn_g2, L2_gnn_be2, L2_gnn_W3, L2_gnn_R3, L2_gnn_b3, L2_gnn_g3, L2_gnn_be3, L3_gnn_Wq, L3_gnn_Wk, L3_gnn_Wv, L3_gnn_Wout):
    import jax
    import jax.numpy as jnp

    def _L0_gnn_ref(h, edge_index, w, fc_w, fc_b, bias):
        import jax, jax.numpy as jnp
        import numpy as np
        N_NODES = 50000
        DEG = 16
        N_HEAD = 4
        F_IN = 32
        F_OUT = 32
        n_head, f_in, f_out = w.shape
        n = h.shape[0]
        src, dst = (edge_index[0], edge_index[1])
        hp = jnp.einsum('nf,hfo->hno', h, w)
        w_src = fc_w[0, :f_out]
        w_dst = fc_w[0, f_out:]
        a_src = jnp.einsum('hnf,f->hn', hp, w_src)
        a_dst = jnp.einsum('hnf,f->hn', hp, w_dst)
        e = a_src[:, src] + a_dst[:, dst] + fc_b[0]
        e = jax.nn.leaky_relu(e, negative_slope=0.2)
        seg_max = jax.ops.segment_max(e.T, src, num_segments=n)
        e = jnp.exp(e - seg_max.T[:, src])
        seg_sum = jax.ops.segment_sum(e.T, src, num_segments=n)
        att = e / seg_sum.T[:, src]
        msg = att[:, :, None] * hp[:, dst, :]
        agg = jax.vmap(lambda m: jax.ops.segment_sum(m, src, num_segments=n))(msg)
        out = agg.mean(axis=0) + bias
        return out

    def _L1_gnn_ref(x, Wq, Wk, Wv, Wo, edge_index):
        import jax, jax.numpy as jnp
        import numpy as np
        N_NODES = 3125
        N_EDGES = 100000
        D_IN = 32
        N_HEADS = 4
        D_HEAD = 8
        N = x.shape[0]
        src, dst = (edge_index[0], edge_index[1])
        q = (x @ Wq).reshape(N, N_HEADS, D_HEAD)
        k = (x @ Wk).reshape(N, N_HEADS, D_HEAD)
        v = (x @ Wv).reshape(N, N_HEADS, D_HEAD)
        inv_sqrt_d = jnp.asarray(1.0 / np.sqrt(D_HEAD), dtype=x.dtype)
        scores = jnp.einsum('ehd,ehd->eh', q[dst], k[src]) * inv_sqrt_d
        m = jax.ops.segment_max(scores, dst, num_segments=N)
        m = jnp.where(jnp.isfinite(m), m, jnp.zeros_like(m))
        e = jnp.exp(scores - m[dst])
        denom = jax.ops.segment_sum(e, dst, num_segments=N)
        msg = jax.ops.segment_sum(e[:, :, None] * v[src], dst, num_segments=N)
        attn_out = msg / jnp.maximum(denom, 1e-16)[:, :, None]
        out = attn_out.reshape(N, N_HEADS * D_HEAD) @ Wo
        return x + out

    def _L2_gnn_ref(patch_embs, edge_index, edge_attr, W1, R1, b1, g1, be1, W2, R2, b2, g2, be2, W3, R3, b3, g3, be3):
        import jax, jax.numpy as jnp
        import numpy as np
        N = 50000
        E = 50000
        C = 32
        KS = 4
        DIM = 3
        K3 = KS ** DIM
        NEG = 0.01
        EPS = 1e-05
        _BITS = np.array([[s >> d & 1 for d in range(DIM)] for s in range(2 ** DIM)], dtype=np.int32)

        def _basis(edge_attr):
            v = edge_attr * (KS - 1)
            lo = jnp.floor(v)
            f = v - lo
            lo = lo.astype(jnp.int32)
            bits = jnp.asarray(_BITS)
            idx = jnp.clip(lo[:, None, :] + bits[None], 0, KS - 1)
            w = jnp.where(bits[None] == 1, f[:, None, :], 1.0 - f[:, None, :])
            basis = jnp.prod(w, axis=-1)
            wi = idx[..., 0] + KS * idx[..., 1] + KS * KS * idx[..., 2]
            return (basis, wi)

        def _sconv(x, src, dst, basis, wi, W, R, b):
            n = x.shape[0]
            z = jnp.einsum('nc,kco->nko', x, W)
            msg = jnp.zeros((src.shape[0], W.shape[2]), x.dtype)
            for s in range(basis.shape[1]):
                msg = msg + basis[:, s, None] * z[src, wi[:, s]]
            agg = jax.ops.segment_sum(msg, dst, num_segments=n)
            cnt = jax.ops.segment_sum(jnp.ones((dst.shape[0],), x.dtype), dst, num_segments=n)
            agg = agg / jnp.clip(cnt, 1.0)[:, None]
            return agg + x @ R + b

        def _bn(x, g, be):
            mu = x.mean(0)
            var = x.var(0)
            return (x - mu) * jax.lax.rsqrt(var + EPS) * g + be

        def _leaky(x):
            return jnp.where(x >= 0, x, NEG * x)
        src, dst = (edge_index[0], edge_index[1])
        basis, wi = _basis(edge_attr)
        x = _bn(_leaky(_sconv(patch_embs, src, dst, basis, wi, W1, R1, b1)) + patch_embs, g1, be1)
        x = _bn(_leaky(_sconv(x, src, dst, basis, wi, W2, R2, b2)) + x, g2, be2)
        x = _bn(_sconv(x, src, dst, basis, wi, W3, R3, b3) + x, g3, be3)
        return x

    def _L3_gnn_ref(x, edge_index, Wq, Wk, Wv, Wout):
        import jax, jax.numpy as jnp
        import numpy as np
        N_NODES = 50000
        N_EDGES = 25000
        FEAT = 32
        HEADS = 4
        sender, receiver = (edge_index[0], edge_index[1])
        n, f = x.shape
        scale = f ** (-0.5)
        Q = jnp.einsum('nf,hfo->hno', x, Wq)
        K = jnp.einsum('nf,hfo->hno', x, Wk)
        V = jnp.einsum('nf,hfo->hno', x, Wv)
        s = jnp.einsum('hef,hef->eh', Q[:, receiver], K[:, sender]) * scale
        m = jax.ops.segment_max(s, receiver, num_segments=n)
        m = jnp.where(jnp.isfinite(m), m, 0.0)
        e = jnp.exp(s - m[receiver])
        denom = jax.ops.segment_sum(e, receiver, num_segments=n)
        Vs = jnp.transpose(V[:, sender], (1, 0, 2))
        num = jax.ops.segment_sum(e[..., None] * Vs, receiver, num_segments=n)
        denom_safe = jnp.where(denom > 0, denom, 1.0)
        attn = jnp.where(denom[..., None] > 0, num / denom_safe[..., None], 0.0)
        out = attn.mean(axis=1)
        return x + out @ Wout
    edge_index = jnp.stack([src, dst])
    h = jnp.maximum(_layernorm(x, axis=-1), 0.0)
    x = x + _L0_gnn_ref(h, edge_index, L0_gnn_w, L0_gnn_fc_w, L0_gnn_fc_b, L0_gnn_bias)
    h = jnp.maximum(_layernorm(x, axis=-1), 0.0)
    x = x + _L1_gnn_ref(h, L1_gnn_Wq, L1_gnn_Wk, L1_gnn_Wv, L1_gnn_Wo, edge_index)
    h = jnp.maximum(_layernorm(x, axis=-1), 0.0)
    x = x + _L2_gnn_ref(h, edge_index, edge_attr_3, L2_gnn_W1, L2_gnn_R1, L2_gnn_b1, L2_gnn_g1, L2_gnn_be1, L2_gnn_W2, L2_gnn_R2, L2_gnn_b2, L2_gnn_g2, L2_gnn_be2, L2_gnn_W3, L2_gnn_R3, L2_gnn_b3, L2_gnn_g3, L2_gnn_be3)
    h = jnp.maximum(_layernorm(x, axis=-1), 0.0)
    x = x + _L3_gnn_ref(h, edge_index, L3_gnn_Wq, L3_gnn_Wk, L3_gnn_Wv, L3_gnn_Wout)
    return x

_drawn_inputs = setup_inputs


def setup_inputs(seed=0):
    import zlib

    import numpy as np

    out = dict(_drawn_inputs(seed))
    spreads = {'L0_gnn_bias': (0.0, 0.1),
     'L2_gnn_b1': (0.0, 0.405),
     'L2_gnn_g1': (1.0, 0.2),
     'L2_gnn_be1': (0.0, 0.8),
     'L2_gnn_b2': (0.0, 0.457),
     'L2_gnn_g2': (1.0, 0.2),
     'L2_gnn_be2': (0.0, 0.8),
     'L2_gnn_b3': (0.0, 0.8),
     'L2_gnn_g3': (1.0, 0.2),
     'L2_gnn_be3': (0.0, 0.1)}
    factors = {'edge_attr_3': 3.883,
     'L2_gnn_W1': 5.279,
     'L2_gnn_W2': 7.395,
     'L2_gnn_W3': 5.763,
     'L3_gnn_Wq': 3.78,
     'L3_gnn_Wk': 3.679}
    for name, (base, spread) in spreads.items():
        noise = np.random.default_rng([zlib.crc32(name.encode()), seed]).standard_normal(out[name].shape)
        drawn = base * np.exp(spread * noise) if base else spread * noise
        out[name] = jnp.asarray(drawn.astype(out[name].dtype))
    for name, factor in factors.items():
        out[name] = (out[name] * factor).astype(out[name].dtype)
    return out
```

```python
import concourse.bass as bass
from concourse import mybir
from contextlib import ExitStack

FP = mybir.dt.float32
BF = mybir.dt.bfloat16
I32 = mybir.dt.int32
U8 = mybir.dt.uint8
ALU = mybir.AluOpType
ACT = mybir.ActivationFunctionType
AX = mybir.AxisListType

P = 128
NODES = 3125
EDGES = 100000
F = 32
H = 4
NT = (NODES + P - 1) // P
LASTN = NODES - (NT - 1) * P
EP = 125
ET = EDGES // EP
EB = 8
SORTS = ET // EB
R = 8
MAXBLOCKS = (EDGES + R * NODES) // R
G = (MAXBLOCKS + P - 1) // P
NB = G * P
DUMMY = NT * P
BIG = 1.0e30
EPS = 1e-5
INV_D8 = 8 ** -0.5
INV_F = F ** -0.5


class Chain:

    def __init__(self, eng, sem):
        self.eng, self.sem, self.n = eng, sem, 0

    def __call__(self, ins):
        ins.then_inc(self.sem, 1)
        self.n += 1
        self.eng.wait_ge(self.sem, self.n)

    def add(self, ins):
        ins.then_inc(self.sem, 1)
        self.n += 1

    def sync(self):
        self.eng.wait_ge(self.sem, self.n)


def build(nc, A, out, D, upto=99):
    ctx = ExitStack()
    with ctx:
        def sb(name, shape, dt=FP):
            return ctx.enter_context(nc.sbuf_tensor(name, shape, dt))

        def sem(name):
            return ctx.enter_context(nc.semaphore(name))

        bank = [ctx.enter_context(nc.psum_tensor(f"bank{i}", [P, 512], FP)) for i in range(8)]

        ident = sb("ident", [P, P])
        identb = sb("identb", [P, P], BF)
        iota_i = sb("iota_i", [P, P], I32)
        iota_b = sb("iota_b", [P, P], BF)
        below = sb("below", [P, P])
        above = sb("above", [P, P])
        ones = sb("ones", [P, P])
        onesb = sb("onesb", [P, 1])

        work = sb("work", [P, 11808])
        pos_ = [0]

        def carve(n, dt=FP, parts=P):
            k = n if dt in (FP, I32) else (n + 1) // 2
            a = work[0:parts, pos_[0]:pos_[0] + k]
            pos_[0] += k
            return a if dt == FP else a.bitcast(dt)

        key_i = [carve(ET, I32, EP) for _ in range(2)]
        key_f = [carve(ET, FP, EP) for _ in range(2)]
        lo_b = [carve(ET, BF, EP) for _ in range(2)]
        hi_b = [carve(ET, BF, EP) for _ in range(2)]
        payload = carve(ET * 4, FP, EP).rearrange("p (t c) -> p t c", c=4)
        tmp_i = carve(ET, I32, EP)
        attr = carve(ET * 3, FP, EP)
        conv = sb("conv", [P, 7168])
        cpos = [0]

        def carve2(n, dt=FP, parts=P):
            k = n if dt in (FP, I32) else (n + 1) // 2
            a = conv[0:parts, cpos[0]:cpos[0] + k]
            cpos[0] += k
            return a if dt == FP else a.bitcast(dt)

        ohlo = [[carve2(EB * P, BF, EP).rearrange("p (j c) -> p j c", c=P) for _ in range(2)] for _ in range(2)]
        ohhi = [[carve2(EB * NT, BF, EP).rearrange("p (j c) -> p j c", c=NT) for _ in range(2)] for _ in range(2)]
        ohloT = [carve2(EB * EP).rearrange("p (j c) -> p j c", c=EP) for _ in range(2)]
        base_sb = [carve2(EB * NT).rearrange("p (j c) -> p j c", c=NT) for _ in range(2)]
        junk = carve2(2 * EB * EP, BF, EP).rearrange("p (j c) -> p j c", c=EP)
        keys_st = [sb(f"keys_st{u}", [EP, 2, EB]) for u in range(2)]
        lo_st = [sb(f"lo_st{u}", [EP, 2, EB], BF) for u in range(2)]
        hi_st = [sb(f"hi_st{u}", [EP, 2, EB], BF) for u in range(2)]
        rank_in = sb("rank_in", [EP, 2, EB])
        picked = carve2(2 * EB * NT, FP, EP).rearrange("p (k j) -> p k j", k=2)
        baseline = sb("baseline", [EP, 2, EB])
        pos_st = [sb(f"pos_st{u}", [EP, 2, EB], I32) for u in range(2)]
        pay_st = [sb(f"pay_st{u}", [EP, EB, 4]) for u in range(2)]
        srt_st = [sb(f"srt_st{u}", [EP, EB]) for u in range(2)]
        deg = [sb(f"deg{k}", [P, NT]) for k in range(2)]
        nblk = [sb(f"nblk{k}", [P, NT]) for k in range(2)]
        nblk_i = sb("nblk_i", [P, NT], I32)
        start = [sb(f"start{k}", [P, NT]) for k in range(2)]
        start_i = [sb(f"start_i{k}", [P, NT], I32) for k in range(2)]
        last_i = [sb(f"last_i{k}", [P, NT], I32) for k in range(2)]
        tot = sb("tot", [P, NT])
        zero = sb("zero", [P, 512])
        gate_in = sb("gate_in", [16, 1])
        gate_out = sb("gate_out", [16, 1])
        fill = sb("fill", [P, 1024, 4])

        s_load = sem("s_load"); s_const = sem("s_const"); s_pool = sem("s_pool")
        s_dve = sem("s_dve"); s_gate = sem("s_gate")
        s_fill = sem("s_fill"); s_filled = sem("s_filled"); s_keys = sem("s_keys")
        s_oh = sem("s_oh"); s_hist = sem("s_hist"); s_histall = sem("s_histall")
        s_nblk = sem("s_nblk"); s_prefix = sem("s_prefix"); s_start = sem("s_start")
        s_base0 = sem("s_base0"); s_flag = sem("s_flag")
        s_oh2 = sem("s_oh2"); s_T = sem("s_T"); s_ohT = sem("s_ohT"); s_key = sem("s_key")
        s_cp = [sem(f"s_cp{k}") for k in range(2)]; s_acc = [sem(f"s_acc{k}") for k in range(2)]
        s_look = sem("s_look"); s_rank = sem("s_rank"); s_pick = sem("s_pick"); s_bl = sem("s_bl"); s_pay = sem("s_pay")
        s_pos = sem("s_pos"); s_sc = [sem(f"s_sc{u}") for u in range(2)]

        hist = [bank[0][:, 0:NT], bank[1][:, 0:NT]]
        look = [bank[2][0:EP, k * 256:k * 256 + EB * NT].rearrange("p (j c) -> p j c", c=NT) for k in range(2)]
        keyrow = [[bank[3 + 2 * 0 + (j // 4)][0:EP, (j % 4) * 128:(j % 4) * 128 + EP] for j in range(EB)],
                  [bank[5 + (j // 4)][0:EP, (j % 4) * 128:(j % 4) * 128 + EP] for j in range(EB)]]
        trb = bank[7].bitcast(BF) if hasattr(bank[7], 'bitcast') else bank[7][:, :].bitcast(BF)

        x = sb("x", [P, NT, F])
        h = sb("h", [P, NT, F])
        hT = sb("hT", [F, NT * P])
        wide = sb("wide", [P, NT * P])
        comb = sb("comb", [P, G * 32])
        fill0 = comb[:, 0:1024]
        lnm = sb("lnm", [P, NT])
        lns = sb("lns", [P, NT])
        rcnt = sb("rcnt", [P, NT])
        eps = sb("eps", [P, 1])
        idx_a = sb("idx_a", [P, G + 2, R + 1], I32)
        idx_c = sb("idx_c", [P, G + 2, R], I32)
        valid = sb("valid", [P, G, R])
        pen = sb("pen", [P, G, R])
        same = sb("same", [F, NB], U8)
        idx_st = [sb(f"idx_st{u}", [P, R + 1], I32) for u in range(2)]
        rows = [sb(f"rows{u}", [P, R * 64]) for u in range(2)]
        qrow = [sb(f"qrow{u}", [P, P]) for u in range(2)]
        flg = sb("flg", [G, P])
        cum = sb("cum", [G, P])
        nodeid = sb("nodeid", [G, P])
        same_g = sb("same_g", [G, P], U8)
        fill_all = fill[:, :, :].rearrange("p c a -> p (c a)")
        w0 = sb("w0", [F, H, F]); w0cat = sb("w0cat", [P, F]); fcw = sb("fcw", [F, 2, F]); fcb = sb("fcb", [P, 1])
        bias0 = sb("bias0", [P, F]); wa = sb("wa", [F, 2 * H]); wtmp = sb("wtmp", [F, H, F])
        wkvq = sb("wkvq", [F, 3 * F]); wo = sb("wo", [F, F])
        w3 = sb("w3", [F, 3, H * F]); w3T = sb("w3T", [F, 3, H * F]); wout = sb("wout", [F, F])
        wqk = sb("wqk", [F, H * F]); wvo = sb("wvo", [F, H * F]); wvocat = sb("wvocat", [P, F])
        cw = sb("cw", [P, 16, F]); cr = sb("cr", [F, 3, F]); cb = sb("cb", [F, 9])
        sel = sb("sel", [H, 2, P]); sel_i = sb("sel_i", [H, 2, P], I32)
        mask = sb("mask", [P, P // R, 16]); mask_i = comb[:, 1024:1024 + 2 * P].bitcast(I32).rearrange("p (b k) -> p b k", b=P // R)
        prt_i = sb("prt_i", [P, 1], I32); prt_f = sb("prt_f", [P, 1])
        cpos[0] = 0
        prod = carve2(1024)
        wE = carve2(256)
        out_st = [carve2(132) for _ in range(2)]
        aT = [carve2(512) for _ in range(2)]
        numS = [carve2(P) for _ in range(2)]
        num1 = carve2(P)
        tab = carve2(NT * 64)
        part = carve2(P)
        sc_ = sb("sc_", [P, R, H]); dif = sb("dif", [P, R, H]); ex = sb("ex", [P, R, H])
        stat = sb("stat", [P, 2 * H])
        runmax = sb("runmax", [H, P + 1]); penr = sb("penr", [H, P]); dd = sb("dd", [H, 2, P]); ww = sb("ww", [H, 2, P])
        den1 = sb("den1", [H, P]); denS = [sb(f"denS{u}", [H, P]) for u in range(2)]
        cpos[0] = 0
        tsb = [carve2(16 * P).rearrange("p (k b) -> p k b", b=P) for _ in range(2)]
        xb = [carve2(R * P).rearrange("p (j k c) -> p j k c", j=R, c=F) for _ in range(2)]
        m12 = [fill_all[:, u * 2048:(u + 1) * 2048].rearrange("p (j c) -> p j c", j=R) for u in range(2)]
        b12 = sb("b12", [P, R, 16])
        aggS = [sb(f"aggS{u}", [F, P]) for u in range(2)]
        cout = [sb(f"cout{u}", [P, F]) for u in range(2)]
        hats = work[:, 0:G * R * 12].rearrange("p (s d k) -> p s d k", d=3, k=4)
        attr_c = wide[:, 0:3 * G * R].rearrange("p (d g j) -> p d g j", d=3, j=R)
        ytmp = comb[0:F, 0:NT * P]
        bn = sb("bn", [F, 8])
        NW = 26
        s_slread = sem("s_slread"); s_yn = sem("s_yn")
        done_of = {0: 1, 1: 2, 4: 3, 5: 4}
        s_xpad = sem("s_xpad"); s_xl = sem("s_xl")

        s_w = sem("s_w"); s_sel = sem("s_sel"); s_prep = sem("s_prep"); s_off = sem("s_off"); s_nid = sem("s_nid")
        s_nidT = sem("s_nidT"); s_same = sem("s_same"); s_samew = sem("s_samew"); s_samer = sem("s_samer"); s_slots = sem("s_slots")
        s_wT = sem("s_wT"); s_wp = sem("s_wp"); s_vo = sem("s_vo"); s_vod = sem("s_vod")
        s_slT = sem("s_slT"); s_slc = sem("s_slc")
        s_var = sem("s_var"); s_std = sem("s_std"); s_h = sem("s_h"); s_hTp = sem("s_hTp"); s_hTc = sem("s_hTc")
        s_tp = sem("s_tp"); s_tc = sem("s_tc"); s_tabr = sem("s_tabr"); s_tabw = sem("s_tabw")
        s_stage = sem("s_stage"); s_rows = [[sem(f"s_rows{l}_{u}") for u in range(2)] for l in range(6)]
        s_prod = sem("s_prod"); s_raw = sem("s_raw"); s_scored = sem("s_scored"); s_bmax = sem("s_bmax"); s_dif = sem("s_dif")
        s_exp = sem("s_exp"); s_ev = sem("s_ev"); s_den = sem("s_den"); s_wv = sem("s_wv"); s_part = sem("s_part")
        s_partT = sem("s_partT"); s_penr = sem("s_penr"); s_carry = sem("s_carry"); s_runmax = sem("s_runmax")
        s_dd = sem("s_dd"); s_ww = sem("s_ww"); s_w0 = sem("s_w0"); s_wx = sem("s_wx"); s_wE = sem("s_wE")
        s_den1 = sem("s_den1"); s_denS = sem("s_denS"); s_num1 = sem("s_num1"); s_numS = sem("s_numS")
        s_back = sem("s_back"); s_outst = sem("s_outst"); s_outw = [sem(f"s_outw{u}") for u in range(2)]
        s_comb = sem("s_comb"); s_norm = sem("s_norm"); s_aT = sem("s_aT"); s_aTc = sem("s_aTc"); s_fin = sem("s_fin")
        s_xb = sem("s_xb"); s_b12 = sem("s_b12"); s_m12 = sem("s_m12"); s_tb = sem("s_tb"); s_tsb = sem("s_tsb")
        s_msg = sem("s_msg"); s_agg = sem("s_agg"); s_y = sem("s_y"); s_yc = sem("s_yc"); s_bnv = sem("s_bnv"); s_bns = sem("s_bns")
        s_xT = sem("s_xT"); s_xTp = sem("s_xTp"); s_cw = sem("s_cw"); s_cwuse = sem("s_cwuse"); s_xout = sem("s_xout"); s_done = sem("s_done")

        CH = [(c, min(4, NT - c)) for c in range(0, NT, 4)]
        NCH = len(CH)
        ATT = {0: 0, 1: 1, 5: 2}
        CONV = {2: 0, 3: 1, 4: 2}
        TABF = {0: 36, 1: 64, 2: F, 3: F, 4: F, 5: F}
        QF = {0: H, 1: F, 5: H * F}
        PF = {0: P, 1: F, 5: P}
        WAYS = {0: 2 * H, 1: 3 * F, 5: H * F}

        def per(u):
            return G // 2 + (1 - u)

        def groups(eng, body):
            body(0, 0, 0)
            with eng.Fori(0, (G - 1) // 2) as i:
                body(2 * i + 1, 1, i)
                body(2 * i + 2, 0, i + 1)

        def batches(eng, body):
            body(0, 0)
            body(1, 1)
            with eng.Fori(1, SORTS // 2) as i:
                for u in range(2):
                    body(2 * i + u, u)

        block = ctx.enter_context(nc.Block())

        @block.sync
        def _(sp):
            n = 0
            for k, name in enumerate(("src", "dst")):
                sp.dma_start(key_i[k], A[name].rearrange("(p t) -> p t", p=EP)).then_inc(s_load, 16)
            with nc.allow_non_contiguous_dma(reason="single columns of a few small vectors"):
                W = []
                W.append(sp.dma_start(x[:, 0:NT - 1, :], A["x"][0:(NT - 1) * P, :].rearrange("(t p) f -> p t f", p=P)))
                W.append(sp.dma_start(w0[:, :, :], A["L0_gnn_w"].rearrange("h f o -> f h o")))
                W.append(sp.dma_start(w0cat[:, :], A["L0_gnn_w"].rearrange("h f o -> (h f) o")))
                W.append(sp.dma_start(fcw[:, :, :], A["L0_gnn_fc_w"].rearrange("a (s o) -> a s o", s=2).to_broadcast([F, 2, F])))
                W.append(sp.dma_start(fcb[:, :], A["L0_gnn_fc_b"].rearrange("(a b) -> a b", b=1).to_broadcast([P, 1])))
                W.append(sp.dma_start(bias0[:, :], A["L0_gnn_bias"].rearrange("(a b) -> a b", a=1).to_broadcast([P, F])))
                for i, name in enumerate(("Wk", "Wv", "Wq")):
                    W.append(sp.dma_start(wkvq[:, i * F:(i + 1) * F], A["L1_gnn_" + name]))
                W.append(sp.dma_start(wo[:, :], A["L1_gnn_Wo"]))
                for i, name in enumerate(("Wq", "Wk", "Wv")):
                    W.append(sp.dma_start(w3[:, i, :].rearrange("f (h o) -> f h o", h=H), A["L3_gnn_" + name].rearrange("h f o -> f h o")))
                W.append(sp.dma_start(wout[:, :], A["L3_gnn_Wout"]))
                for i in range(3):
                    W.append(sp.dma_start(cr[:, i, :], A[f"L2_gnn_R{i + 1}"]))
                    for j, name in enumerate(("b", "g", "be")):
                        W.append(sp.dma_start(cb[:, 3 * i + j:3 * i + j + 1], A[f"L2_gnn_{name}{i + 1}"].rearrange("(c a) -> c a", a=1)))
                for ins in W:
                    ins.then_inc(s_w, 16)
                assert len(W) == NW, len(W)
                sp.wait_ge(s_xpad, 1)
                sp.dma_start(x[0:LASTN, NT - 1, :], A["x"][(NT - 1) * P:NODES, :]).then_inc(s_xl, 16)
            sp.dma_start(attr, A["edge_attr_3"].rearrange("(p t) c -> p (t c)", p=EP)).then_inc(s_load, 16)
            sp.wait_ge(s_fill, 4)
            sp.dma_start(D["slots0"].rearrange("(g c) a -> g (c a)", g=G), comb[0:G, 0:1024]).then_inc(s_filled, 16)
            sp.dma_start(D["slots1"].rearrange("(g c) a -> g (c a)", g=G), fill[0:G, :, :].rearrange("p c a -> p (c a)")).then_inc(s_filled, 16)
            for k in range(2):
                sp.dma_start(D[f"flags{k}"].rearrange("(g c) a -> g (c a)", g=G), zero[0:G, 0:P]).then_inc(s_filled, 16)
            for u in range(2):
                sp.wait_ge(s_sc[u], (SORTS // 2) * 2 * EB * 16)
            sp.wait_ge(s_flag, 2 * NT * 16)

            def load_groups(k):
                sp.dma_start(flg[:, :], D[f"flags{k}"].rearrange("(g p) a -> g (p a)", p=P)).then_inc(s_slots, 16)
                w = 4 if k else 1
                sp.dma_start(comb[:, 0:G * R * w].rearrange("p (g c) -> p g c", g=G),
                             D[f"slots{k}"].rearrange("(g p r) a -> p g (r a)", p=P, r=R)).then_inc(s_slots, 16)
                if k:
                    sp.dma_start(fill_all[0:G, :], D["slots1"].rearrange("(g c) a -> g (c a)", g=G)).then_inc(s_slots, 16)
                sp.wait_ge(s_same, k + 1)
                sp.dma_start(D[f"same{k}"].rearrange("(g p) -> g p", p=P), same_g[:, :]).then_inc(s_samew, 16)
                sp.wait_ge(s_samew, 16 * (k + 1))
                sp.dma_start(same[:, :], D[f"same{k}"].rearrange("(a n) -> a n", a=1).to_broadcast([F, NB])).then_inc(s_samer, 16)

            def tables(l):
                sp.wait_ge(s_tabr, l + 1)
                f = TABF[l]
                rowsrc = (tab[:, 0:NT * f].rearrange("p (t c) -> p t c", c=f) if l in (0, 1) else h[:, :, :])
                sp.dma_start(D[f"tab{l}"][0:NT * P, :].rearrange("(t p) c -> p t c", p=P), rowsrc).then_inc(s_tabw, 16)
                sp.dma_start(D[f"tab{l}"][NT * P:NT * P + 1, :], zero[0:1, 0:f]).then_inc(s_tabw, 16)
                if l in QF:
                    q = QF[l]
                    sp.dma_start(D[f"q{l}"].rearrange("(t p) c -> p t c", p=P),
                                 wide[:, 0:NT * q].rearrange("p (t c) -> p t c", c=q)).then_inc(s_tabw, 16)

            def blocks_out(l):
                w = PF[l] + H if l in ATT else F
                src = out_st if l in ATT else cout

                def store(g, u, o):
                    sp.wait_ge(s_outst, l * G + g + 1)
                    sp.dma_start(D[f"blk{l}"].rearrange("(g p) c -> g p c", p=P)[bass.ds(g, 1), :, :].rearrange("a p c -> (a p) c"),
                                 src[u][:, 0:w]).then_inc(s_outw[u], 16)
                groups(sp, store)

            sp.wait_ge(s_vo, 1)
            for hh in range(H):
                sp.dma_start(wvocat[hh * F:(hh + 1) * F, :], wvo[:, hh * F:(hh + 1) * F]).then_inc(s_vod, 16)
            for l in range(LAYERS):
                if l < 2:
                    if l:
                        sp.wait_ge(s_done, 1)
                    load_groups(l)
                if l in CONV:
                    if CONV[l]:
                        sp.wait_ge(s_msg, CONV[l] * G)
                    sp.dma_start(cw[:, :, :], A[f"L2_gnn_W{CONV[l] + 1}"].rearrange("(k q) c o -> (q c) k o", q=4)).then_inc(s_cw, 16)
                tables(l)
                blocks_out(l)
            sp.wait_ge(s_done, LAYERS if LAYERS < 3 else max(2, LAYERS - 2))
            sp.dma_start(out[0:(NT - 1) * P, :].rearrange("(t p) f -> p t f", p=P), x[:, 0:NT - 1, :]).then_inc(s_xout, 16)
            sp.dma_start(out[(NT - 1) * P:NODES, :], x[0:LASTN, NT - 1, :]).then_inc(s_xout, 16)
            sp.wait_ge(s_xout, 32)

        @block.gpsimd
        def _(pool):
            c = Chain(pool, s_pool)
            c.add(nc.gpsimd.memset(ident[:, :], 0.0))
            c.add(nc.gpsimd.memset(below[:, :], 1.0))
            c.add(nc.gpsimd.memset(above[:, :], 1.0))
            c.add(nc.gpsimd.memset(ones[:, :], 1.0))
            c(nc.gpsimd.iota(iota_i[:, :], pattern=[[1, P]], base=0, channel_multiplier=0))
            nc.gpsimd.affine_select(out=ident[:, :], in_=ident[:, :], compare_op=ALU.not_equal, fill=1.0, base=0,
                                    pattern=[[-1, P]], channel_multiplier=1).then_inc(s_const, 1)
            nc.gpsimd.affine_select(out=below[:, :], in_=below[:, :], compare_op=ALU.is_gt, fill=0.0, base=0,
                                    pattern=[[-1, P]], channel_multiplier=1).then_inc(s_const, 1)
            nc.gpsimd.affine_select(out=above[:, :], in_=above[:, :], compare_op=ALU.is_gt, fill=0.0, base=0,
                                    pattern=[[1, P]], channel_multiplier=-1).then_inc(s_const, 1)
            nc.gpsimd.memset(gate_in[:, :], 0.0).then_inc(s_const, 1)
            nc.gpsimd.iota(sel_i[:, 0, :].rearrange("p (a b) -> p a b", a=H), pattern=[[1, H], [0, F]], base=0, channel_multiplier=-1).then_inc(s_const, 1)
            nc.gpsimd.iota(sel_i[:, 1, :].rearrange("p (a b) -> p a b", b=R), pattern=[[1, P // R], [0, R]], base=0, channel_multiplier=-1).then_inc(s_const, 1)
            nc.gpsimd.iota(mask_i, pattern=[[1, P // R], [0, 16]], base=0, channel_multiplier=0).then_inc(s_const, 1)
            nc.gpsimd.iota(prt_i[:, :], pattern=[[0, 1]], base=0, channel_multiplier=1).then_inc(s_const, 1)
            pool.wait_ge(s_const, 8)
            gates = [0]

            def gate(*waits):
                pool.wait_ge(s_gate, gates[0])
                for s, v in waits:
                    pool.wait_ge(s, v)
                nc.gpsimd.tensor_tensor(gate_out[:, :], gate_in[:, :], gate_in[:, :], ALU.add).then_inc(s_gate, 1)
                gates[0] = gates[0] + 1

            pool.wait_ge(s_filled, 64)
            pool.wait_ge(s_start, 2)
            for k in range(2):
                for t in range(NT):
                    n = P if t < NT - 1 else LASTN
                    pool.indirect_dma_start(
                        out=D[f"flags{k}"], out_offset=bass.IndirectOffsetOnAxis(ap=start_i[k][0:n, t:t + 1], axis=0),
                        in_=ones[0:n, 0:1], in_offset=None).then_inc(s_flag, 16)

            def scatter(g, u):
                gates[0] = g
                gate((s_pos, g + 1))
                for j in range(EB):
                    pool.indirect_dma_start(
                        out=D["slots1"], out_offset=bass.IndirectOffsetOnAxis(ap=pos_st[u][:, 1, j:j + 1], axis=0),
                        in_=pay_st[u][:, j, :], in_offset=None).then_inc(s_sc[u], 16)
                    pool.indirect_dma_start(
                        out=D["slots0"], out_offset=bass.IndirectOffsetOnAxis(ap=pos_st[u][:, 0, j:j + 1], axis=0),
                        in_=srt_st[u][:, j:j + 1], in_offset=None).then_inc(s_sc[u], 16)
            batches(pool, scatter)
            tabw = 0
            for l in range(LAYERS):
                tabw += 48 if l in ATT else 32

                def gather(g, u, o):
                    gates[0] = SORTS + l * G + g
                    need = [(s_stage, l * (G + 2) + g + 1)]
                    if isinstance(g, int) and g == 0:
                        need.append((s_tabw, tabw))
                    gate(*need)
                    f = TABF[l]
                    for r in range(R):
                        pool.indirect_dma_start(
                            out=rows[u][:, r * f:(r + 1) * f], out_offset=None, in_=D[f"tab{l}"],
                            in_offset=bass.IndirectOffsetOnAxis(ap=idx_st[u][:, r:r + 1], axis=0)).then_inc(s_rows[l][u], 16)
                    if l in QF:
                        pool.indirect_dma_start(
                            out=qrow[u][:, 0:QF[l]], out_offset=None, in_=D[f"q{l}"],
                            in_offset=bass.IndirectOffsetOnAxis(ap=idx_st[u][:, R:R + 1], axis=0)).then_inc(s_rows[l][u], 16)
                groups(pool, gather)
                pool.wait_ge(s_outw[0], 16 * (G // 2 + 1) * (l + 1))
                pool.wait_ge(s_outw[1], 16 * (G // 2) * (l + 1))
                if l == 1:
                    pool.wait_ge(s_slread, 1)
                w = PF[l] + H if l in ATT else F
                for t in range(NT):
                    pool.indirect_dma_start(
                        out=comb[:, t * w:(t + 1) * w], out_offset=None, in_=D[f"blk{l}"],
                        in_offset=bass.IndirectOffsetOnAxis(ap=last_i[0 if l == 0 else 1][:, t:t + 1], axis=0)).then_inc(s_comb, 16)

        @block.vector
        def _(dve):
            c = Chain(dve, s_dve)
            v = nc.vector
            v.memset(fill[:, :, 1:4], 0.0).then_inc(s_fill, 1)
            v.memset(fill[:, :, 0:1], float(DUMMY)).then_inc(s_fill, 1)
            v.memset(fill0, float(DUMMY)).then_inc(s_fill, 1)
            v.memset(zero[:, :], 0.0).then_inc(s_fill, 1)
            dve.wait_ge(s_const, 8)
            c.add(v.tensor_copy(identb[:, :], ident[:, :]))
            c.add(v.tensor_copy(iota_b[:, :], iota_i[:, :]))
            c(v.memset(onesb[:, :], 1.0))
            v.memset(x[:, NT - 1, :], 0.0).then_inc(s_xpad, 1)
            c.add(v.memset(eps[:, :], EPS))
            c.add(v.memset(idx_a[:, G:G + 2, :], 0))
            c(v.memset(idx_c[:, G:G + 2, :], 0))
            c.add(v.tensor_single_scalar(sel[:, :, :], sel_i[:, :, :], 0.0, op=ALU.is_equal))
            c(v.tensor_single_scalar(prt_i[:, :], prt_i[:, :], R.bit_length() - 1, op=ALU.arith_shift_right))
            c(v.tensor_copy(prt_f[:, :], prt_i[:, :]))
            c(v.tensor_scalar(mask[:, :, :], mask_i, prt_f[:, 0:1], None, ALU.is_equal))
            dve.wait_ge(s_w, 16 * NW)
            for i in range(2):
                c(v.tensor_tensor(wtmp[:, :, :], w0[:, :, :], fcw[:, i:i + 1, :].to_broadcast([F, H, F]), ALU.mult))
                c(v.tensor_reduce(wa[:, i * H:(i + 1) * H], wtmp[:, :, :], AX.X, ALU.add))
            for i in range(3):
                v.transpose(w3T[:, i, :], w3[:, i, :]).then_inc(s_wT, 1)
            dve.wait_ge(s_load, 48)
            for k in range(2):
                c.add(v.tensor_copy(key_f[k], key_i[k]))
                c(v.tensor_single_scalar(tmp_i, key_i[k], 127, op=ALU.bitwise_and))
                c(v.tensor_copy(lo_b[k], tmp_i))
                c(v.tensor_single_scalar(tmp_i, key_i[k], 7, op=ALU.arith_shift_right))
                c(v.tensor_copy(hi_b[k], tmp_i))
            c.add(v.tensor_copy(payload[:, :, 0], key_f[0]))
            c(v.tensor_copy(payload[:, :, 1:4], attr.rearrange("p (t c) -> p t c", c=3)))

            def onehots(g, u, done):
                for k in range(2):
                    v.tensor_tensor(ohlo[k][u], iota_b[0:EP, None, :].to_broadcast([EP, EB, P]),
                                    lo_b[k][:, bass.ds(g * EB, EB)].unsqueeze(2).to_broadcast([EP, EB, P]),
                                    ALU.is_equal).then_inc(done, 1)
                    v.tensor_tensor(ohhi[k][u], iota_b[0:EP, None, 0:NT].to_broadcast([EP, EB, NT]),
                                    hi_b[k][:, bass.ds(g * EB, EB)].unsqueeze(2).to_broadcast([EP, EB, NT]),
                                    ALU.is_equal).then_inc(done, 1)

            def count(g, u):
                if not (isinstance(g, int) and g < 2):
                    dve.wait_ge(s_hist, g - 1)
                onehots(g, u, s_oh)
            batches(dve, count)

            dve.wait_ge(s_histall, 2)
            for k in range(2):
                c(v.tensor_copy(deg[k][:, :], hist[k]))
                c(v.tensor_scalar(tot[:, :], deg[k][:, :], 1.0, float(R - 1), ALU.max, ALU.add))
                c(v.tensor_copy(nblk_i[:, :], tot[:, :]))
                c(v.tensor_single_scalar(nblk_i[:, :], nblk_i[:, :], R.bit_length() - 1, op=ALU.arith_shift_right))
                c(v.tensor_copy(nblk[k][:, :], nblk_i[:, :]))
                v.sem_inc(s_nblk, 1) if False else v.tensor_copy(tot[:, :], nblk[k][:, :]).then_inc(s_nblk, 1)
                dve.wait_ge(s_prefix, k + 1)
                c(v.tensor_copy(tot[:, :], bank[3][:, NT:2 * NT]))
                c(v.tensor_tensor_scan(start[k][:, :], ones[:, 0:NT], tot[:, :], 0.0, ALU.mult, ALU.add))
                c(v.tensor_tensor(start[k][:, :], start[k][:, :], tot[:, :], ALU.subtract))
                c(v.tensor_tensor(start[k][:, :], start[k][:, :], bank[3][:, 0:NT], ALU.add))
                c(v.tensor_tensor(tot[:, :], start[k][:, :], nblk[k][:, :], ALU.add))
                c(v.tensor_scalar(tot[:, :], tot[:, :], -1.0, None, ALU.add))
                c(v.tensor_copy(last_i[k][:, :], tot[:, :]))
                c(v.tensor_copy(start_i[k][:, :], start[k][:, :]))
                v.tensor_scalar(start[k][:, :], start[k][:, :], float(R), None, ALU.mult).then_inc(s_start, 1)
            dve.wait_ge(s_start, 2)

            def columns(g, u):
                onehots(g, u, s_oh2)
                for k in range(2):
                    v.tensor_copy(lo_st[u][:, k, :], lo_b[k][:, bass.ds(g * EB, EB)]).then_inc(s_oh2, 1)
                    v.tensor_scalar(hi_st[u][:, k, :], hi_b[k][:, bass.ds(g * EB, EB)], 128.0, None, ALU.mult).then_inc(s_oh2, 1)
                    v.tensor_copy(keys_st[u][:, k, :], key_f[k][:, bass.ds(g * EB, EB)]).then_inc(s_oh2, 1)

            def positions(g, u):
                dve.wait_ge(s_key, g + 1)
                for k in range(2):
                    for j in range(EB):
                        v.scalar_tensor_tensor(junk[:, k * EB + j, :], keyrow[k][j], keys_st[u][:, k, j:j + 1],
                                               below[0:EP, 0:EP], ALU.is_equal, ALU.mult,
                                               accum_out=rank_in[:, k, j:j + 1]).then_inc(s_rank, 1)
                dve.wait_ge(s_look, 2 * g + 2)
                for k in range(2):
                    v.tensor_tensor(picked[:, k, :].rearrange("p (j c) -> p j c", c=NT), look[k], ohhi[k][u],
                                    ALU.mult).then_inc(s_pick, 1)
                dve.wait_ge(s_pick, 2 * g + 2)
                v.tensor_reduce(baseline[:, :, :].rearrange("p k j -> p (k j)"),
                                picked[:, :, :].rearrange("p k (j c) -> p (k j) c", c=NT), AX.X, ALU.add).then_inc(s_bl, 1)
                if not (isinstance(g, int) and g < 2):
                    dve.wait_ge(s_sc[u], (g - u) * (EB * 16))
                v.tensor_copy(pay_st[u][:, :, :], payload[:, bass.ds(g * EB, EB), :]).then_inc(s_pay, 1)
                v.tensor_copy(srt_st[u][:, :], key_f[1][:, bass.ds(g * EB, EB)]).then_inc(s_pay, 1)
                dve.wait_ge(s_pay, 2 * g + 2)
                dve.wait_ge(s_bl, g + 1)
                dve.wait_ge(s_rank, 16 * g + 16)
                v.tensor_tensor(pos_st[u][:, :, :], baseline[:, :, :], rank_in[:, :, :], ALU.add).then_inc(s_pos, 1)
                dve.wait_ge(s_pos, g + 1)

            columns(0, 0)
            columns(1, 1)
            positions(0, 0)
            with dve.Fori(1, SORTS // 2) as i:
                columns(2 * i, 0)
                positions(2 * i - 1, 1)
                columns(2 * i + 1, 1)
                positions(2 * i, 0)
            positions(SORTS - 1, 1)

            dve.wait_ge(s_wp, 1)
            c.add(v.tensor_scalar(wqk[:, :], bank[3][0:F, 0:P], INV_F, None, ALU.mult))
            v.tensor_scalar(wvo[:, :], bank[3][0:F, P:2 * P], 1.0 / H, None, ALU.mult).then_inc(s_vo, 1)
            c.add(v.tensor_scalar(w0cat[:, :], w0cat[:, :], 1.0 / H, None, ALU.mult))
            c(v.tensor_scalar(wkvq[:, 2 * F:3 * F], wkvq[:, 2 * F:3 * F], INV_D8, None, ALU.mult))
            c(v.tensor_scalar(rcnt[:, :], deg[1][:, :], 1.0, None, ALU.max))
            c(v.reciprocal(rcnt[:, :], rcnt[:, :]))
            dve.wait_ge(s_xl, 16)

            def prepare(k):
                dve.wait_ge(s_slots, 32 if k == 0 else 80)
                c(v.tensor_tensor_scan(cum[:, :], ones[0:G, :], flg[:, :], 0.0, ALU.mult, ALU.add))
                v.tensor_scalar(same_g[:, :], flg[:, :], -1.0, 1.0, ALU.mult, ALU.add).then_inc(s_same, 1)
                v.tensor_copy(nodeid[:, 0:1], cum[:, P - 1:P]).then_inc(s_prep, 1)
                dve.wait_ge(s_off, k + 1)
                v.tensor_scalar(nodeid[:, :], cum[:, :], bank[3][0:G, 0:1], -1.0, ALU.add, ALU.add).then_inc(s_nid, 1)
                dve.wait_ge(s_nidT, k + 1)
                c.add(v.tensor_copy(idx_a[:, 0:G, R], bank[3][:, 0:G]))
                w = 4 if k else 1
                slot = comb[:, 0:G * R * w].rearrange("p (g r c) -> p g r c", r=R, c=w)[:, :, :, 0]
                c.add(v.tensor_copy(idx_a[:, 0:G, 0:R], slot))
                c(v.tensor_scalar(valid[:, :, :], slot, float(DUMMY), None, ALU.is_lt))
                c(v.tensor_scalar(pen[:, :, :], valid[:, :, :], -1.0, BIG, ALU.add, ALU.mult))
                if k:
                    for n, (j, fld) in enumerate((j, fld) for j in range(R) for fld in range(4)):
                        dve.wait_ge(s_slT, n + 1)
                        dst = idx_c[:, 0:G, j] if fld == 0 else attr_c[:, fld - 1, :, j]
                        v.tensor_copy(dst, bank[4 + n % 2][:, 0:G]).then_inc(s_slc, 1)
                    dve.wait_ge(s_slc, 32)
                    flat = wide[:, 0:3 * G * R]
                    c(v.tensor_scalar(flat, flat, 3.0, 0.0, ALU.mult, ALU.max))
                    c(v.tensor_scalar(flat, flat, 3.0, None, ALU.min))
                    line = comb[:, 0:G * R]
                    for d in range(3):
                        a = wide[:, d * G * R:(d + 1) * G * R]
                        for kk in range(4):
                            c(v.tensor_scalar(line, a, -1.0, 1.0 + kk, ALU.mult, ALU.add))
                            c(v.scalar_tensor_tensor(hats[:, :, d, kk], a, 1.0 - kk, line, ALU.add, ALU.min))
                    hf = work[:, 0:G * R * 12]
                    v.tensor_scalar(hf, hf, 0.0, None, ALU.max).then_inc(s_slread, 1)
                    dve.wait_ge(s_slread, 1)
                dve.wait_ge(s_samer, 16 * (k + 1))

            def layernorm(n):
                cx = comb[:, 0:NT * F].rearrange("p (t f) -> p t f", f=F)
                sq = wide[:, 0:NT * F].rearrange("p (t f) -> p t f", f=F)
                c(v.tensor_reduce(lnm[:, :], x[:, :, :], AX.X, ALU.add))
                c(v.tensor_scalar(lnm[:, :], lnm[:, :], 1.0 / F, None, ALU.mult))
                c(v.tensor_tensor(cx, x[:, :, :], lnm[:, :].unsqueeze(2).to_broadcast([P, NT, F]), ALU.subtract))
                c(v.tensor_tensor(sq, cx, cx, ALU.mult))
                c(v.tensor_reduce(lns[:, :], sq, AX.X, ALU.add))
                v.tensor_scalar(lns[:, :], lns[:, :], 1.0 / F, None, ALU.mult).then_inc(s_var, 1)
                dve.wait_ge(s_std, n + 1)
                c(v.reciprocal(lns[:, :], lns[:, :]))
                c(v.tensor_tensor(cx, cx, lns[:, :].unsqueeze(2).to_broadcast([P, NT, F]), ALU.mult))
                v.tensor_scalar(h[:, :, :], cx, 0.0, None, ALU.max).then_inc(s_h, 1)
                dve.wait_ge(s_h, n + 1)
                for i, (t, m) in enumerate(CH):
                    dve.wait_ge(s_hTp, NCH * n + i + 1)
                    v.tensor_copy(hT[:, t * P:(t + m) * P], bank[4 + i % 2][0:F, 0:m * P]).then_inc(s_hTc, 1)
                dve.wait_ge(s_hTc, NCH * (n + 1))

            def node_tables(l):
                a, f, q, w = ATT[l], TABF[l], QF[l], WAYS[l]
                tb = tab[:, 0:NT * f].rearrange("p (t c) -> p t c", c=f)
                qt = wide[:, 0:NT * q].rearrange("p (t c) -> p t c", c=q)
                if l == 0:
                    c.add(v.tensor_copy(tb[:, :, 0:F], h[:, :, :]))
                for i, (t, m) in enumerate(CH):
                    dve.wait_ge(s_tp, NCH * a + i + 1)
                    ps = bank[6 + i % 2][:, 0:m * w].rearrange("p (t c) -> p t c", c=w)
                    if l == 0:
                        v.tensor_copy(tb[:, t:t + m, F:F + H], ps[:, :, H:2 * H]).then_inc(s_tc, 1)
                        v.tensor_scalar(qt[:, t:t + m, :], ps[:, :, 0:H], fcb[:, 0:1], None, ALU.add).then_inc(s_tc, 1)
                    elif l == 1:
                        v.tensor_copy(tb[:, t:t + m, :], ps[:, :, 0:2 * F]).then_inc(s_tc, 1)
                        v.tensor_copy(qt[:, t:t + m, :], ps[:, :, 2 * F:3 * F]).then_inc(s_tc, 1)
                    else:
                        v.tensor_copy(qt[:, t:t + m, 0:F], ps[:, :, 0:F]).then_inc(s_tc, 1)
                        v.tensor_copy(qt[:, t:t + m, F:], ps[:, :, F:]).then_inc(s_tc, 1)
                dve.wait_ge(s_tc, 2 * NCH * (a + 1))
                c.sync()
                v.memset(runmax[:, P:P + 1], -BIG).then_inc(s_tabr, 1)

            def stage(l, g, u):
                base = l * (G + 2)
                src, n = (idx_a, R + 1) if l in ATT else (idx_c, R)
                v.tensor_copy(idx_st[u][:, 0:n], src[:, bass.ds(g, 1), :].rearrange("p a c -> p (a c)")).then_inc(s_stage, 1)

            def attention(l):
                a, f, q, pf = ATT[l], TABF[l], QF[l], PF[l]
                dve.wait_ge(s_tabr, l + 1)
                c.add(v.memset(numS[1][:, P - 1:P], 0.0))
                c(v.memset(denS[1][:, P - 1:P], 0.0))
                if l:
                    dve.wait_ge(s_stage, l * (G + 2))
                for u in range(2):
                    stage(l, u, u)

                def scores(g, u, o):
                    n = a * G + g + 1
                    X = rows[u][:, 0:R * f].rearrange("p (r c) -> p r c", c=f)
                    Q = qrow[u][:, 0:q]
                    dve.wait_ge(s_rows[l][u], (o + 1) * ((R + 1) * 16))
                    if l == 0:
                        v.tensor_tensor(dif[:, :, :], X[:, :, F:F + H], Q.unsqueeze(1).to_broadcast([P, R, H]), ALU.add).then_inc(s_prod, 1)
                        dve.wait_ge(s_prod, n)
                        v.scalar_tensor_tensor(sc_[:, :, :], dif[:, :, :], 0.2, dif[:, :, :], ALU.mult, ALU.max).then_inc(s_raw, 1)
                    elif l == 1:
                        pr = prod[:, 0:R * F].rearrange("p (r c) -> p r c", c=F)
                        v.tensor_tensor(pr, X[:, :, 0:F], Q.unsqueeze(1).to_broadcast([P, R, F]), ALU.mult).then_inc(s_prod, 1)
                        dve.wait_ge(s_prod, n)
                        v.tensor_reduce(sc_[:, :, :].rearrange("p r h -> p (r h)"), prod[:, 0:R * F].rearrange("p (a c) -> p a c", c=F // H), AX.X, ALU.add).then_inc(s_raw, 1)
                    else:
                        pr = prod[:, :].rearrange("p (r h c) -> p r h c", h=H, c=F)
                        v.tensor_tensor(pr, X.unsqueeze(2).to_broadcast([P, R, H, F]),
                                        Q.rearrange("p (h c) -> p h c", h=H).unsqueeze(1).to_broadcast([P, R, H, F]), ALU.mult).then_inc(s_prod, 1)
                        dve.wait_ge(s_prod, n)
                        v.tensor_reduce(sc_[:, :, :].rearrange("p r h -> p (r h)"), prod[:, :].rearrange("p (a c) -> p a c", c=F), AX.X, ALU.add).then_inc(s_raw, 1)
                    dve.wait_ge(s_raw, n)
                    v.tensor_tensor(sc_[:, :, :], sc_[:, :, :], pen[:, bass.ds(g, 1), :].rearrange("p a r -> p (a r)").unsqueeze(2).to_broadcast([P, R, H]), ALU.add).then_inc(s_scored, 1)
                    dve.wait_ge(s_scored, n)
                    if not (isinstance(g, int) and g == 0 and a == 0):
                        dve.wait_ge(s_partT, n - 1)
                    v.tensor_reduce(stat[:, H:2 * H], sc_[:, :, :].rearrange("p r h -> p h r"), AX.X, ALU.max).then_inc(s_bmax, 1)
                    dve.wait_ge(s_bmax, n)
                    v.tensor_tensor(dif[:, :, :], sc_[:, :, :], stat[:, H:2 * H].unsqueeze(1).to_broadcast([P, R, H]), ALU.subtract).then_inc(s_dif, 1)

                def weigh(g, u):
                    n = a * G + g + 1
                    dve.wait_ge(s_exp, n)
                    v.tensor_tensor(ex[:, :, :], ex[:, :, :], valid[:, bass.ds(g, 1), :].rearrange("p a r -> p (a r)").unsqueeze(2).to_broadcast([P, R, H]), ALU.mult).then_inc(s_ev, 1)
                    dve.wait_ge(s_ev, n)
                    v.tensor_reduce(stat[:, 0:H], ex[:, :, :].rearrange("p r h -> p h r"), AX.X, ALU.add).then_inc(s_den, 1)

                def sums(g, u):
                    n = a * G + g + 1
                    X = rows[u][:, 0:R * f].rearrange("p (r c) -> p r c", c=f)
                    if l == 1:
                        pr = prod[:, 0:R * F].rearrange("p (r h c) -> p r h c", h=H, c=F // H)
                        v.tensor_tensor(pr, X[:, :, F:2 * F].rearrange("p r (h c) -> p r h c", h=H),
                                        ex[:, :, :].unsqueeze(3).to_broadcast([P, R, H, F // H]), ALU.mult).then_inc(s_wv, 1)
                        dve.wait_ge(s_wv, n)
                        v.tensor_reduce(part[:, 0:F], prod[:, 0:R * F].rearrange("p (r c) -> p c r", c=F), AX.X, ALU.add).then_inc(s_part, 1)
                    else:
                        pr = prod[:, :].rearrange("p (r h c) -> p r h c", h=H, c=F)
                        v.tensor_tensor(pr, X[:, :, 0:F].unsqueeze(2).to_broadcast([P, R, H, F]),
                                        ex[:, :, :].unsqueeze(3).to_broadcast([P, R, H, F]), ALU.mult).then_inc(s_wv, 1)
                        dve.wait_ge(s_wv, n)
                        v.tensor_reduce(part[:, :], prod[:, :].rearrange("p (r c) -> p c r", c=P), AX.X, ALU.add).then_inc(s_part, 1)
                    dve.wait_ge(s_part, n)
                    stage(l, g + 2, u)

                def carry_max(g):
                    n = a * G + g + 1
                    sm = same[0:H, bass.ds(g * P, P)]
                    v.tensor_scalar(penr[:, :], sm, -1.0, BIG, ALU.add, ALU.mult).then_inc(s_penr, 1)
                    v.tensor_copy(runmax[:, 0:1], runmax[:, P:P + 1]).then_inc(s_carry, 1)
                    dve.wait_ge(s_penr, n)
                    dve.wait_ge(s_carry, n)
                    dve.wait_ge(s_partT, n)
                    v.tensor_tensor_scan(runmax[:, 1:P + 1], penr[:, :], bank[1][0:H, P:2 * P], runmax[:, 0:1], ALU.add, ALU.max).then_inc(s_runmax, 1)
                    dve.wait_ge(s_runmax, n)
                    v.tensor_tensor(dd[:, 0, :], bank[1][0:H, P:2 * P], runmax[:, 1:P + 1], ALU.subtract).then_inc(s_dd, 1)
                    v.tensor_tensor(dd[:, 1, :], runmax[:, 0:P], runmax[:, 1:P + 1], ALU.subtract).then_inc(s_dd, 1)
                    dve.wait_ge(s_dd, 3 * n - 1)
                    v.tensor_scalar(dd[:, 1, :], dd[:, 1, :], 0.0, None, ALU.min).then_inc(s_dd, 1)

                def carry_den(g, u):
                    n = a * G + g + 1
                    sm = same[0:H, bass.ds(g * P, P)]
                    dve.wait_ge(s_ww, n)
                    v.tensor_tensor(ww[:, 1, :], ww[:, 1, :], sm, ALU.mult).then_inc(s_w0, 1)
                    dve.wait_ge(s_w0, n)
                    v.tensor_tensor(den1[:, :], bank[1][0:H, 0:P], ww[:, 0, :], ALU.mult).then_inc(s_den1, 1)
                    dve.wait_ge(s_den1, n)
                    v.tensor_tensor_scan(denS[u][:, :], ww[:, 1, :], den1[:, :], denS[1 - u][:, P - 1:P], ALU.mult, ALU.add).then_inc(s_denS, 1)

                def carry_num(g, u):
                    n = a * G + g + 1
                    dve.wait_ge(s_wE, n)
                    v.tensor_tensor(num1[0:pf, :], bank[0][0:pf, 0:P], wE[0:pf, 0:P], ALU.mult).then_inc(s_num1, 1)
                    dve.wait_ge(s_num1, n)
                    v.tensor_tensor_scan(numS[u][0:pf, :], wE[0:pf, P:2 * P], num1[0:pf, :], numS[1 - u][0:pf, P - 1:P], ALU.mult, ALU.add).then_inc(s_numS, 1)
                    dve.wait_ge(s_numS, n)
                    dve.wait_ge(s_denS, n)

                def body(g, u, o):
                    scores(g, u, o)
                    carry_max(g - 1)
                    weigh(g, u)
                    carry_den(g - 1, 1 - u)
                    sums(g, u)
                    carry_num(g - 1, 1 - u)

                scores(0, 0, 0)
                weigh(0, 0)
                sums(0, 0)
                with dve.Fori(0, (G - 1) // 2) as i:
                    body(2 * i + 1, 1, i)
                    body(2 * i + 2, 0, i + 1)
                carry_max(G - 1)
                carry_den(G - 1, 0)
                carry_num(G - 1, 0)

            def attention_nodes(l):
                a, pf = ATT[l], PF[l]
                w = pf + H
                dve.wait_ge(s_comb, 16 * NT * (l + 1))
                cm = comb[:, 0:NT * w].rearrange("p (t c) -> p t c", c=w)
                d = cm[:, :, pf:w]
                c(v.tensor_scalar(d, d, 1e-16, None, ALU.max))
                c(v.reciprocal(d, d))
                for hh in range(H):
                    m = pf // H
                    v.tensor_tensor(cm[:, :, hh * m:(hh + 1) * m], cm[:, :, hh * m:(hh + 1) * m],
                                    cm[:, :, pf + hh:pf + hh + 1].to_broadcast([P, NT, m]), ALU.mult).then_inc(s_norm, 1)
                dve.wait_ge(s_norm, 4 * (a + 1))
                dve.wait_ge(s_fin, a + 1)
                for i, (t, m) in enumerate(((0, 16), (16, NT - 16))):
                    ps = bank[6 + i][:, 0:m * F].rearrange("p (t c) -> p t c", c=F)
                    c(v.tensor_tensor(x[:, t:t + m, :], x[:, t:t + m, :], ps, ALU.add))
                if l == 0:
                    v.tensor_tensor(x[:, :, :], x[:, :, :], bias0[:, None, :].to_broadcast([P, NT, F]), ALU.add).then_inc(s_done, 1)
                else:
                    v.tensor_tensor(x[:, :, :], x[:, :, :], h[:, :, :], ALU.add).then_inc(s_done, 1)
                dve.wait_ge(s_done, done_of[l])

            def convolution(l):
                q = CONV[l]
                dve.wait_ge(s_stage, l * (G + 2))
                c(v.memset(aggS[1][:, P - 1:P], 0.0))
                for u in range(2):
                    stage(l, u, u)

                def body(g, u, o):
                    n = q * G + g + 1
                    X = rows[u][:, 0:R * F].rearrange("p (j c) -> p j c", c=F)
                    hat = hats[:, bass.ds(g * R, R), :, :]
                    if not (isinstance(g, int) and g < 2 and q == 0):
                        dve.wait_ge(s_tb, n - 2)
                    v.tensor_tensor(b12[:, :, :].rearrange("p j (b a) -> p j b a", b=4),
                                    hat[:, :, 2, :].unsqueeze(3).to_broadcast([P, R, 4, 4]),
                                    hat[:, :, 1, :].unsqueeze(2).to_broadcast([P, R, 4, 4]), ALU.mult).then_inc(s_b12, 1)
                    dve.wait_ge(s_b12, n)
                    v.tensor_tensor(m12[u].rearrange("p j (b k) -> p j b k", k=16), b12[:, :, :].unsqueeze(2).to_broadcast([P, R, P // R, 16]),
                                    mask[:, :, :].unsqueeze(1).to_broadcast([P, R, P // R, 16]), ALU.mult).then_inc(s_m12, 1)
                    dve.wait_ge(s_rows[l][u], (o + 1) * (R * 16))
                    v.tensor_tensor(xb[u], X.unsqueeze(2).to_broadcast([P, R, 4, F]),
                                    hat[:, :, 0, :].unsqueeze(3).to_broadcast([P, R, 4, F]), ALU.mult).then_inc(s_xb, 1)
                    dve.wait_ge(s_xb, n)
                    stage(l, g + 2, u)
                    if not (isinstance(g, int) and g < 2):
                        scan(g - 2, u)

                def scan(g, u):
                    n = q * G + g + 1
                    dve.wait_ge(s_msg, n)
                    if isinstance(g, int) and g == 0:
                        dve.wait_ge(s_m12, n)
                    else:
                        dve.wait_ge(s_agg, n - 1)
                    v.tensor_tensor_scan(aggS[u][:, :], same[:, bass.ds(g * P, P)], bank[2][0:F, 0:P],
                                         aggS[1 - u][:, P - 1:P], ALU.mult, ALU.add).then_inc(s_agg, 1)
                body(0, 0, 0)
                body(1, 1, 0)
                body(2, 0, 1)
                with dve.Fori(1, (G - 1) // 2) as i:
                    body(2 * i + 1, 1, i)
                    body(2 * i + 2, 0, i + 1)
                scan(G - 2, (G - 2) % 2)
                scan(G - 1, (G - 1) % 2)

            def conv_nodes(l):
                q = CONV[l]
                y = wide[0:F, 0:NT * P]
                dve.wait_ge(s_comb, 16 * NT * (l + 1))
                cm = comb[:, 0:NT * F].rearrange("p (t c) -> p t c", c=F)
                v.tensor_tensor(cm, cm, rcnt[:, :].unsqueeze(2).to_broadcast([P, NT, F]), ALU.mult).then_inc(s_yn, 1)
                dve.wait_ge(s_yc, NCH * (q + 1))
                if q < 2:
                    c(v.scalar_tensor_tensor(y, y, 0.01, y, ALU.mult, ALU.max))
                c(v.tensor_tensor(y, y, hT[:, :], ALU.add))
                mu, var, scale = bn[:, 0:1], bn[:, 1:2], bn[:, 2:3]
                c(v.tensor_reduce(mu, y[:, 0:NODES], AX.X, ALU.add))
                c(v.tensor_scalar(mu, mu, 1.0 / NODES, None, ALU.mult))
                c(v.tensor_scalar(y, y, mu, None, ALU.subtract))
                c(v.tensor_tensor(ytmp[:, :], y, y, ALU.mult))
                c(v.tensor_reduce(var, ytmp[:, 0:NODES], AX.X, ALU.add))
                v.tensor_scalar(var, var, 1.0 / NODES, None, ALU.mult).then_inc(s_bnv, 1)
                dve.wait_ge(s_bns, q + 1)
                c(v.reciprocal(scale, var))
                c(v.tensor_tensor(scale, scale, cb[:, 3 * q + 1:3 * q + 2], ALU.mult))
                v.tensor_scalar(hT[:, :], y, scale, cb[:, 3 * q + 2:3 * q + 3], ALU.mult, ALU.add).then_inc(s_xT, 1)
                for i, (t, m) in enumerate(((0, 16), (16, NT - 16))):
                    dve.wait_ge(s_xTp, 2 * q + i + 1)
                    c(v.tensor_copy(h[:, t:t + m, :], bank[6 + i][:, 0:m * F].rearrange("p (t c) -> p t c", c=F)))
                if q < 2:
                    v.memset(bn[:, 4:5], 0.0).then_inc(s_tabr, 1)
                else:
                    v.tensor_tensor(x[:, :, :], x[:, :, :], h[:, :, :], ALU.add).then_inc(s_done, 1)
                    dve.wait_ge(s_done, done_of[l])

            for l in range(LAYERS):
                if l < 2:
                    prepare(l)
                if l in (0, 1, 2, 5):
                    layernorm((0, 1, 2, 5).index(l))
                if l == 2:
                    v.memset(bn[:, 4:5], 0.0).then_inc(s_tabr, 1)
                if l in ATT:
                    node_tables(l)
                    attention(l)
                    attention_nodes(l)
                else:
                    convolution(l)
                    conv_nodes(l)

        @block.tensor
        def _(pe):
            mm = nc.tensor.matmul
            pe.wait_ge(s_fill, 4)
            for k in range(2):
                mm(hist[k], zero[:, 0:P], zero[:, 0:NT], start=True, stop=False)

            def count(g, u):
                pe.wait_ge(s_oh, 4 * g + 4)
                for k in range(2):
                    for j in range(EB):
                        last = mm(hist[k], ohlo[k][u][:, j, :], ohhi[k][u][:, j, :], start=False, stop=False)
                last.then_inc(s_hist, 1)
            batches(pe, count)
            for k in range(2):
                mm(hist[k], zero[:, 0:P], zero[:, 0:NT], start=False, stop=True).then_inc(s_histall, 1)
            for k in range(2):
                pe.wait_ge(s_nblk, k + 1)
                if k:
                    pe.wait_ge(s_start, k)
                mm(bank[3][:, 0:NT], above[:, :], nblk[k][:, :], start=True, stop=True)
                mm(bank[3][:, NT:2 * NT], ones[:, :], nblk[k][:, :], start=True, stop=True).then_inc(s_prefix, 1)
            pe.wait_ge(s_start, 2)
            for k in range(2):
                mm(hist[k], ident[:, :], start[k][:, :], start=True, stop=True).then_inc(s_acc[k], 1)

            def rank(g, u):
                first = isinstance(g, int) and g == 0
                pe.wait_ge(s_oh2, 10 * g + 10)
                for k in range(2):
                    if k or not first:
                        pe.wait_ge(s_ohT, 2 * g + k)
                    for j in range(EB):
                        last = nc.tensor.transpose(trb[:, j * P:j * P + EP], ohlo[k][u][:, j, :], identb[0:EP, 0:EP])
                    last.then_inc(s_T, 1)
                for j in range(EB):
                    for k in range(2):
                        pe.wait_ge(s_cp[k], EB * g + j + 1)
                        mm(hist[k], ohlo[k][u][:, j, :], ohhi[k][u][:, j, :], start=False, stop=True,
                           skip_group_check=True).then_inc(s_acc[k], 1)
                if not first:
                    pe.wait_ge(s_pick, 2 * g)
                for k in range(2):
                    pe.wait_ge(s_ohT, 2 * g + k + 1)
                    for j in range(EB):
                        last = mm(look[k][:, j, :], ohloT[k][:, j, :], base_sb[k][:, j, :], start=True, stop=True)
                    last.then_inc(s_look, 1)
                if not first:
                    pe.wait_ge(s_rank, 16 * g)
                for k in range(2):
                    for j in range(EB):
                        lo = lo_st[u][:, k, j:j + 1].to_broadcast([EP, EP])
                        hi = hi_st[u][:, k, j:j + 1].to_broadcast([EP, EP])
                        mm(keyrow[k][j], lo, identb[0:EP, 0:EP], start=True, stop=False)
                        last = mm(keyrow[k][j], hi, identb[0:EP, 0:EP], start=False, stop=True)
                last.then_inc(s_key, 1)
            batches(pe, rank)

            tr = nc.tensor.transpose

            def bank_ours(i):
                mm(bank[i][0:F, 0:1], zero[:, 0:F], zero[:, 0:1], start=True, stop=True)

            pe.wait_ge(s_wT, 3)
            pe.wait_ge(s_rank, 16 * SORTS)
            for hh in range(H):
                one = slice(hh * F, (hh + 1) * F)
                mm(bank[3][0:F, hh * F:(hh + 1) * F], w3T[:, 0, one], w3T[:, 1, one], start=True, stop=True)
                last = mm(bank[3][0:F, P + hh * F:P + (hh + 1) * F], w3T[:, 2, one], wout[:, :], start=True, stop=True)
            last.then_inc(s_wp, 1)

            def prepare(k):
                pe.wait_ge(s_prep, k + 1)
                if k == 0:
                    pe.wait_ge(s_vo, 1)
                mm(bank[3][0:G, 0:1], above[0:G, 0:G], nodeid[:, 0:1], start=True, stop=True).then_inc(s_off, 1)
                pe.wait_ge(s_nid, k + 1)
                tr(bank[3][:, 0:G], nodeid[:, :], ident[0:G, 0:G]).then_inc(s_nidT, 1)
                if k:
                    pe.wait_ge(s_slots, 80)
                    for n, (j, fld) in enumerate((j, fld) for j in range(R) for fld in range(4)):
                        if n >= 2:
                            pe.wait_ge(s_slc, n - 1)
                        view = fill_all[0:G, j * 512:(j + 1) * 512].rearrange("g (s c) -> g s c", c=4)
                        tr(bank[4 + n % 2][:, 0:G], view[:, :, fld], ident[0:G, 0:G]).then_inc(s_slT, 1)

            def h_transposed(n):
                pe.wait_ge(s_h, n + 1)
                for i, (t, m) in enumerate(CH):
                    if i >= 2:
                        pe.wait_ge(s_hTc, NCH * n + i - 1)
                    for k in range(m):
                        last = tr(bank[4 + i % 2][0:F, k * P:(k + 1) * P], h[:, t + k, :], ident[:, :])
                    last.then_inc(s_hTp, 1)

            def node_tables(l):
                a, w = ATT[l], WAYS[l]
                wt = {0: wa, 1: wkvq, 5: wqk}[l]
                pe.wait_ge(s_hTc, NCH * ((0, 1, 2, 5).index(l) + 1))
                for i, (t, m) in enumerate(CH):
                    if i >= 2:
                        pe.wait_ge(s_tc, 2 * NCH * a + 2 * (i - 1))
                    for k in range(m):
                        last = mm(bank[6 + i % 2][:, k * w:(k + 1) * w], hT[:, (t + k) * P:(t + k + 1) * P], wt[:, :], start=True, stop=True)
                    last.then_inc(s_tp, 1)

            def attention(l):
                a, pf = ATT[l], PF[l]

                def inward(g):
                    n = a * G + g + 1
                    pe.wait_ge(s_den, n)
                    pe.wait_ge(s_part, n)
                    tr(bank[0][0:pf, 0:P], part[:, 0:pf], ident[:, :])
                    tr(bank[1][0:H, 0:P], stat[:, 0:H], ident[:, :])
                    tr(bank[1][0:H, P:2 * P], stat[:, H:2 * H], ident[:, :]).then_inc(s_partT, 1)

                def outward(g, u):
                    n = a * G + g + 1
                    pe.wait_ge(s_w0, n)
                    mm(bank[2][:, 0:2 * P], sel[:, 0 if pf == P else 1, :], ww[:, :, :].rearrange("p a b -> p (a b)"),
                       start=True, stop=True).then_inc(s_wx, 1)
                    pe.wait_ge(s_denS, n)
                    pe.wait_ge(s_numS, n)
                    if not (isinstance(g, int) and g == 0):
                        pe.wait_ge(s_outst, l * G + g)
                    if pf < P:
                        bank_ours(3)
                    tr(bank[3][:, 0:pf], numS[u][0:pf, :], ident[0:pf, 0:pf])
                    tr(bank[3][:, pf:pf + H], denS[u][:, :], ident[0:H, 0:H]).then_inc(s_back, 1)

                def body(g, u):
                    outward(g - 1, 1 - u)
                    inward(g)
                inward(0)
                body(1, 1)
                body(2, 0)
                with pe.Fori(1, (G - 1) // 2) as i:
                    body(2 * i + 1, 1)
                    body(2 * i + 2, 0)
                outward(G - 1, 0)

            def attention_nodes(l):
                a, pf = ATT[l], PF[l]
                w = pf + H
                wt = {0: w0cat, 1: wo, 5: wvocat}[l]
                cm = comb[:, 0:NT * w].rearrange("p (t c) -> p t c", c=w)
                pe.wait_ge(s_norm, 4 * (a + 1))
                pe.wait_ge(s_vod, 64)

                def products(i):
                    t, m = CH[i]
                    pe.wait_ge(s_aTc, NCH * a + i + 1)
                    for k in range(m):
                        n = t + k
                        last = mm(bank[6 + n // 16][:, (n % 16) * F:(n % 16 + 1) * F], aT[i % 2][0:pf, k * P:(k + 1) * P], wt[:, :], start=True, stop=True)
                    return last
                for i, (t, m) in enumerate(CH):
                    for k in range(m):
                        last = tr(bank[4 + i % 2][0:pf, k * P:(k + 1) * P], cm[:, t + k, 0:pf], ident[:, :])
                    last.then_inc(s_aT, 1)
                    if i:
                        products(i - 1)
                products(NCH - 1).then_inc(s_fin, 1)

            def convolution(l):
                q = CONV[l]
                pe.wait_ge(s_cw, 16 * (q + 1))

                def outer(g, u):
                    n = q * G + g + 1
                    pe.wait_ge(s_m12, n)
                    pe.wait_ge(s_xb, n)
                    if not (isinstance(g, int) and g == 0):
                        pe.wait_ge(s_tsb, n - 1)
                    for j in range(R):
                        last = mm(bank[4 + j // 2][:, (j % 2) * 2 * P:(j % 2 + 1) * 2 * P], xb[u][:, j, :, :].rearrange("p k c -> p (k c)"),
                                  m12[u][:, j, :], start=True, stop=True)
                    last.then_inc(s_tb, 1)

                def weights(g, u):
                    n = q * G + g + 1
                    pe.wait_ge(s_tsb, n)
                    if not (isinstance(g, int) and g == 0):
                        pe.wait_ge(s_agg, n - 1)
                    for k in range(16):
                        last = mm(bank[2][0:F, 0:P], cw[:, k, :], tsb[u][:, k, :], start=(k == 0), stop=(k == 15))
                    last.then_inc(s_msg, 1)

                def back(g, u):
                    n = q * G + g + 1
                    pe.wait_ge(s_agg, n)
                    if not (isinstance(g, int) and g == 0):
                        pe.wait_ge(s_outst, l * G + g)
                    bank_ours(3)
                    tr(bank[3][:, 0:F], aggS[u][:, :], ident[0:F, 0:F]).then_inc(s_back, 1)

                def body(g, u, o):
                    outer(g, u)
                    if not (isinstance(g, int) and g == 0):
                        weights(g - 1, 1 - u)
                        if not (isinstance(g, int) and g == 1):
                            back(g - 2, u)
                body(0, 0, 0)
                body(1, 1, 0)
                body(2, 0, 0)
                with pe.Fori(1, (G - 1) // 2) as i:
                    body(2 * i + 1, 1, i)
                    body(2 * i + 2, 0, i + 1)
                back(G - 2, (G - 2) % 2)
                weights(G - 1, (G - 1) % 2)
                back(G - 1, (G - 1) % 2)

            def conv_nodes(l):
                q = CONV[l]
                cm = comb[:, 0:NT * F].rearrange("p (t c) -> p t c", c=F)
                pe.wait_ge(s_yn, q + 1)
                for i, (t, m) in enumerate(CH):
                    if i >= 2:
                        pe.wait_ge(s_yc, NCH * q + i - 1)
                    last = mm(bank[4 + i % 2][0:F, 0:m * P], cr[:, q, :], hT[:, t * P:(t + m) * P], start=True, stop=False)
                    for k in range(m):
                        last = mm(bank[4 + i % 2][0:F, k * P:(k + 1) * P], cm[:, t + k, :], ident[:, :], start=False, stop=(k == m - 1))
                    last.then_inc(s_y, 1)
                pe.wait_ge(s_xT, q + 1)
                for i, (t, m) in enumerate(((0, 16), (16, NT - 16))):
                    for k in range(m):
                        last = tr(bank[6 + i][:, k * F:(k + 1) * F], hT[:, (t + k) * P:(t + k + 1) * P], ident[0:F, 0:F])
                    last.then_inc(s_xTp, 1)
                if q < 2:
                    nc.tensor.nop().then_inc(s_cwuse, 1) if False else None

            for l in range(LAYERS):
                if l < 2:
                    prepare(l)
                if l in (0, 1, 2, 5):
                    h_transposed((0, 1, 2, 5).index(l))
                if l in ATT:
                    node_tables(l)
                    attention(l)
                    attention_nodes(l)
                else:
                    convolution(l)
                    conv_nodes(l)

        @block.scalar
        def _(act):
            def rank(g, u):
                first = isinstance(g, int) and g == 0
                if not first:
                    act.wait_ge(s_look, 2 * g)
                for k in range(2):
                    act.wait_ge(s_T, 2 * g + k + 1)
                    nc.scalar.activation(ohloT[k], trb[:, :].rearrange("p (j c) -> p j c", c=P)[:, :, 0:EP],
                                         ACT.Copy).then_inc(s_ohT, 1)
                for j in range(EB):
                    for k in range(2):
                        act.wait_ge(s_acc[k], EB * g + j + 1)
                        nc.scalar.activation(base_sb[k][:, j, :], hist[k], ACT.Copy).then_inc(s_cp[k], 1)
            batches(act, rank)
            cp = nc.scalar.activation

            def layernorm(n):
                act.wait_ge(s_var, n + 1)
                cp(lns[:, :], lns[:, :], ACT.Sqrt, bias=eps[:, 0:1]).then_inc(s_std, 1)

            def attention(l):
                a, pf = ATT[l], PF[l]

                def exps(g):
                    n = a * G + g + 1
                    act.wait_ge(s_dif, n)
                    cp(ex[:, :, :], dif[:, :, :], ACT.Exp).then_inc(s_exp, 1)

                def carries(g):
                    n = a * G + g + 1
                    act.wait_ge(s_dd, 3 * n)
                    cp(ww[:, :, :], dd[:, :, :], ACT.Exp).then_inc(s_ww, 1)

                def spread(g):
                    n = a * G + g + 1
                    act.wait_ge(s_wx, n)
                    cp(wE[0:pf, :], bank[2][0:pf, 0:2 * P], ACT.Copy).then_inc(s_wE, 1)

                def outs(g, u, o):
                    act.wait_ge(s_back, l * G + g + 1)
                    if not (isinstance(g, int) and g < 2):
                        act.wait_ge(s_outw[u], 16 * (per(u) * l + o))
                    elif l:
                        act.wait_ge(s_outw[u], 16 * per(u) * l)
                    cp(out_st[u][:, 0:pf + H], bank[3][:, 0:pf + H], ACT.Copy).then_inc(s_outst, 1)

                def body(g, u, o):
                    exps(g)
                    carries(g - 1)
                    outs(g - 2, u, o - 1)
                    spread(g - 1)
                exps(0)
                exps(1)
                carries(0)
                spread(0)
                body(2, 0, 1)
                body(3, 1, 1)
                with act.Fori(2, (G - 1) // 2) as i:
                    body(2 * i, 0, i)
                    body(2 * i + 1, 1, i)
                body(G - 1, 0, (G - 1) // 2)
                carries(G - 1)
                outs(G - 2, 1, (G - 2) // 2)
                spread(G - 1)
                outs(G - 1, 0, (G - 1) // 2)

            def attention_nodes(l):
                a, pf = ATT[l], PF[l]
                for i, (t, m) in enumerate(CH):
                    act.wait_ge(s_aT, NCH * a + i + 1)
                    cp(aT[i % 2][0:pf, 0:m * P], bank[4 + i % 2][0:pf, 0:m * P], ACT.Copy).then_inc(s_aTc, 1)

            def convolution(l):
                q = CONV[l]

                def body(g, u, o):
                    n = q * G + g + 1
                    act.wait_ge(s_tb, n)
                    if not (isinstance(g, int) and g < 2):
                        act.wait_ge(s_msg, n - 2)
                    view = tsb[u].rearrange("p k n -> p n k")
                    for b in range(4):
                        last = cp(view[:, 32 * b:32 * b + 32, :], bank[4 + b][:, :].rearrange("p (n k) -> p n k", k=16), ACT.Copy)
                    last.then_inc(s_tsb, 1)
                    if not (isinstance(g, int) and g < 2):
                        outs(g - 2, u, o - 1)

                def outs(g, u, o):
                    act.wait_ge(s_back, l * G + g + 1)
                    if isinstance(g, int) and g < 2:
                        act.wait_ge(s_outw[u], 16 * per(u) * l)
                    else:
                        act.wait_ge(s_outw[u], 16 * (per(u) * l + o))
                    cp(cout[u][:, :], bank[3][:, 0:F], ACT.Copy).then_inc(s_outst, 1)
                body(0, 0, 0)
                body(1, 1, 0)
                body(2, 0, 1)
                body(3, 1, 1)
                with act.Fori(2, (G - 1) // 2) as i:
                    body(2 * i, 0, i)
                    body(2 * i + 1, 1, i)
                body(G - 1, 0, (G - 1) // 2)
                outs(G - 2, 1, (G - 2) // 2)
                outs(G - 1, 0, (G - 1) // 2)

            def conv_nodes(l):
                q = CONV[l]
                for i, (t, m) in enumerate(CH):
                    act.wait_ge(s_y, NCH * q + i + 1)
                    cp(wide[0:F, t * P:(t + m) * P], bank[4 + i % 2][0:F, 0:m * P], ACT.Identity,
                       bias=cb[:, 3 * q:3 * q + 1]).then_inc(s_yc, 1)
                act.wait_ge(s_bnv, q + 1)
                cp(bn[:, 1:2], bn[:, 1:2], ACT.Sqrt, bias=eps[0:F, 0:1]).then_inc(s_bns, 1)

            for l in range(LAYERS):
                if l in (0, 1, 2, 5):
                    layernorm((0, 1, 2, 5).index(l))
                if l in ATT:
                    attention(l)
                    attention_nodes(l)
                else:
                    convolution(l)
                    conv_nodes(l)


LAYERS = 6
_NAMES = ["x", "src", "dst", "edge_attr_3"]
_SCRATCH = {
    "slots0": (NB * R, 1), "slots1": (NB * R, 4), "flags0": (NB, 1), "flags1": (NB, 1),
    "tab0": (DUMMY + 1, 36), "tab1": (DUMMY + 1, 64), "tab2": (DUMMY + 1, F), "tab3": (DUMMY + 1, F),
    "tab4": (DUMMY + 1, F), "tab5": (DUMMY + 1, F),
    "q0": (NT * P, H), "q1": (NT * P, F), "q5": (NT * P, P),
    "blk0": (NB, P + H), "blk1": (NB, F + H), "blk2": (NB, F), "blk3": (NB, F), "blk4": (NB, F), "blk5": (NB, P + H),
}


def kernel(**inputs):
    import numpy as np
    import concourse.bacc as bacc
    from concourse.bass_utils import run_bass_kernel_spmd as run

    nc = bacc.Bacc("TRN2", target_bir_lowering=False, num_devices=1)
    arrays, A = {}, {}
    for n, v in inputs.items():
        a = np.ascontiguousarray(v)
        arrays["in_" + n] = a
        A[n] = nc.dram_tensor("in_" + n, a.shape, mybir.dt.from_np(a.dtype), kind="ExternalInput").ap()
    D = {n: nc.dram_tensor("d_" + n, s, FP, kind="Internal").ap() for n, s in _SCRATCH.items()}
    for k in range(2):
        D[f"same{k}"] = nc.dram_tensor(f"d_same{k}", (NB,), U8, kind="Internal").ap()
    o = nc.dram_tensor("out", (NODES, F), FP, kind="ExternalOutput").ap()
    build(nc, A, o, D)
    return run(nc, [arrays], core_ids=[0]).results[0]["out"]
```

```python
import concourse.bass as bass
from concourse import mybir
from contextlib import ExitStack

FP = mybir.dt.float32
BF = mybir.dt.bfloat16
I32 = mybir.dt.int32
U8 = mybir.dt.uint8
ALU = mybir.AluOpType
ACT = mybir.ActivationFunctionType
AX = mybir.AxisListType

P = 128
NODES = 3125
EDGES = 100000
F = 32
H = 4
NT = (NODES + P - 1) // P
LASTN = NODES - (NT - 1) * P
EP = 125
ET = EDGES // EP
EB = 8
SORTS = ET // EB
R = 8
MAXBLOCKS = (EDGES + R * NODES) // R
G = (MAXBLOCKS + P - 1) // P
NB = G * P
RING = 4
DUMMY = NT * P
BIG = 1.0e30
EPS = 1e-5
INV_D8 = 8 ** -0.5
INV_F = F ** -0.5


class Chain:

    def __init__(self, eng, sem):
        self.eng, self.sem, self.n = eng, sem, 0

    def __call__(self, ins):
        ins.then_inc(self.sem, 1)
        self.n += 1
        self.eng.wait_ge(self.sem, self.n)

    def add(self, ins):
        ins.then_inc(self.sem, 1)
        self.n += 1

    def sync(self):
        self.eng.wait_ge(self.sem, self.n)


def build(nc, A, out, D, upto=99):
    ctx = ExitStack()
    with ctx:
        def sb(name, shape, dt=FP):
            return ctx.enter_context(nc.sbuf_tensor(name, shape, dt))

        def sem(name):
            return ctx.enter_context(nc.semaphore(name))

        bank = [ctx.enter_context(nc.psum_tensor(f"bank{i}", [P, 512], FP)) for i in range(8)]

        ident = sb("ident", [P, P])
        identb = sb("identb", [P, P], BF)
        iota_i = sb("iota_i", [P, P], I32)
        iota_b = sb("iota_b", [P, P], BF)
        below = sb("below", [P, P])
        above = sb("above", [P, P])
        ones = sb("ones", [P, P])
        onesb = sb("onesb", [P, 1])

        work = sb("work", [P, 11808])
        pos_ = [0]

        def carve(n, dt=FP, parts=P):
            k = n if dt in (FP, I32) else (n + 1) // 2
            a = work[0:parts, pos_[0]:pos_[0] + k]
            pos_[0] += k
            return a if dt == FP else a.bitcast(dt)

        key_i = [carve(ET, I32, EP) for _ in range(2)]
        key_f = [carve(ET, FP, EP) for _ in range(2)]
        lo_b = [carve(ET, BF, EP) for _ in range(2)]
        hi_b = [carve(ET, BF, EP) for _ in range(2)]
        payload = carve(ET * 4, FP, EP).rearrange("p (t c) -> p t c", c=4)
        tmp_i = carve(ET, I32, EP)
        attr = carve(ET * 3, FP, EP)
        conv = sb("conv", [P, 7168])
        cpos = [0]

        def carve2(n, dt=FP, parts=P):
            k = n if dt in (FP, I32) else (n + 1) // 2
            a = conv[0:parts, cpos[0]:cpos[0] + k]
            cpos[0] += k
            return a if dt == FP else a.bitcast(dt)

        ohlo = [[carve2(EB * P, BF, EP).rearrange("p (j c) -> p j c", c=P) for _ in range(2)] for _ in range(2)]
        ohhi = [[carve2(EB * NT, BF, EP).rearrange("p (j c) -> p j c", c=NT) for _ in range(2)] for _ in range(2)]
        ohloT = [carve2(EB * EP).rearrange("p (j c) -> p j c", c=EP) for _ in range(2)]
        base_sb = [carve2(EB * NT).rearrange("p (j c) -> p j c", c=NT) for _ in range(2)]
        junk = carve2(2 * EB * EP, BF, EP).rearrange("p (j c) -> p j c", c=EP)
        keys_st = [sb(f"keys_st{u}", [EP, 2, EB]) for u in range(2)]
        lo_st = [sb(f"lo_st{u}", [EP, 2, EB], BF) for u in range(2)]
        hi_st = [sb(f"hi_st{u}", [EP, 2, EB], BF) for u in range(2)]
        rank_in = sb("rank_in", [EP, 2, EB])
        picked = carve2(2 * EB * NT, FP, EP).rearrange("p (k j) -> p k j", k=2)
        baseline = sb("baseline", [EP, 2, EB])
        pos_st = [sb(f"pos_st{u}", [EP, 2, EB], I32) for u in range(2)]
        pay_st = [sb(f"pay_st{u}", [EP, EB, 4]) for u in range(2)]
        srt_st = [sb(f"srt_st{u}", [EP, EB]) for u in range(2)]
        deg = [sb(f"deg{k}", [P, NT]) for k in range(2)]
        nblk = [sb(f"nblk{k}", [P, NT]) for k in range(2)]
        nblk_i = sb("nblk_i", [P, NT], I32)
        start = [sb(f"start{k}", [P, NT]) for k in range(2)]
        start_i = [sb(f"start_i{k}", [P, NT], I32) for k in range(2)]
        last_i = [sb(f"last_i{k}", [P, NT], I32) for k in range(2)]
        tot = sb("tot", [P, NT])
        zero = sb("zero", [P, 512])
        gate_in = sb("gate_in", [16, 1])
        gate_out = sb("gate_out", [16, 1])
        fill = sb("fill", [P, 1024, 4])

        s_load = sem("s_load"); s_const = sem("s_const"); s_pool = sem("s_pool")
        s_dve = sem("s_dve"); s_gate = sem("s_gate")
        s_fill = sem("s_fill"); s_filled = sem("s_filled"); s_keys = sem("s_keys")
        s_oh = sem("s_oh"); s_hist = sem("s_hist"); s_histall = sem("s_histall")
        s_nblk = sem("s_nblk"); s_prefix = sem("s_prefix"); s_start = sem("s_start")
        s_base0 = sem("s_base0"); s_flag = sem("s_flag")
        s_oh2 = sem("s_oh2"); s_T = sem("s_T"); s_ohT = sem("s_ohT"); s_key = sem("s_key")
        s_cp = [sem(f"s_cp{k}") for k in range(2)]; s_acc = [sem(f"s_acc{k}") for k in range(2)]
        s_look = sem("s_look"); s_rank = sem("s_rank"); s_pick = sem("s_pick"); s_bl = sem("s_bl"); s_pay = sem("s_pay")
        s_pos = sem("s_pos"); s_sc = [sem(f"s_sc{u}") for u in range(2)]

        hist = [bank[0][:, 0:NT], bank[1][:, 0:NT]]
        look = [bank[2][0:EP, k * 256:k * 256 + EB * NT].rearrange("p (j c) -> p j c", c=NT) for k in range(2)]
        keyrow = [[bank[3 + 2 * 0 + (j // 4)][0:EP, (j % 4) * 128:(j % 4) * 128 + EP] for j in range(EB)],
                  [bank[5 + (j // 4)][0:EP, (j % 4) * 128:(j % 4) * 128 + EP] for j in range(EB)]]
        trb = bank[7].bitcast(BF) if hasattr(bank[7], 'bitcast') else bank[7][:, :].bitcast(BF)

        x = sb("x", [P, NT, F])
        h = sb("h", [P, NT, F])
        hT = sb("hT", [F, NT * P])
        wide = sb("wide", [P, NT * P])
        comb = sb("comb", [P, G * 32])
        fill0 = comb[:, 0:1024]
        lnm = sb("lnm", [P, NT])
        lns = sb("lns", [P, NT])
        rcnt = sb("rcnt", [P, NT])
        eps = sb("eps", [P, 1])
        idx_a = sb("idx_a", [P, G + RING, R], I32)
        idx_c = sb("idx_c", [P, G + RING, R], I32)
        valid = sb("valid", [P, G, R])
        pen = sb("pen", [P, G, R])
        same = sb("same", [F, NB], U8)
        idx_st = [sb(f"idx_st{b}", [P, R], I32) for b in range(RING)]
        rows = [sb(f"rows{b}", [P, R * 64]) for b in range(RING)]
        window = [sb(f"window{u}", [P, P]) for u in range(2)]
        spread_q = [sb(f"spread_q{u}", [P, P]) for u in range(2)]
        loc_g = sb("loc_g", [G, P], U8)
        first_i = sb("first_i", [G, 1], I32)
        part_f = sb("part_f", [P, 1])
        flg = sb("flg", [G, P])
        cum = sb("cum", [G, P])
        starts_g = sb("starts_g", [G, 1])
        same_g = sb("same_g", [G, P], U8)
        fill_all = fill[:, :, :].rearrange("p c a -> p (c a)")
        loc = fill_all.bitcast(U8)[:, 0:(G + 2) * P]
        w0 = sb("w0", [F, H, F]); w0cat = sb("w0cat", [P, F]); fcw = sb("fcw", [F, 2, F]); fcb = sb("fcb", [P, 1])
        bias0 = sb("bias0", [P, F]); wa = sb("wa", [F, 2 * H]); wtmp = sb("wtmp", [F, H, F])
        wkvq = sb("wkvq", [F, 3 * F]); wo = sb("wo", [F, F])
        w3 = sb("w3", [F, 3, H * F]); w3T = sb("w3T", [F, 3, H * F]); wout = sb("wout", [F, F])
        wqk = sb("wqk", [F, H * F]); wvo = sb("wvo", [F, H * F]); wvocat = sb("wvocat", [P, F])
        cw = sb("cw", [P, 16, F]); cr = sb("cr", [F, 3, F]); cb = sb("cb", [F, 9])
        sel = sb("sel", [H, 2, P]); sel_i = sb("sel_i", [H, 2, P], I32)
        mask = sb("mask", [P, P // R, 16]); mask_i = comb[:, 1024:1024 + 2 * P].bitcast(I32).rearrange("p (b k) -> p b k", b=P // R)
        prt_i = sb("prt_i", [P, 1], I32); prt_f = sb("prt_f", [P, 1])
        cpos[0] = 0
        prod = carve2(1024)
        wE = carve2(256)
        out_st = [carve2(132) for _ in range(2)]
        aT = [carve2(512) for _ in range(2)]
        numS = [carve2(P) for _ in range(2)]
        num1 = carve2(P)
        tab = carve2(NT * 64)
        part = carve2(P)
        sc_ = sb("sc_", [P, R, H]); dif = sb("dif", [P, R, H]); ex = sb("ex", [P, R, H])
        stat = sb("stat", [P, 2 * H])
        runmax = sb("runmax", [H, P + 1]); penr = sb("penr", [H, P]); dd = sb("dd", [H, 2, P]); ww = sb("ww", [H, 2, P])
        den1 = sb("den1", [H, P]); denS = [sb(f"denS{u}", [H, P]) for u in range(2)]
        cpos[0] = 0
        tsb = [carve2(16 * P).rearrange("p (k b) -> p k b", b=P) for _ in range(2)]
        xb = [carve2(R * P).rearrange("p (j k c) -> p j k c", j=R, c=F) for _ in range(2)]
        m12 = [fill_all[:, u * 2048:(u + 1) * 2048].rearrange("p (j c) -> p j c", j=R) for u in range(2)]
        b12 = sb("b12", [P, R, 16])
        aggS = [sb(f"aggS{u}", [F, P]) for u in range(2)]
        cout = [sb(f"cout{u}", [P, F]) for u in range(2)]
        hats = work[:, 0:G * R * 12].rearrange("p (s d k) -> p s d k", d=3, k=4)
        attr_c = wide[:, 0:3 * G * R].rearrange("p (d g j) -> p d g j", d=3, j=R)
        ytmp = comb[0:F, 0:NT * P]
        bn = sb("bn", [F, 8])
        NW = 26
        s_slread = sem("s_slread"); s_yn = sem("s_yn")
        done_of = {0: 1, 1: 2, 4: 3, 5: 4}
        s_xpad = sem("s_xpad"); s_xl = sem("s_xl")

        s_w = sem("s_w"); s_sel = sem("s_sel"); s_prep = sem("s_prep"); s_off = sem("s_off"); s_nid = sem("s_nid")
        s_first = sem("s_first"); s_win = [sem(f"s_win{u}") for u in range(2)]; s_E = sem("s_E"); s_q = sem("s_q"); s_same = sem("s_same"); s_samew = sem("s_samew"); s_samer = sem("s_samer"); s_slots = sem("s_slots")
        s_wT = sem("s_wT"); s_wp = sem("s_wp"); s_vo = sem("s_vo"); s_vod = sem("s_vod")
        s_slT = sem("s_slT"); s_slc = sem("s_slc")
        s_var = sem("s_var"); s_std = sem("s_std"); s_h = sem("s_h"); s_hTp = sem("s_hTp"); s_hTc = sem("s_hTc")
        s_tp = sem("s_tp"); s_tc = sem("s_tc"); s_tabr = sem("s_tabr"); s_tabw = sem("s_tabw")
        s_stage = sem("s_stage"); s_rows = [sem(f"s_rows{b}") for b in range(RING)]
        s_prod = sem("s_prod"); s_raw = sem("s_raw"); s_scored = sem("s_scored"); s_bmax = sem("s_bmax"); s_dif = sem("s_dif")
        s_exp = sem("s_exp"); s_ev = sem("s_ev"); s_den = sem("s_den"); s_wv = sem("s_wv"); s_part = sem("s_part")
        s_partT = sem("s_partT"); s_penr = sem("s_penr"); s_carry = sem("s_carry"); s_runmax = sem("s_runmax")
        s_dd = sem("s_dd"); s_ww = sem("s_ww"); s_w0 = sem("s_w0"); s_wx = sem("s_wx"); s_wE = sem("s_wE")
        s_den1 = sem("s_den1"); s_denS = sem("s_denS"); s_num1 = sem("s_num1"); s_numS = sem("s_numS")
        s_back = sem("s_back"); s_outst = sem("s_outst"); s_outw = [sem(f"s_outw{u}") for u in range(2)]
        s_comb = sem("s_comb"); s_norm = sem("s_norm"); s_aT = sem("s_aT"); s_aTc = sem("s_aTc"); s_fin = sem("s_fin")
        s_xb = sem("s_xb"); s_b12 = sem("s_b12"); s_m12 = sem("s_m12"); s_tb = sem("s_tb"); s_tsb = sem("s_tsb")
        s_msg = sem("s_msg"); s_agg = sem("s_agg"); s_y = sem("s_y"); s_yc = sem("s_yc"); s_bnv = sem("s_bnv"); s_bns = sem("s_bns")
        s_xT = sem("s_xT"); s_xTp = sem("s_xTp"); s_cw = sem("s_cw"); s_cwuse = sem("s_cwuse"); s_xout = sem("s_xout"); s_done = sem("s_done")

        CH = [(c, min(4, NT - c)) for c in range(0, NT, 4)]
        NCH = len(CH)
        ATT = {0: 0, 1: 1, 5: 2}
        CONV = {2: 0, 3: 1, 4: 2}
        TABF = {0: 36, 1: 64, 2: F, 3: F, 4: F, 5: F}
        QF = {0: H, 1: F, 5: H * F}
        PF = {0: P, 1: F, 5: P}
        WAYS = {0: 2 * H, 1: 3 * F, 5: H * F}

        tabw = {l: sum(64 if m in ATT else 32 for m in range(l + 1)) for l in range(LAYERS)}

        def per(u):
            return G // 2 + (1 - u)

        def groups(eng, body):
            body(0, 0, 0)
            with eng.Fori(0, (G - 1) // 2) as i:
                body(2 * i + 1, 1, i)
                body(2 * i + 2, 0, i + 1)

        def ring(b):
            return (G - b + RING - 1) // RING

        def quads(eng, body, first=0):
            for g in range(first, 3):
                body(g, g % 2, g, 0)
            assert (G - 3) % RING == 0 and RING == 4
            with eng.Fori(0, (G - 3) // RING) as i:
                body(RING * i + 3, 1, 3, i)
                for b in range(3):
                    body(RING * i + 4 + b, b % 2, b, i + 1)

        def batches(eng, body):
            body(0, 0)
            body(1, 1)
            with eng.Fori(1, SORTS // 2) as i:
                for u in range(2):
                    body(2 * i + u, u)

        block = ctx.enter_context(nc.Block())

        @block.sync
        def _(sp):
            n = 0
            for k, name in enumerate(("src", "dst")):
                sp.dma_start(key_i[k], A[name].rearrange("(p t) -> p t", p=EP)).then_inc(s_load, 16)
            with nc.allow_non_contiguous_dma(reason="single columns of a few small vectors"):
                W = []
                W.append(sp.dma_start(x[:, 0:NT - 1, :], A["x"][0:(NT - 1) * P, :].rearrange("(t p) f -> p t f", p=P)))
                W.append(sp.dma_start(w0[:, :, :], A["L0_gnn_w"].rearrange("h f o -> f h o")))
                W.append(sp.dma_start(w0cat[:, :], A["L0_gnn_w"].rearrange("h f o -> (h f) o")))
                W.append(sp.dma_start(fcw[:, :, :], A["L0_gnn_fc_w"].rearrange("a (s o) -> a s o", s=2).to_broadcast([F, 2, F])))
                W.append(sp.dma_start(fcb[:, :], A["L0_gnn_fc_b"].rearrange("(a b) -> a b", b=1).to_broadcast([P, 1])))
                W.append(sp.dma_start(bias0[:, :], A["L0_gnn_bias"].rearrange("(a b) -> a b", a=1).to_broadcast([P, F])))
                for i, name in enumerate(("Wk", "Wv", "Wq")):
                    W.append(sp.dma_start(wkvq[:, i * F:(i + 1) * F], A["L1_gnn_" + name]))
                W.append(sp.dma_start(wo[:, :], A["L1_gnn_Wo"]))
                for i, name in enumerate(("Wq", "Wk", "Wv")):
                    W.append(sp.dma_start(w3[:, i, :].rearrange("f (h o) -> f h o", h=H), A["L3_gnn_" + name].rearrange("h f o -> f h o")))
                W.append(sp.dma_start(wout[:, :], A["L3_gnn_Wout"]))
                for i in range(3):
                    W.append(sp.dma_start(cr[:, i, :], A[f"L2_gnn_R{i + 1}"]))
                    for j, name in enumerate(("b", "g", "be")):
                        W.append(sp.dma_start(cb[:, 3 * i + j:3 * i + j + 1], A[f"L2_gnn_{name}{i + 1}"].rearrange("(c a) -> c a", a=1)))
                for ins in W:
                    ins.then_inc(s_w, 16)
                assert len(W) == NW, len(W)
                sp.wait_ge(s_xpad, 1)
                sp.dma_start(x[0:LASTN, NT - 1, :], A["x"][(NT - 1) * P:NODES, :]).then_inc(s_xl, 16)
            sp.dma_start(attr, A["edge_attr_3"].rearrange("(p t) c -> p (t c)", p=EP)).then_inc(s_load, 16)
            sp.wait_ge(s_fill, 4)
            sp.dma_start(D["slots0"].rearrange("(g c) a -> g (c a)", g=G), comb[0:G, 0:1024]).then_inc(s_filled, 16)
            sp.dma_start(D["slots1"].rearrange("(g c) a -> g (c a)", g=G), fill[0:G, :, :].rearrange("p c a -> p (c a)")).then_inc(s_filled, 16)
            for k in range(2):
                sp.dma_start(D[f"flags{k}"].rearrange("(g c) a -> g (c a)", g=G), zero[0:G, 0:P]).then_inc(s_filled, 16)
            for u in range(2):
                sp.wait_ge(s_sc[u], (SORTS // 2) * 2 * EB * 16)
            sp.wait_ge(s_flag, 2 * NT * 16)

            def load_groups(k):
                sp.dma_start(flg[:, :], D[f"flags{k}"].rearrange("(g p) a -> g (p a)", p=P)).then_inc(s_slots, 16)
                w = 4 if k else 1
                sp.dma_start(comb[:, 0:G * R * w].rearrange("p (g c) -> p g c", g=G),
                             D[f"slots{k}"].rearrange("(g p r) a -> p g (r a)", p=P, r=R)).then_inc(s_slots, 16)
                if k:
                    sp.dma_start(fill_all[0:G, :], D["slots1"].rearrange("(g c) a -> g (c a)", g=G)).then_inc(s_slots, 16)
                sp.wait_ge(s_same, 2 * (k + 1))
                sp.dma_start(D[f"same{k}"].rearrange("(g p) -> g p", p=P), same_g[:, :]).then_inc(s_samew, 16)
                sp.dma_start(D[f"loc{k}"].rearrange("(g p) -> g p", p=P), loc_g[:, :]).then_inc(s_samew, 16)
                sp.wait_ge(s_nid, k + 1)
                sp.dma_start(D[f"first{k}"].rearrange("(g a) -> g a", a=1), first_i[:, :]).then_inc(s_samew, 16)
                sp.wait_ge(s_samew, 48 * (k + 1))
                sp.dma_start(same[:, :], D[f"same{k}"].rearrange("(a n) -> a n", a=1).to_broadcast([F, NB])).then_inc(s_samer, 16)
                if k:
                    sp.wait_ge(s_slc, 32)
                load_loc(k)

            def load_loc(k):
                sp.dma_start(loc[:, 0:NB], D[f"loc{k}"].rearrange("(a n) -> a n", a=1).to_broadcast([P, NB])).then_inc(s_samer, 16)

            def tables(l):
                sp.wait_ge(s_tabr, l + 1)
                f = TABF[l]
                rowsrc = (tab[:, 0:NT * f].rearrange("p (t c) -> p t c", c=f) if l in (0, 1) else h[:, :, :])
                sp.dma_start(D[f"tab{l}"][0:NT * P, :].rearrange("(t p) c -> p t c", p=P), rowsrc).then_inc(s_tabw, 16)
                sp.dma_start(D[f"tab{l}"][NT * P:NT * P + 1, :], zero[0:1, 0:f]).then_inc(s_tabw, 16)
                if l in QF:
                    q = QF[l]
                    sp.dma_start(D[f"q{l}"][NT * P:, :], zero[:, 0:q]).then_inc(s_tabw, 16)
                    sp.dma_start(D[f"q{l}"][0:NT * P, :].rearrange("(t p) c -> p t c", p=P),
                                 wide[:, 0:NT * q].rearrange("p (t c) -> p t c", c=q)).then_inc(s_tabw, 16)

            def blocks_out(l):
                w = PF[l] + H if l in ATT else F
                src = out_st if l in ATT else cout

                def store(g, u, o):
                    sp.wait_ge(s_outst, l * G + g + 1)
                    sp.dma_start(D[f"blk{l}"].rearrange("(g p) c -> g p c", p=P)[bass.ds(g, 1), :, :].rearrange("a p c -> (a p) c"),
                                 src[u][:, 0:w]).then_inc(s_outw[u], 16)

                def fetch(g, u, o):
                    k = 0 if l == 0 else 1
                    n0 = sp.value_load(D[f"first{k}"].rearrange("(a g) -> a g", a=1)[:, bass.ds(g, 1)], min_val=0, max_val=NODES - 1)
                    if not (isinstance(g, int) and g < 2):
                        sp.wait_ge(s_q, ATT[l] * G + g - 1)
                    sp.dma_start(window[u][:, 0:QF[l]], D[f"q{l}"][bass.ds(n0, P), :]).then_inc(s_win[u], 16)

                if l not in ATT:
                    groups(sp, store)
                    return
                sp.wait_ge(s_tabw, tabw[l])
                for g in range(4):
                    fetch(g, g % 2, g // 2)
                store(0, 0, 0)
                fetch(4, 0, 2)
                store(1, 1, 0)
                with sp.Fori(2, (G - 1) // 2) as i:
                    fetch(2 * i + 1, 1, i)
                    store(2 * i - 2, 0, i - 1)
                    fetch(2 * i + 2, 0, i + 1)
                    store(2 * i - 1, 1, i - 1)
                for g in range(G - 3, G):
                    store(g, g % 2, g // 2)

            sp.wait_ge(s_vo, 1)
            for hh in range(H):
                sp.dma_start(wvocat[hh * F:(hh + 1) * F, :], wvo[:, hh * F:(hh + 1) * F]).then_inc(s_vod, 16)
            for l in range(LAYERS):
                if l < 2:
                    if l:
                        sp.wait_ge(s_done, 1)
                    load_groups(l)
                if l in CONV:
                    if CONV[l]:
                        sp.wait_ge(s_msg, CONV[l] * G)
                    sp.dma_start(cw[:, :, :], A[f"L2_gnn_W{CONV[l] + 1}"].rearrange("(k q) c o -> (q c) k o", q=4)).then_inc(s_cw, 16)
                if l == 5:
                    sp.wait_ge(s_msg, 3 * G)
                    load_loc(1)
                tables(l)
                blocks_out(l)
            sp.wait_ge(s_done, LAYERS if LAYERS < 3 else max(2, LAYERS - 2))
            sp.dma_start(out[0:(NT - 1) * P, :].rearrange("(t p) f -> p t f", p=P), x[:, 0:NT - 1, :]).then_inc(s_xout, 16)
            sp.dma_start(out[(NT - 1) * P:NODES, :], x[0:LASTN, NT - 1, :]).then_inc(s_xout, 16)
            sp.wait_ge(s_xout, 32)

        @block.gpsimd
        def _(pool):
            c = Chain(pool, s_pool)
            c.add(nc.gpsimd.memset(ident[:, :], 0.0))
            c.add(nc.gpsimd.memset(below[:, :], 1.0))
            c.add(nc.gpsimd.memset(above[:, :], 1.0))
            c.add(nc.gpsimd.memset(ones[:, :], 1.0))
            c(nc.gpsimd.iota(iota_i[:, :], pattern=[[1, P]], base=0, channel_multiplier=0))
            nc.gpsimd.affine_select(out=ident[:, :], in_=ident[:, :], compare_op=ALU.not_equal, fill=1.0, base=0,
                                    pattern=[[-1, P]], channel_multiplier=1).then_inc(s_const, 1)
            nc.gpsimd.affine_select(out=below[:, :], in_=below[:, :], compare_op=ALU.is_gt, fill=0.0, base=0,
                                    pattern=[[-1, P]], channel_multiplier=1).then_inc(s_const, 1)
            nc.gpsimd.affine_select(out=above[:, :], in_=above[:, :], compare_op=ALU.is_gt, fill=0.0, base=0,
                                    pattern=[[1, P]], channel_multiplier=-1).then_inc(s_const, 1)
            nc.gpsimd.memset(gate_in[:, :], 0.0).then_inc(s_const, 1)
            nc.gpsimd.iota(sel_i[:, 0, :].rearrange("p (a b) -> p a b", a=H), pattern=[[1, H], [0, F]], base=0, channel_multiplier=-1).then_inc(s_const, 1)
            nc.gpsimd.iota(sel_i[:, 1, :].rearrange("p (a b) -> p a b", b=R), pattern=[[1, P // R], [0, R]], base=0, channel_multiplier=-1).then_inc(s_const, 1)
            nc.gpsimd.iota(mask_i, pattern=[[1, P // R], [0, 16]], base=0, channel_multiplier=0).then_inc(s_const, 1)
            nc.gpsimd.iota(prt_i[:, :], pattern=[[0, 1]], base=0, channel_multiplier=1).then_inc(s_const, 1)
            pool.wait_ge(s_const, 8)
            gates = [0]

            def gate(*waits):
                pool.wait_ge(s_gate, gates[0])
                for s, v in waits:
                    pool.wait_ge(s, v)
                nc.gpsimd.tensor_tensor(gate_out[:, :], gate_in[:, :], gate_in[:, :], ALU.add).then_inc(s_gate, 1)
                gates[0] = gates[0] + 1

            pool.wait_ge(s_filled, 64)
            pool.wait_ge(s_start, 2)
            for k in range(2):
                for t in range(NT):
                    n = P if t < NT - 1 else LASTN
                    pool.indirect_dma_start(
                        out=D[f"flags{k}"], out_offset=bass.IndirectOffsetOnAxis(ap=start_i[k][0:n, t:t + 1], axis=0),
                        in_=ones[0:n, 0:1], in_offset=None).then_inc(s_flag, 16)

            def scatter(g, u):
                gates[0] = g
                gate((s_pos, g + 1))
                for j in range(EB):
                    pool.indirect_dma_start(
                        out=D["slots1"], out_offset=bass.IndirectOffsetOnAxis(ap=pos_st[u][:, 1, j:j + 1], axis=0),
                        in_=pay_st[u][:, j, :], in_offset=None).then_inc(s_sc[u], 16)
                    pool.indirect_dma_start(
                        out=D["slots0"], out_offset=bass.IndirectOffsetOnAxis(ap=pos_st[u][:, 0, j:j + 1], axis=0),
                        in_=srt_st[u][:, j:j + 1], in_offset=None).then_inc(s_sc[u], 16)
            batches(pool, scatter)
            for l in range(LAYERS):

                def gather(g, u, b, o):
                    gates[0] = SORTS + l * G + g
                    need = [(s_stage, l * (G + RING) + g + 1)]
                    if isinstance(g, int) and g == 0:
                        need.append((s_tabw, tabw[l]))
                    gate(*need)
                    f = TABF[l]
                    for r in range(R):
                        pool.indirect_dma_start(
                            out=rows[b][:, r * f:(r + 1) * f], out_offset=None, in_=D[f"tab{l}"],
                            in_offset=bass.IndirectOffsetOnAxis(ap=idx_st[b][:, r:r + 1], axis=0)).then_inc(s_rows[b], 16)
                quads(pool, gather)
                pool.wait_ge(s_outw[0], 16 * (G // 2 + 1) * (l + 1))
                pool.wait_ge(s_outw[1], 16 * (G // 2) * (l + 1))
                if l == 1:
                    pool.wait_ge(s_slread, 1)
                w = PF[l] + H if l in ATT else F
                for t in range(NT):
                    pool.indirect_dma_start(
                        out=comb[:, t * w:(t + 1) * w], out_offset=None, in_=D[f"blk{l}"],
                        in_offset=bass.IndirectOffsetOnAxis(ap=last_i[0 if l == 0 else 1][:, t:t + 1], axis=0)).then_inc(s_comb, 16)

        @block.vector
        def _(dve):
            c = Chain(dve, s_dve)
            v = nc.vector
            v.memset(fill[:, :, 1:4], 0.0).then_inc(s_fill, 1)
            v.memset(fill[:, :, 0:1], float(DUMMY)).then_inc(s_fill, 1)
            v.memset(fill0, float(DUMMY)).then_inc(s_fill, 1)
            v.memset(zero[:, :], 0.0).then_inc(s_fill, 1)
            dve.wait_ge(s_const, 8)
            c.add(v.tensor_copy(identb[:, :], ident[:, :]))
            c.add(v.tensor_copy(iota_b[:, :], iota_i[:, :]))
            c(v.memset(onesb[:, :], 1.0))
            v.memset(x[:, NT - 1, :], 0.0).then_inc(s_xpad, 1)
            c.add(v.memset(eps[:, :], EPS))
            c.add(v.memset(idx_a[:, G:, :], 0))
            c(v.memset(idx_c[:, G:, :], 0))
            c.add(v.tensor_single_scalar(sel[:, :, :], sel_i[:, :, :], 0.0, op=ALU.is_equal))
            c(v.tensor_copy(part_f[:, :], prt_i[:, :]))
            c(v.tensor_single_scalar(prt_i[:, :], prt_i[:, :], R.bit_length() - 1, op=ALU.arith_shift_right))
            c(v.tensor_copy(prt_f[:, :], prt_i[:, :]))
            c(v.tensor_scalar(mask[:, :, :], mask_i, prt_f[:, 0:1], None, ALU.is_equal))
            dve.wait_ge(s_w, 16 * NW)
            for i in range(2):
                c(v.tensor_tensor(wtmp[:, :, :], w0[:, :, :], fcw[:, i:i + 1, :].to_broadcast([F, H, F]), ALU.mult))
                c(v.tensor_reduce(wa[:, i * H:(i + 1) * H], wtmp[:, :, :], AX.X, ALU.add))
            for i in range(3):
                v.transpose(w3T[:, i, :], w3[:, i, :]).then_inc(s_wT, 1)
            dve.wait_ge(s_load, 48)
            for k in range(2):
                c.add(v.tensor_copy(key_f[k], key_i[k]))
                c(v.tensor_single_scalar(tmp_i, key_i[k], 127, op=ALU.bitwise_and))
                c(v.tensor_copy(lo_b[k], tmp_i))
                c(v.tensor_single_scalar(tmp_i, key_i[k], 7, op=ALU.arith_shift_right))
                c(v.tensor_copy(hi_b[k], tmp_i))
            c.add(v.tensor_copy(payload[:, :, 0], key_f[0]))
            c(v.tensor_copy(payload[:, :, 1:4], attr.rearrange("p (t c) -> p t c", c=3)))

            def onehots(g, u, done):
                for k in range(2):
                    v.tensor_tensor(ohlo[k][u], iota_b[0:EP, None, :].to_broadcast([EP, EB, P]),
                                    lo_b[k][:, bass.ds(g * EB, EB)].unsqueeze(2).to_broadcast([EP, EB, P]),
                                    ALU.is_equal).then_inc(done, 1)
                    v.tensor_tensor(ohhi[k][u], iota_b[0:EP, None, 0:NT].to_broadcast([EP, EB, NT]),
                                    hi_b[k][:, bass.ds(g * EB, EB)].unsqueeze(2).to_broadcast([EP, EB, NT]),
                                    ALU.is_equal).then_inc(done, 1)

            def count(g, u):
                if not (isinstance(g, int) and g < 2):
                    dve.wait_ge(s_hist, g - 1)
                onehots(g, u, s_oh)
            batches(dve, count)

            dve.wait_ge(s_histall, 2)
            for k in range(2):
                c(v.tensor_copy(deg[k][:, :], hist[k]))
                c(v.tensor_scalar(tot[:, :], deg[k][:, :], 1.0, float(R - 1), ALU.max, ALU.add))
                c(v.tensor_copy(nblk_i[:, :], tot[:, :]))
                c(v.tensor_single_scalar(nblk_i[:, :], nblk_i[:, :], R.bit_length() - 1, op=ALU.arith_shift_right))
                c(v.tensor_copy(nblk[k][:, :], nblk_i[:, :]))
                v.sem_inc(s_nblk, 1) if False else v.tensor_copy(tot[:, :], nblk[k][:, :]).then_inc(s_nblk, 1)
                dve.wait_ge(s_prefix, k + 1)
                c(v.tensor_copy(tot[:, :], bank[3][:, NT:2 * NT]))
                c(v.tensor_tensor_scan(start[k][:, :], ones[:, 0:NT], tot[:, :], 0.0, ALU.mult, ALU.add))
                c(v.tensor_tensor(start[k][:, :], start[k][:, :], tot[:, :], ALU.subtract))
                c(v.tensor_tensor(start[k][:, :], start[k][:, :], bank[3][:, 0:NT], ALU.add))
                c(v.tensor_tensor(tot[:, :], start[k][:, :], nblk[k][:, :], ALU.add))
                c(v.tensor_scalar(tot[:, :], tot[:, :], -1.0, None, ALU.add))
                c(v.tensor_copy(last_i[k][:, :], tot[:, :]))
                c(v.tensor_copy(start_i[k][:, :], start[k][:, :]))
                v.tensor_scalar(start[k][:, :], start[k][:, :], float(R), None, ALU.mult).then_inc(s_start, 1)
            dve.wait_ge(s_start, 2)

            def columns(g, u):
                onehots(g, u, s_oh2)
                for k in range(2):
                    v.tensor_copy(lo_st[u][:, k, :], lo_b[k][:, bass.ds(g * EB, EB)]).then_inc(s_oh2, 1)
                    v.tensor_scalar(hi_st[u][:, k, :], hi_b[k][:, bass.ds(g * EB, EB)], 128.0, None, ALU.mult).then_inc(s_oh2, 1)
                    v.tensor_copy(keys_st[u][:, k, :], key_f[k][:, bass.ds(g * EB, EB)]).then_inc(s_oh2, 1)

            def positions(g, u):
                dve.wait_ge(s_key, g + 1)
                for k in range(2):
                    for j in range(EB):
                        v.scalar_tensor_tensor(junk[:, k * EB + j, :], keyrow[k][j], keys_st[u][:, k, j:j + 1],
                                               below[0:EP, 0:EP], ALU.is_equal, ALU.mult,
                                               accum_out=rank_in[:, k, j:j + 1]).then_inc(s_rank, 1)
                dve.wait_ge(s_look, 2 * g + 2)
                for k in range(2):
                    v.tensor_tensor(picked[:, k, :].rearrange("p (j c) -> p j c", c=NT), look[k], ohhi[k][u],
                                    ALU.mult).then_inc(s_pick, 1)
                dve.wait_ge(s_pick, 2 * g + 2)
                v.tensor_reduce(baseline[:, :, :].rearrange("p k j -> p (k j)"),
                                picked[:, :, :].rearrange("p k (j c) -> p (k j) c", c=NT), AX.X, ALU.add).then_inc(s_bl, 1)
                if not (isinstance(g, int) and g < 2):
                    dve.wait_ge(s_sc[u], (g - u) * (EB * 16))
                v.tensor_copy(pay_st[u][:, :, :], payload[:, bass.ds(g * EB, EB), :]).then_inc(s_pay, 1)
                v.tensor_copy(srt_st[u][:, :], key_f[1][:, bass.ds(g * EB, EB)]).then_inc(s_pay, 1)
                dve.wait_ge(s_pay, 2 * g + 2)
                dve.wait_ge(s_bl, g + 1)
                dve.wait_ge(s_rank, 16 * g + 16)
                v.tensor_tensor(pos_st[u][:, :, :], baseline[:, :, :], rank_in[:, :, :], ALU.add).then_inc(s_pos, 1)
                dve.wait_ge(s_pos, g + 1)

            columns(0, 0)
            columns(1, 1)
            positions(0, 0)
            with dve.Fori(1, SORTS // 2) as i:
                columns(2 * i, 0)
                positions(2 * i - 1, 1)
                columns(2 * i + 1, 1)
                positions(2 * i, 0)
            positions(SORTS - 1, 1)

            dve.wait_ge(s_wp, 1)
            c.add(v.tensor_scalar(wqk[:, :], bank[3][0:F, 0:P], INV_F, None, ALU.mult))
            v.tensor_scalar(wvo[:, :], bank[3][0:F, P:2 * P], 1.0 / H, None, ALU.mult).then_inc(s_vo, 1)
            c.add(v.tensor_scalar(w0cat[:, :], w0cat[:, :], 1.0 / H, None, ALU.mult))
            c(v.tensor_scalar(wkvq[:, 2 * F:3 * F], wkvq[:, 2 * F:3 * F], INV_D8, None, ALU.mult))
            c(v.tensor_scalar(rcnt[:, :], deg[1][:, :], 1.0, None, ALU.max))
            c(v.reciprocal(rcnt[:, :], rcnt[:, :]))
            dve.wait_ge(s_xl, 16)

            def prepare(k):
                dve.wait_ge(s_slots, 32 if k == 0 else 80)
                c(v.tensor_tensor_scan(cum[:, :], ones[0:G, :], flg[:, :], 0.0, ALU.mult, ALU.add))
                v.tensor_copy(starts_g[:, :], cum[:, P - 1:P]).then_inc(s_prep, 1)
                v.tensor_scalar(same_g[:, :], flg[:, :], -1.0, 1.0, ALU.mult, ALU.add).then_inc(s_same, 1)
                v.tensor_scalar(loc_g[:, :], cum[:, :], cum[:, 0:1], None, ALU.subtract).then_inc(s_same, 1)
                dve.wait_ge(s_off, k + 1)
                v.tensor_scalar(first_i[:, :], cum[:, 0:1], bank[3][0:G, 0:1], -1.0, ALU.add, ALU.add).then_inc(s_nid, 1)
                w = 4 if k else 1
                slot = comb[:, 0:G * R * w].rearrange("p (g r c) -> p g r c", r=R, c=w)[:, :, :, 0]
                c.add(v.tensor_copy(idx_a[:, 0:G, 0:R], slot))
                c(v.tensor_scalar(valid[:, :, :], slot, float(DUMMY), None, ALU.is_lt))
                c(v.tensor_scalar(pen[:, :, :], valid[:, :, :], -1.0, BIG, ALU.add, ALU.mult))
                if k:
                    for n, (j, fld) in enumerate((j, fld) for j in range(R) for fld in range(4)):
                        dve.wait_ge(s_slT, n + 1)
                        dst = idx_c[:, 0:G, j] if fld == 0 else attr_c[:, fld - 1, :, j]
                        v.tensor_copy(dst, bank[4 + n % 2][:, 0:G]).then_inc(s_slc, 1)
                    dve.wait_ge(s_slc, 32)
                    flat = wide[:, 0:3 * G * R]
                    c(v.tensor_scalar(flat, flat, 3.0, 0.0, ALU.mult, ALU.max))
                    c(v.tensor_scalar(flat, flat, 3.0, None, ALU.min))
                    line = comb[:, 0:G * R]
                    for d in range(3):
                        a = wide[:, d * G * R:(d + 1) * G * R]
                        for kk in range(4):
                            c(v.tensor_scalar(line, a, -1.0, 1.0 + kk, ALU.mult, ALU.add))
                            c(v.scalar_tensor_tensor(hats[:, :, d, kk], a, 1.0 - kk, line, ALU.add, ALU.min))
                    hf = work[:, 0:G * R * 12]
                    v.tensor_scalar(hf, hf, 0.0, None, ALU.max).then_inc(s_slread, 1)
                    dve.wait_ge(s_slread, 1)
                dve.wait_ge(s_samer, 32 * (k + 1))

            def layernorm(n):
                cx = comb[:, 0:NT * F].rearrange("p (t f) -> p t f", f=F)
                sq = wide[:, 0:NT * F].rearrange("p (t f) -> p t f", f=F)
                c(v.tensor_reduce(lnm[:, :], x[:, :, :], AX.X, ALU.add))
                c(v.tensor_scalar(lnm[:, :], lnm[:, :], 1.0 / F, None, ALU.mult))
                c(v.tensor_tensor(cx, x[:, :, :], lnm[:, :].unsqueeze(2).to_broadcast([P, NT, F]), ALU.subtract))
                c(v.tensor_tensor(sq, cx, cx, ALU.mult))
                c(v.tensor_reduce(lns[:, :], sq, AX.X, ALU.add))
                v.tensor_scalar(lns[:, :], lns[:, :], 1.0 / F, None, ALU.mult).then_inc(s_var, 1)
                dve.wait_ge(s_std, n + 1)
                c(v.reciprocal(lns[:, :], lns[:, :]))
                c(v.tensor_tensor(cx, cx, lns[:, :].unsqueeze(2).to_broadcast([P, NT, F]), ALU.mult))
                v.tensor_scalar(h[:, :, :], cx, 0.0, None, ALU.max).then_inc(s_h, 1)
                dve.wait_ge(s_h, n + 1)
                for i, (t, m) in enumerate(CH):
                    dve.wait_ge(s_hTp, NCH * n + i + 1)
                    v.tensor_copy(hT[:, t * P:(t + m) * P], bank[4 + i % 2][0:F, 0:m * P]).then_inc(s_hTc, 1)
                dve.wait_ge(s_hTc, NCH * (n + 1))

            def node_tables(l):
                a, f, q, w = ATT[l], TABF[l], QF[l], WAYS[l]
                tb = tab[:, 0:NT * f].rearrange("p (t c) -> p t c", c=f)
                qt = wide[:, 0:NT * q].rearrange("p (t c) -> p t c", c=q)
                if l == 0:
                    c.add(v.tensor_copy(tb[:, :, 0:F], h[:, :, :]))
                for i, (t, m) in enumerate(CH):
                    dve.wait_ge(s_tp, NCH * a + i + 1)
                    ps = bank[6 + i % 2][:, 0:m * w].rearrange("p (t c) -> p t c", c=w)
                    if l == 0:
                        v.tensor_copy(tb[:, t:t + m, F:F + H], ps[:, :, H:2 * H]).then_inc(s_tc, 1)
                        v.tensor_scalar(qt[:, t:t + m, :], ps[:, :, 0:H], fcb[:, 0:1], None, ALU.add).then_inc(s_tc, 1)
                    elif l == 1:
                        v.tensor_copy(tb[:, t:t + m, :], ps[:, :, 0:2 * F]).then_inc(s_tc, 1)
                        v.tensor_copy(qt[:, t:t + m, :], ps[:, :, 2 * F:3 * F]).then_inc(s_tc, 1)
                    else:
                        v.tensor_copy(qt[:, t:t + m, 0:F], ps[:, :, 0:F]).then_inc(s_tc, 1)
                        v.tensor_copy(qt[:, t:t + m, F:], ps[:, :, F:]).then_inc(s_tc, 1)
                dve.wait_ge(s_tc, 2 * NCH * (a + 1))
                c.sync()
                v.memset(runmax[:, P:P + 1], -BIG).then_inc(s_tabr, 1)

            def stage(l, g, b):
                src = idx_a if l in ATT else idx_c
                v.tensor_copy(idx_st[b][:, :], src[:, bass.ds(g, 1), :].rearrange("p a c -> p (a c)")).then_inc(s_stage, 1)

            def place(g, u):
                v.tensor_scalar(spread_q[u][:, :], loc[:, bass.ds(g * P, P)], part_f[:, 0:1], None, ALU.is_equal).then_inc(s_E, 1)

            def attention(l):
                a, f, q, pf = ATT[l], TABF[l], QF[l], PF[l]
                dve.wait_ge(s_tabr, l + 1)
                if l == 5:
                    dve.wait_ge(s_samer, 80)
                c.add(v.memset(loc[:, NB:], 0))
                c.add(v.memset(numS[1][:, P - 1:P], 0.0))
                c(v.memset(denS[1][:, P - 1:P], 0.0))
                if l:
                    dve.wait_ge(s_stage, l * (G + RING))
                for b in range(RING):
                    stage(l, b, b)
                for u in range(2):
                    place(u, u)

                def slots(ap):
                    return ap.rearrange("p a r -> p (a r)").unsqueeze(2).to_broadcast([P, R, H])

                def products(g, u, b, o):
                    n = a * G + g + 1
                    X = rows[b][:, 0:R * f].rearrange("p (r c) -> p r c", c=f)
                    Q = bank[4 + u][:, 0:q]
                    if not (isinstance(g, int) and g == 0 and a == 0):
                        dve.wait_ge(s_part, n - 1)
                    dve.wait_ge(s_q, n)
                    dve.wait_ge(s_rows[b], (o + (l * ring(b) + 1)) * (R * 16))
                    if l == 0:
                        v.tensor_tensor(dif[:, :, :], X[:, :, F:F + H], Q.unsqueeze(1).to_broadcast([P, R, H]), ALU.add).then_inc(s_prod, 1)
                    elif l == 1:
                        v.tensor_tensor(prod[:, 0:R * F].rearrange("p (r c) -> p r c", c=F), X[:, :, 0:F],
                                        Q.unsqueeze(1).to_broadcast([P, R, F]), ALU.mult).then_inc(s_prod, 1)
                    else:
                        v.tensor_tensor(prod[:, :].rearrange("p (r h c) -> p r h c", h=H, c=F), X.unsqueeze(2).to_broadcast([P, R, H, F]),
                                        Q.rearrange("p (h c) -> p h c", h=H).unsqueeze(1).to_broadcast([P, R, H, F]), ALU.mult).then_inc(s_prod, 1)

                def scores(g):
                    dve.wait_ge(s_prod, a * G + g + 1)
                    if l == 0:
                        v.scalar_tensor_tensor(sc_[:, :, :], dif[:, :, :], 0.2, dif[:, :, :], ALU.mult, ALU.max).then_inc(s_raw, 1)
                    else:
                        m = R * F if l == 1 else R * H * F
                        v.tensor_reduce(sc_[:, :, :].rearrange("p r h -> p (r h)"),
                                        prod[:, 0:m].rearrange("p (a c) -> p a c", a=R * H), AX.X, ALU.add).then_inc(s_raw, 1)

                def penalty(g):
                    dve.wait_ge(s_raw, a * G + g + 1)
                    v.tensor_tensor(sc_[:, :, :], sc_[:, :, :], slots(pen[:, bass.ds(g, 1), :]), ALU.add).then_inc(s_scored, 1)

                def block_max(g):
                    n = a * G + g + 1
                    dve.wait_ge(s_scored, n)
                    if not (isinstance(g, int) and g == 0 and a == 0):
                        dve.wait_ge(s_partT, n - 1)
                    v.tensor_reduce(stat[:, H:2 * H], sc_[:, :, :].rearrange("p r h -> p h r"), AX.X, ALU.max).then_inc(s_bmax, 1)

                def less_max(g):
                    dve.wait_ge(s_bmax, a * G + g + 1)
                    v.tensor_tensor(dif[:, :, :], sc_[:, :, :], stat[:, H:2 * H].unsqueeze(1).to_broadcast([P, R, H]), ALU.subtract).then_inc(s_dif, 1)

                def filled(g):
                    dve.wait_ge(s_exp, a * G + g + 1)
                    v.tensor_tensor(ex[:, :, :], ex[:, :, :], slots(valid[:, bass.ds(g, 1), :]), ALU.mult).then_inc(s_ev, 1)

                def block_den(g):
                    dve.wait_ge(s_ev, a * G + g + 1)
                    v.tensor_reduce(stat[:, 0:H], ex[:, :, :].rearrange("p r h -> p h r"), AX.X, ALU.add).then_inc(s_den, 1)

                def weighted(g, b):
                    X = rows[b][:, 0:R * f].rearrange("p (r c) -> p r c", c=f)
                    if l == 1:
                        v.tensor_tensor(prod[:, 0:R * F].rearrange("p (r h c) -> p r h c", h=H, c=F // H),
                                        X[:, :, F:2 * F].rearrange("p r (h c) -> p r h c", h=H),
                                        ex[:, :, :].unsqueeze(3).to_broadcast([P, R, H, F // H]), ALU.mult).then_inc(s_wv, 1)
                    else:
                        v.tensor_tensor(prod[:, :].rearrange("p (r h c) -> p r h c", h=H, c=F), X[:, :, 0:F].unsqueeze(2).to_broadcast([P, R, H, F]),
                                        ex[:, :, :].unsqueeze(3).to_broadcast([P, R, H, F]), ALU.mult).then_inc(s_wv, 1)

                def block_sums(g, b):
                    dve.wait_ge(s_wv, a * G + g + 1)
                    v.tensor_reduce(part[:, 0:pf], prod[:, 0:R * pf].rearrange("p (r c) -> p c r", c=pf), AX.X, ALU.add).then_inc(s_part, 1)
                    stage(l, g + RING, b)

                def carry_in(g):
                    v.tensor_scalar(penr[:, :], same[0:H, bass.ds(g * P, P)], -1.0, BIG, ALU.add, ALU.mult).then_inc(s_penr, 1)
                    v.tensor_copy(runmax[:, 0:1], runmax[:, P:P + 1]).then_inc(s_carry, 1)

                def carry_max(g):
                    n = a * G + g + 1
                    dve.wait_ge(s_penr, n)
                    dve.wait_ge(s_carry, n)
                    dve.wait_ge(s_partT, n)
                    v.tensor_tensor_scan(runmax[:, 1:P + 1], penr[:, :], bank[1][0:H, P:2 * P], runmax[:, 0:1], ALU.add, ALU.max).then_inc(s_runmax, 1)

                def carry_diff(g):
                    dve.wait_ge(s_runmax, a * G + g + 1)
                    v.tensor_tensor(dd[:, 0, :], bank[1][0:H, P:2 * P], runmax[:, 1:P + 1], ALU.subtract).then_inc(s_dd, 1)
                    v.tensor_tensor(dd[:, 1, :], runmax[:, 0:P], runmax[:, 1:P + 1], ALU.subtract).then_inc(s_dd, 1)

                def carry_clip(g):
                    n = a * G + g + 1
                    dve.wait_ge(s_dd, 3 * n - 1)
                    if not (isinstance(g, int) and g == 0 and a == 0):
                        dve.wait_ge(s_numS, n - 1)
                        dve.wait_ge(s_denS, n - 1)
                    v.tensor_scalar(dd[:, 1, :], dd[:, 1, :], 0.0, None, ALU.min).then_inc(s_dd, 1)

                def carry_same(g):
                    dve.wait_ge(s_ww, a * G + g + 1)
                    v.tensor_tensor(ww[:, 1, :], ww[:, 1, :], same[0:H, bass.ds(g * P, P)], ALU.mult).then_inc(s_w0, 1)

                def carry_den1(g):
                    dve.wait_ge(s_w0, a * G + g + 1)
                    v.tensor_tensor(den1[:, :], bank[1][0:H, 0:P], ww[:, 0, :], ALU.mult).then_inc(s_den1, 1)

                def carry_den(g, u):
                    dve.wait_ge(s_den1, a * G + g + 1)
                    v.tensor_tensor_scan(denS[u][:, :], ww[:, 1, :], den1[:, :], denS[1 - u][:, P - 1:P], ALU.mult, ALU.add).then_inc(s_denS, 1)

                def carry_num1(g):
                    dve.wait_ge(s_wE, a * G + g + 1)
                    v.tensor_tensor(num1[0:pf, :], bank[0][0:pf, 0:P], wE[0:pf, 0:P], ALU.mult).then_inc(s_num1, 1)

                def carry_num(g, u):
                    dve.wait_ge(s_num1, a * G + g + 1)
                    v.tensor_tensor_scan(numS[u][0:pf, :], wE[0:pf, P:2 * P], num1[0:pf, :], numS[1 - u][0:pf, P - 1:P], ALU.mult, ALU.add).then_inc(s_numS, 1)

                def body(g, u, b, o):
                    carry_in(g - 1)
                    products(g, u, b, o)
                    scores(g)
                    carry_max(g - 1)
                    penalty(g)
                    carry_diff(g - 1)
                    block_max(g)
                    carry_clip(g - 1)
                    less_max(g)
                    place(g + 2, u)
                    filled(g)
                    carry_same(g - 1)
                    block_den(g)
                    carry_den1(g - 1)
                    weighted(g, b)
                    carry_den(g - 1, 1 - u)
                    block_sums(g, b)
                    carry_num1(g - 1)
                    carry_num(g - 1, 1 - u)

                products(0, 0, 0, 0)
                scores(0)
                penalty(0)
                block_max(0)
                less_max(0)
                place(2, 0)
                filled(0)
                block_den(0)
                weighted(0, 0)
                block_sums(0, 0)
                quads(dve, body, 1)
                carry_in(G - 1)
                carry_max(G - 1)
                carry_diff(G - 1)
                carry_clip(G - 1)
                carry_same(G - 1)
                carry_den1(G - 1)
                carry_den(G - 1, 0)
                carry_num1(G - 1)
                carry_num(G - 1, 0)

            def attention_nodes(l):
                a, pf = ATT[l], PF[l]
                w = pf + H
                dve.wait_ge(s_comb, 16 * NT * (l + 1))
                cm = comb[:, 0:NT * w].rearrange("p (t c) -> p t c", c=w)
                d = cm[:, :, pf:w]
                c(v.tensor_scalar(d, d, 1e-16, None, ALU.max))
                c(v.reciprocal(d, d))
                for hh in range(H):
                    m = pf // H
                    v.tensor_tensor(cm[:, :, hh * m:(hh + 1) * m], cm[:, :, hh * m:(hh + 1) * m],
                                    cm[:, :, pf + hh:pf + hh + 1].to_broadcast([P, NT, m]), ALU.mult).then_inc(s_norm, 1)
                dve.wait_ge(s_norm, 4 * (a + 1))
                dve.wait_ge(s_fin, a + 1)
                for i, (t, m) in enumerate(((0, 16), (16, NT - 16))):
                    ps = bank[6 + i][:, 0:m * F].rearrange("p (t c) -> p t c", c=F)
                    c(v.tensor_tensor(x[:, t:t + m, :], x[:, t:t + m, :], ps, ALU.add))
                if l == 0:
                    v.tensor_tensor(x[:, :, :], x[:, :, :], bias0[:, None, :].to_broadcast([P, NT, F]), ALU.add).then_inc(s_done, 1)
                else:
                    v.tensor_tensor(x[:, :, :], x[:, :, :], h[:, :, :], ALU.add).then_inc(s_done, 1)
                dve.wait_ge(s_done, done_of[l])

            def convolution(l):
                q = CONV[l]
                dve.wait_ge(s_stage, l * (G + RING))
                c(v.memset(aggS[1][:, P - 1:P], 0.0))
                for b in range(RING):
                    stage(l, b, b)

                def body(g, u, b, o):
                    n = q * G + g + 1
                    X = rows[b][:, 0:R * F].rearrange("p (j c) -> p j c", c=F)
                    hat = hats[:, bass.ds(g * R, R), :, :]
                    if not (isinstance(g, int) and g < 2 and q == 0):
                        dve.wait_ge(s_tb, n - 2)
                    v.tensor_tensor(b12[:, :, :].rearrange("p j (b a) -> p j b a", b=4),
                                    hat[:, :, 2, :].unsqueeze(3).to_broadcast([P, R, 4, 4]),
                                    hat[:, :, 1, :].unsqueeze(2).to_broadcast([P, R, 4, 4]), ALU.mult).then_inc(s_b12, 1)
                    dve.wait_ge(s_b12, n)
                    v.tensor_tensor(m12[u].rearrange("p j (b k) -> p j b k", k=16), b12[:, :, :].unsqueeze(2).to_broadcast([P, R, P // R, 16]),
                                    mask[:, :, :].unsqueeze(1).to_broadcast([P, R, P // R, 16]), ALU.mult).then_inc(s_m12, 1)
                    dve.wait_ge(s_rows[b], (o + (l * ring(b) + 1)) * (R * 16))
                    v.tensor_tensor(xb[u], X.unsqueeze(2).to_broadcast([P, R, 4, F]),
                                    hat[:, :, 0, :].unsqueeze(3).to_broadcast([P, R, 4, F]), ALU.mult).then_inc(s_xb, 1)
                    dve.wait_ge(s_xb, n)
                    stage(l, g + RING, b)
                    if not (isinstance(g, int) and g < 2):
                        scan(g - 2, u)

                def scan(g, u):
                    n = q * G + g + 1
                    dve.wait_ge(s_msg, n)
                    if isinstance(g, int) and g == 0:
                        dve.wait_ge(s_m12, n)
                    else:
                        dve.wait_ge(s_agg, n - 1)
                    v.tensor_tensor_scan(aggS[u][:, :], same[:, bass.ds(g * P, P)], bank[2][0:F, 0:P],
                                         aggS[1 - u][:, P - 1:P], ALU.mult, ALU.add).then_inc(s_agg, 1)
                quads(dve, body)
                scan(G - 2, (G - 2) % 2)
                scan(G - 1, (G - 1) % 2)

            def conv_nodes(l):
                q = CONV[l]
                y = wide[0:F, 0:NT * P]
                dve.wait_ge(s_comb, 16 * NT * (l + 1))
                cm = comb[:, 0:NT * F].rearrange("p (t c) -> p t c", c=F)
                v.tensor_tensor(cm, cm, rcnt[:, :].unsqueeze(2).to_broadcast([P, NT, F]), ALU.mult).then_inc(s_yn, 1)
                dve.wait_ge(s_yc, NCH * (q + 1))
                if q < 2:
                    c(v.scalar_tensor_tensor(y, y, 0.01, y, ALU.mult, ALU.max))
                c(v.tensor_tensor(y, y, hT[:, :], ALU.add))
                mu, var, scale = bn[:, 0:1], bn[:, 1:2], bn[:, 2:3]
                c(v.tensor_reduce(mu, y[:, 0:NODES], AX.X, ALU.add))
                c(v.tensor_scalar(mu, mu, 1.0 / NODES, None, ALU.mult))
                c(v.tensor_scalar(y, y, mu, None, ALU.subtract))
                c(v.tensor_tensor(ytmp[:, :], y, y, ALU.mult))
                c(v.tensor_reduce(var, ytmp[:, 0:NODES], AX.X, ALU.add))
                v.tensor_scalar(var, var, 1.0 / NODES, None, ALU.mult).then_inc(s_bnv, 1)
                dve.wait_ge(s_bns, q + 1)
                c(v.reciprocal(scale, var))
                c(v.tensor_tensor(scale, scale, cb[:, 3 * q + 1:3 * q + 2], ALU.mult))
                v.tensor_scalar(hT[:, :], y, scale, cb[:, 3 * q + 2:3 * q + 3], ALU.mult, ALU.add).then_inc(s_xT, 1)
                for i, (t, m) in enumerate(((0, 16), (16, NT - 16))):
                    dve.wait_ge(s_xTp, 2 * q + i + 1)
                    c(v.tensor_copy(h[:, t:t + m, :], bank[6 + i][:, 0:m * F].rearrange("p (t c) -> p t c", c=F)))
                if q < 2:
                    v.memset(bn[:, 4:5], 0.0).then_inc(s_tabr, 1)
                else:
                    v.tensor_tensor(x[:, :, :], x[:, :, :], h[:, :, :], ALU.add).then_inc(s_done, 1)
                    dve.wait_ge(s_done, done_of[l])

            for l in range(LAYERS):
                if l < 2:
                    prepare(l)
                if l in (0, 1, 2, 5):
                    layernorm((0, 1, 2, 5).index(l))
                if l == 2:
                    v.memset(bn[:, 4:5], 0.0).then_inc(s_tabr, 1)
                if l in ATT:
                    node_tables(l)
                    attention(l)
                    attention_nodes(l)
                else:
                    convolution(l)
                    conv_nodes(l)

        @block.tensor
        def _(pe):
            mm = nc.tensor.matmul
            pe.wait_ge(s_fill, 4)
            for k in range(2):
                mm(hist[k], zero[:, 0:P], zero[:, 0:NT], start=True, stop=False)

            def count(g, u):
                pe.wait_ge(s_oh, 4 * g + 4)
                for k in range(2):
                    for j in range(EB):
                        last = mm(hist[k], ohlo[k][u][:, j, :], ohhi[k][u][:, j, :], start=False, stop=False)
                last.then_inc(s_hist, 1)
            batches(pe, count)
            for k in range(2):
                mm(hist[k], zero[:, 0:P], zero[:, 0:NT], start=False, stop=True).then_inc(s_histall, 1)
            for k in range(2):
                pe.wait_ge(s_nblk, k + 1)
                if k:
                    pe.wait_ge(s_start, k)
                mm(bank[3][:, 0:NT], above[:, :], nblk[k][:, :], start=True, stop=True)
                mm(bank[3][:, NT:2 * NT], ones[:, :], nblk[k][:, :], start=True, stop=True).then_inc(s_prefix, 1)
            pe.wait_ge(s_start, 2)
            for k in range(2):
                mm(hist[k], ident[:, :], start[k][:, :], start=True, stop=True).then_inc(s_acc[k], 1)

            def rank(g, u):
                first = isinstance(g, int) and g == 0
                pe.wait_ge(s_oh2, 10 * g + 10)
                for k in range(2):
                    if k or not first:
                        pe.wait_ge(s_ohT, 2 * g + k)
                    for j in range(EB):
                        last = nc.tensor.transpose(trb[:, j * P:j * P + EP], ohlo[k][u][:, j, :], identb[0:EP, 0:EP])
                    last.then_inc(s_T, 1)
                for j in range(EB):
                    for k in range(2):
                        pe.wait_ge(s_cp[k], EB * g + j + 1)
                        mm(hist[k], ohlo[k][u][:, j, :], ohhi[k][u][:, j, :], start=False, stop=True,
                           skip_group_check=True).then_inc(s_acc[k], 1)
                if not first:
                    pe.wait_ge(s_pick, 2 * g)
                for k in range(2):
                    pe.wait_ge(s_ohT, 2 * g + k + 1)
                    for j in range(EB):
                        last = mm(look[k][:, j, :], ohloT[k][:, j, :], base_sb[k][:, j, :], start=True, stop=True)
                    last.then_inc(s_look, 1)
                if not first:
                    pe.wait_ge(s_rank, 16 * g)
                for k in range(2):
                    for j in range(EB):
                        lo = lo_st[u][:, k, j:j + 1].to_broadcast([EP, EP])
                        hi = hi_st[u][:, k, j:j + 1].to_broadcast([EP, EP])
                        mm(keyrow[k][j], lo, identb[0:EP, 0:EP], start=True, stop=False)
                        last = mm(keyrow[k][j], hi, identb[0:EP, 0:EP], start=False, stop=True)
                last.then_inc(s_key, 1)
            batches(pe, rank)

            tr = nc.tensor.transpose

            def bank_ours(i):
                mm(bank[i][0:F, 0:1], zero[:, 0:F], zero[:, 0:1], start=True, stop=True)

            pe.wait_ge(s_wT, 3)
            pe.wait_ge(s_rank, 16 * SORTS)
            for hh in range(H):
                one = slice(hh * F, (hh + 1) * F)
                mm(bank[3][0:F, hh * F:(hh + 1) * F], w3T[:, 0, one], w3T[:, 1, one], start=True, stop=True)
                last = mm(bank[3][0:F, P + hh * F:P + (hh + 1) * F], w3T[:, 2, one], wout[:, :], start=True, stop=True)
            last.then_inc(s_wp, 1)

            def prepare(k):
                pe.wait_ge(s_prep, k + 1)
                if k == 0:
                    pe.wait_ge(s_vo, 1)
                mm(bank[3][0:G, 0:1], above[0:G, 0:G], starts_g[:, :], start=True, stop=True).then_inc(s_off, 1)
                if k:
                    pe.wait_ge(s_slots, 80)
                    for n, (j, fld) in enumerate((j, fld) for j in range(R) for fld in range(4)):
                        if n >= 2:
                            pe.wait_ge(s_slc, n - 1)
                        view = fill_all[0:G, j * 512:(j + 1) * 512].rearrange("g (s c) -> g s c", c=4)
                        tr(bank[4 + n % 2][:, 0:G], view[:, :, fld], ident[0:G, 0:G]).then_inc(s_slT, 1)

            def h_transposed(n):
                pe.wait_ge(s_h, n + 1)
                for i, (t, m) in enumerate(CH):
                    if i >= 2:
                        pe.wait_ge(s_hTc, NCH * n + i - 1)
                    for k in range(m):
                        last = tr(bank[4 + i % 2][0:F, k * P:(k + 1) * P], h[:, t + k, :], ident[:, :])
                    last.then_inc(s_hTp, 1)

            def node_tables(l):
                a, w = ATT[l], WAYS[l]
                wt = {0: wa, 1: wkvq, 5: wqk}[l]
                pe.wait_ge(s_hTc, NCH * ((0, 1, 2, 5).index(l) + 1))
                for i, (t, m) in enumerate(CH):
                    if i >= 2:
                        pe.wait_ge(s_tc, 2 * NCH * a + 2 * (i - 1))
                    for k in range(m):
                        last = mm(bank[6 + i % 2][:, k * w:(k + 1) * w], hT[:, (t + k) * P:(t + k + 1) * P], wt[:, :], start=True, stop=True)
                    last.then_inc(s_tp, 1)

            def attention(l):
                a, pf = ATT[l], PF[l]

                def query(g, u, o):
                    pe.wait_ge(s_win[u], 16 * (a * per(u) + o + 1))
                    pe.wait_ge(s_E, a * (G + 2) + g + 1)
                    mm(bank[4 + u][:, 0:QF[l]], spread_q[u][:, :], window[u][:, 0:QF[l]], start=True, stop=True).then_inc(s_q, 1)

                def inward(g):
                    n = a * G + g + 1
                    pe.wait_ge(s_den, n)
                    pe.wait_ge(s_part, n)
                    tr(bank[0][0:pf, 0:P], part[:, 0:pf], ident[:, :])
                    tr(bank[1][0:H, 0:P], stat[:, 0:H], ident[:, :])
                    tr(bank[1][0:H, P:2 * P], stat[:, H:2 * H], ident[:, :]).then_inc(s_partT, 1)

                def outward(g, u):
                    n = a * G + g + 1
                    pe.wait_ge(s_w0, n)
                    mm(bank[2][:, 0:2 * P], sel[:, 0 if pf == P else 1, :], ww[:, :, :].rearrange("p a b -> p (a b)"),
                       start=True, stop=True).then_inc(s_wx, 1)
                    pe.wait_ge(s_denS, n)
                    pe.wait_ge(s_numS, n)
                    if not (isinstance(g, int) and g == 0):
                        pe.wait_ge(s_outst, l * G + g)
                    if pf < P:
                        bank_ours(3)
                    tr(bank[3][:, 0:pf], numS[u][0:pf, :], ident[0:pf, 0:pf])
                    tr(bank[3][:, pf:pf + H], denS[u][:, :], ident[0:H, 0:H]).then_inc(s_back, 1)

                def body(g, u):
                    outward(g - 1, 1 - u)
                    inward(g)
                query(0, 0, 0)
                query(1, 1, 0)
                inward(0)
                query(2, 0, 1)
                body(1, 1)
                with pe.Fori(1, (G - 1) // 2) as i:
                    query(2 * i + 1, 1, i)
                    body(2 * i, 0)
                    query(2 * i + 2, 0, i + 1)
                    body(2 * i + 1, 1)
                body(G - 1, 0)
                outward(G - 1, 0)

            def attention_nodes(l):
                a, pf = ATT[l], PF[l]
                w = pf + H
                wt = {0: w0cat, 1: wo, 5: wvocat}[l]
                cm = comb[:, 0:NT * w].rearrange("p (t c) -> p t c", c=w)
                pe.wait_ge(s_norm, 4 * (a + 1))
                pe.wait_ge(s_vod, 64)

                def products(i):
                    t, m = CH[i]
                    pe.wait_ge(s_aTc, NCH * a + i + 1)
                    for k in range(m):
                        n = t + k
                        last = mm(bank[6 + n // 16][:, (n % 16) * F:(n % 16 + 1) * F], aT[i % 2][0:pf, k * P:(k + 1) * P], wt[:, :], start=True, stop=True)
                    return last
                for i, (t, m) in enumerate(CH):
                    for k in range(m):
                        last = tr(bank[4 + i % 2][0:pf, k * P:(k + 1) * P], cm[:, t + k, 0:pf], ident[:, :])
                    last.then_inc(s_aT, 1)
                    if i:
                        products(i - 1)
                products(NCH - 1).then_inc(s_fin, 1)

            def convolution(l):
                q = CONV[l]
                pe.wait_ge(s_cw, 16 * (q + 1))

                def outer(g, u):
                    n = q * G + g + 1
                    pe.wait_ge(s_m12, n)
                    pe.wait_ge(s_xb, n)
                    if not (isinstance(g, int) and g == 0):
                        pe.wait_ge(s_tsb, n - 1)
                    for j in range(R):
                        last = mm(bank[4 + j // 2][:, (j % 2) * 2 * P:(j % 2 + 1) * 2 * P], xb[u][:, j, :, :].rearrange("p k c -> p (k c)"),
                                  m12[u][:, j, :], start=True, stop=True)
                    last.then_inc(s_tb, 1)

                def weights(g, u):
                    n = q * G + g + 1
                    pe.wait_ge(s_tsb, n)
                    if not (isinstance(g, int) and g == 0):
                        pe.wait_ge(s_agg, n - 1)
                    for k in range(16):
                        last = mm(bank[2][0:F, 0:P], cw[:, k, :], tsb[u][:, k, :], start=(k == 0), stop=(k == 15))
                    last.then_inc(s_msg, 1)

                def back(g, u):
                    n = q * G + g + 1
                    pe.wait_ge(s_agg, n)
                    if not (isinstance(g, int) and g == 0):
                        pe.wait_ge(s_outst, l * G + g)
                    bank_ours(3)
                    tr(bank[3][:, 0:F], aggS[u][:, :], ident[0:F, 0:F]).then_inc(s_back, 1)

                def body(g, u, o):
                    outer(g, u)
                    if not (isinstance(g, int) and g == 0):
                        weights(g - 1, 1 - u)
                        if not (isinstance(g, int) and g == 1):
                            back(g - 2, u)
                body(0, 0, 0)
                body(1, 1, 0)
                body(2, 0, 0)
                with pe.Fori(1, (G - 1) // 2) as i:
                    body(2 * i + 1, 1, i)
                    body(2 * i + 2, 0, i + 1)
                back(G - 2, (G - 2) % 2)
                weights(G - 1, (G - 1) % 2)
                back(G - 1, (G - 1) % 2)

            def conv_nodes(l):
                q = CONV[l]
                cm = comb[:, 0:NT * F].rearrange("p (t c) -> p t c", c=F)
                pe.wait_ge(s_yn, q + 1)
                for i, (t, m) in enumerate(CH):
                    if i >= 2:
                        pe.wait_ge(s_yc, NCH * q + i - 1)
                    last = mm(bank[4 + i % 2][0:F, 0:m * P], cr[:, q, :], hT[:, t * P:(t + m) * P], start=True, stop=False)
                    for k in range(m):
                        last = mm(bank[4 + i % 2][0:F, k * P:(k + 1) * P], cm[:, t + k, :], ident[:, :], start=False, stop=(k == m - 1))
                    last.then_inc(s_y, 1)
                pe.wait_ge(s_xT, q + 1)
                for i, (t, m) in enumerate(((0, 16), (16, NT - 16))):
                    for k in range(m):
                        last = tr(bank[6 + i][:, k * F:(k + 1) * F], hT[:, (t + k) * P:(t + k + 1) * P], ident[0:F, 0:F])
                    last.then_inc(s_xTp, 1)
                if q < 2:
                    nc.tensor.nop().then_inc(s_cwuse, 1) if False else None

            for l in range(LAYERS):
                if l < 2:
                    prepare(l)
                if l in (0, 1, 2, 5):
                    h_transposed((0, 1, 2, 5).index(l))
                if l in ATT:
                    node_tables(l)
                    attention(l)
                    attention_nodes(l)
                else:
                    convolution(l)
                    conv_nodes(l)

        @block.scalar
        def _(act):
            def rank(g, u):
                first = isinstance(g, int) and g == 0
                if not first:
                    act.wait_ge(s_look, 2 * g)
                for k in range(2):
                    act.wait_ge(s_T, 2 * g + k + 1)
                    nc.scalar.activation(ohloT[k], trb[:, :].rearrange("p (j c) -> p j c", c=P)[:, :, 0:EP],
                                         ACT.Copy).then_inc(s_ohT, 1)
                for j in range(EB):
                    for k in range(2):
                        act.wait_ge(s_acc[k], EB * g + j + 1)
                        nc.scalar.activation(base_sb[k][:, j, :], hist[k], ACT.Copy).then_inc(s_cp[k], 1)
            batches(act, rank)
            cp = nc.scalar.activation

            def layernorm(n):
                act.wait_ge(s_var, n + 1)
                cp(lns[:, :], lns[:, :], ACT.Sqrt, bias=eps[:, 0:1]).then_inc(s_std, 1)

            def attention(l):
                a, pf = ATT[l], PF[l]

                def exps(g):
                    n = a * G + g + 1
                    act.wait_ge(s_dif, n)
                    cp(ex[:, :, :], dif[:, :, :], ACT.Exp).then_inc(s_exp, 1)

                def carries(g):
                    n = a * G + g + 1
                    act.wait_ge(s_dd, 3 * n)
                    cp(ww[:, :, :], dd[:, :, :], ACT.Exp).then_inc(s_ww, 1)

                def spread(g):
                    n = a * G + g + 1
                    act.wait_ge(s_wx, n)
                    cp(wE[0:pf, :], bank[2][0:pf, 0:2 * P], ACT.Copy).then_inc(s_wE, 1)

                def outs(g, u, o):
                    act.wait_ge(s_back, l * G + g + 1)
                    if not (isinstance(g, int) and g < 2):
                        act.wait_ge(s_outw[u], 16 * (per(u) * l + o))
                    elif l:
                        act.wait_ge(s_outw[u], 16 * per(u) * l)
                    cp(out_st[u][:, 0:pf + H], bank[3][:, 0:pf + H], ACT.Copy).then_inc(s_outst, 1)

                def body(g, u, o):
                    exps(g)
                    carries(g - 1)
                    outs(g - 2, u, o - 1)
                    spread(g - 1)
                exps(0)
                exps(1)
                carries(0)
                spread(0)
                body(2, 0, 1)
                body(3, 1, 1)
                with act.Fori(2, (G - 1) // 2) as i:
                    body(2 * i, 0, i)
                    body(2 * i + 1, 1, i)
                body(G - 1, 0, (G - 1) // 2)
                carries(G - 1)
                outs(G - 2, 1, (G - 2) // 2)
                spread(G - 1)
                outs(G - 1, 0, (G - 1) // 2)

            def attention_nodes(l):
                a, pf = ATT[l], PF[l]
                for i, (t, m) in enumerate(CH):
                    act.wait_ge(s_aT, NCH * a + i + 1)
                    cp(aT[i % 2][0:pf, 0:m * P], bank[4 + i % 2][0:pf, 0:m * P], ACT.Copy).then_inc(s_aTc, 1)

            def convolution(l):
                q = CONV[l]

                def body(g, u, o):
                    n = q * G + g + 1
                    act.wait_ge(s_tb, n)
                    if not (isinstance(g, int) and g < 2):
                        act.wait_ge(s_msg, n - 2)
                    view = tsb[u].rearrange("p k n -> p n k")
                    for b in range(4):
                        last = cp(view[:, 32 * b:32 * b + 32, :], bank[4 + b][:, :].rearrange("p (n k) -> p n k", k=16), ACT.Copy)
                    last.then_inc(s_tsb, 1)
                    if not (isinstance(g, int) and g < 2):
                        outs(g - 2, u, o - 1)

                def outs(g, u, o):
                    act.wait_ge(s_back, l * G + g + 1)
                    if isinstance(g, int) and g < 2:
                        act.wait_ge(s_outw[u], 16 * per(u) * l)
                    else:
                        act.wait_ge(s_outw[u], 16 * (per(u) * l + o))
                    cp(cout[u][:, :], bank[3][:, 0:F], ACT.Copy).then_inc(s_outst, 1)
                body(0, 0, 0)
                body(1, 1, 0)
                body(2, 0, 1)
                body(3, 1, 1)
                with act.Fori(2, (G - 1) // 2) as i:
                    body(2 * i, 0, i)
                    body(2 * i + 1, 1, i)
                body(G - 1, 0, (G - 1) // 2)
                outs(G - 2, 1, (G - 2) // 2)
                outs(G - 1, 0, (G - 1) // 2)

            def conv_nodes(l):
                q = CONV[l]
                for i, (t, m) in enumerate(CH):
                    act.wait_ge(s_y, NCH * q + i + 1)
                    cp(wide[0:F, t * P:(t + m) * P], bank[4 + i % 2][0:F, 0:m * P], ACT.Identity,
                       bias=cb[:, 3 * q:3 * q + 1]).then_inc(s_yc, 1)
                act.wait_ge(s_bnv, q + 1)
                cp(bn[:, 1:2], bn[:, 1:2], ACT.Sqrt, bias=eps[0:F, 0:1]).then_inc(s_bns, 1)

            for l in range(LAYERS):
                if l in (0, 1, 2, 5):
                    layernorm((0, 1, 2, 5).index(l))
                if l in ATT:
                    attention(l)
                    attention_nodes(l)
                else:
                    convolution(l)
                    conv_nodes(l)


LAYERS = 6
_NAMES = ["x", "src", "dst", "edge_attr_3"]
_SCRATCH = {
    "slots0": (NB * R, 1), "slots1": (NB * R, 4), "flags0": (NB, 1), "flags1": (NB, 1),
    "tab0": (DUMMY + 1, 36), "tab1": (DUMMY + 1, 64), "tab2": (DUMMY + 1, F), "tab3": (DUMMY + 1, F),
    "tab4": (DUMMY + 1, F), "tab5": (DUMMY + 1, F),
    "q0": ((NT + 1) * P, H), "q1": ((NT + 1) * P, F), "q5": ((NT + 1) * P, P),
    "blk0": (NB, P + H), "blk1": (NB, F + H), "blk2": (NB, F), "blk3": (NB, F), "blk4": (NB, F), "blk5": (NB, P + H),
}


def kernel(**inputs):
    import numpy as np
    import concourse.bacc as bacc
    from concourse.bass_utils import run_bass_kernel_spmd as run

    nc = bacc.Bacc("TRN2", target_bir_lowering=False, num_devices=1)
    arrays, A = {}, {}
    for n, v in inputs.items():
        a = np.ascontiguousarray(v)
        arrays["in_" + n] = a
        A[n] = nc.dram_tensor("in_" + n, a.shape, mybir.dt.from_np(a.dtype), kind="ExternalInput").ap()
    D = {n: nc.dram_tensor("d_" + n, s, FP, kind="Internal").ap() for n, s in _SCRATCH.items()}
    for k in range(2):
        D[f"same{k}"] = nc.dram_tensor(f"d_same{k}", (NB,), U8, kind="Internal").ap()
        D[f"loc{k}"] = nc.dram_tensor(f"d_loc{k}", (NB,), U8, kind="Internal").ap()
        D[f"first{k}"] = nc.dram_tensor(f"d_first{k}", (G,), I32, kind="Internal").ap()
    o = nc.dram_tensor("out", (NODES, F), FP, kind="ExternalOutput").ap()
    build(nc, A, o, D)
    return run(nc, [arrays], core_ids=[0]).results[0]["out"]
```

```python
import concourse.bass as bass
from concourse import mybir
from contextlib import ExitStack

FP = mybir.dt.float32
BF = mybir.dt.bfloat16
I32 = mybir.dt.int32
U8 = mybir.dt.uint8
ALU = mybir.AluOpType
ACT = mybir.ActivationFunctionType
AX = mybir.AxisListType

P = 128
NODES = 3125
EDGES = 100000
F = 32
H = 4
NT = (NODES + P - 1) // P
LASTN = NODES - (NT - 1) * P
EP = P
EB = 8
ET = -(-EDGES // (EP * 2 * EB)) * 2 * EB
SORTS = ET // EB
LASTE = EDGES - (EP - 1) * ET
R = 8
MAXBLOCKS = (EDGES + R * NODES) // R
G = (MAXBLOCKS + P - 1) // P
NB = G * P
RING = 4
PADKEY = NT * P - 1
SLOTS = NB * R + P * R
assert MAXBLOCKS + PADKEY - NODES + -(-(EP * ET - EDGES) // R) <= NB
DUMMY = NT * P
BIG = 1.0e30
EPS = 1e-5
LAYERS = 6
INV_D8 = 8 ** -0.5
INV_F = F ** -0.5


class Chain:

    def __init__(self, eng, sem):
        self.eng, self.sem, self.n = eng, sem, 0

    def __call__(self, ins):
        ins.then_inc(self.sem, 1)
        self.n += 1
        self.eng.wait_ge(self.sem, self.n)

    def add(self, ins):
        ins.then_inc(self.sem, 1)
        self.n += 1

    def sync(self):
        self.eng.wait_ge(self.sem, self.n)


def build(nc, A, out, D):
    ctx = ExitStack()
    with ctx:
        def sb(name, shape, dt=FP):
            return ctx.enter_context(nc.sbuf_tensor(name, shape, dt))

        def sem(name):
            return ctx.enter_context(nc.semaphore(name))

        bank = [ctx.enter_context(nc.psum_tensor(f"bank{i}", [P, 512], FP)) for i in range(8)]

        ident = sb("ident", [P, P])
        identb = sb("identb", [P, P], BF)
        iota_i = sb("iota_i", [P, P], I32)
        iota_b = sb("iota_b", [P, P], BF)
        below = sb("below", [P, P])
        above = sb("above", [P, P])
        ones = sb("ones", [P, P])

        work = sb("work", [P, 11808])
        pos_ = [0]

        def carve(n, dt=FP, parts=P):
            k = n if dt in (FP, I32) else (n + 1) // 2
            a = work[0:parts, pos_[0]:pos_[0] + k]
            pos_[0] += k
            return a if dt == FP else a.bitcast(dt)

        key_i = [carve(ET, I32, EP) for _ in range(2)]
        key_f = [carve(ET, FP, EP) for _ in range(2)]
        lo_b = [carve(ET, BF, EP) for _ in range(2)]
        hi_b = [carve(ET, BF, EP) for _ in range(2)]
        payload = carve(ET * 4, FP, EP).rearrange("p (t c) -> p t c", c=4)
        tmp_i = carve(ET, I32, EP)
        attr = carve(ET * 3, FP, EP)
        conv = sb("conv", [P, 7168])
        cpos = [0]

        def carve2(n, dt=FP, parts=P):
            k = n if dt in (FP, I32) else (n + 1) // 2
            a = conv[0:parts, cpos[0]:cpos[0] + k]
            cpos[0] += k
            return a if dt == FP else a.bitcast(dt)

        ohlo = [[carve2(EB * P, BF, EP).rearrange("p (j c) -> p j c", c=P) for _ in range(2)] for _ in range(2)]
        ohhi = [[carve2(EB * NT, BF, EP).rearrange("p (j c) -> p j c", c=NT) for _ in range(2)] for _ in range(2)]
        ohloT = [carve2(EB * EP).rearrange("p (j c) -> p j c", c=EP) for _ in range(2)]
        base_sb = [carve2(EB * NT).rearrange("p (j c) -> p j c", c=NT) for _ in range(2)]
        junk = carve2(EB * EP, BF, EP).rearrange("p (j c) -> p j c", c=EP)
        keys_st = [sb(f"keys_st{u}", [EP, EB]) for u in range(2)]
        lo_st = [sb(f"lo_st{u}", [EP, EB], BF) for u in range(2)]
        hi_st = [sb(f"hi_st{u}", [EP, EB], BF) for u in range(2)]
        rank_in = sb("rank_in", [EP, EB])
        picked = carve2(EB * NT, FP, EP).rearrange("p (j c) -> p j c", c=NT)
        baseline = sb("baseline", [EP, EB])
        pos_st = [sb(f"pos_st{u}", [EP, EB], I32) for u in range(2)]
        pay_st = [sb(f"pay_st{u}", [EP, EB, 4]) for u in range(2)]
        srt_st = [sb(f"srt_st{u}", [EP, EB]) for u in range(2)]
        deg = [sb(f"deg{k}", [P, NT]) for k in range(2)]
        nblk = [sb(f"nblk{k}", [P, NT]) for k in range(2)]
        nblk_i = sb("nblk_i", [P, NT], I32)
        start = [sb(f"start{k}", [P, NT]) for k in range(2)]
        start_i = [sb(f"start_i{k}", [P, NT], I32) for k in range(2)]
        last_i = [sb(f"last_i{k}", [P, NT], I32) for k in range(2)]
        tot = sb("tot", [P, NT])
        zero = sb("zero", [P, 512])
        fill = sb("fill", [P, 1024, 4])

        s_load = sem("s_load"); s_keyin = [sem(f"s_keyin{k}") for k in range(2)]; s_const = sem("s_const"); s_pool = sem("s_pool")
        s_dve = sem("s_dve"); s_gate = sem("s_gate")
        s_fill = sem("s_fill"); s_filled = sem("s_filled");
        s_oh = sem("s_oh"); s_pad = sem("s_pad"); s_hist = sem("s_hist"); s_histall = sem("s_histall")
        s_nblk = sem("s_nblk"); s_prefix = sem("s_prefix"); s_start = sem("s_start")
        s_flag = sem("s_flag")
        s_oh2 = sem("s_oh2"); s_T = sem("s_T"); s_ohT = sem("s_ohT"); s_key = sem("s_key")
        s_cp = [sem(f"s_cp{k}") for k in range(2)]; s_acc = [sem(f"s_acc{k}") for k in range(2)]
        s_look = sem("s_look"); s_rank = sem("s_rank"); s_pick = sem("s_pick"); s_bl = sem("s_bl"); s_pay = sem("s_pay")
        s_pos = sem("s_pos"); s_sc = [sem(f"s_sc{u}") for u in range(2)]

        hist = [bank[0][:, 0:NT], bank[1][:, 0:NT]]
        look = bank[2][0:EP, 0:EB * NT].rearrange("p (j c) -> p j c", c=NT)
        keyrow = [[bank[3 + 2 * u + j // 4][0:EP, (j % 4) * P:(j % 4) * P + EP] for j in range(EB)] for u in range(2)]
        trb = bank[7][:, :].bitcast(BF)

        x = sb("x", [P, NT, F])
        h = sb("h", [P, NT, F])
        hT = sb("hT", [F, NT * P])
        wide = sb("wide", [P, NT * P])
        comb = sb("comb", [P, G * 32])
        fill0 = comb[:, 0:1024]
        lnm = sb("lnm", [P, NT])
        lns = sb("lns", [P, NT])
        rcnt = sb("rcnt", [P, NT])
        eps = sb("eps", [P, 1])
        less2 = sb("less2", [P, 1])
        idx_a = sb("idx_a", [P, G + RING, R], I32)
        idx_c = sb("idx_c", [P, G + RING, R], I32)
        valid = sb("valid", [P, G, R])
        pen = sb("pen", [P, G, R])
        same = sb("same", [F, NB], U8)
        idx_st = [sb(f"idx_st{b}", [P, R], I32) for b in range(RING)]
        rows = [sb(f"rows{b}", [P, R * 64]) for b in range(RING)]
        window = [sb(f"window{u}", [P, P]) for u in range(2)]
        spread_q = [sb(f"spread_q{u}", [P, P]) for u in range(2)]
        loc_g = sb("loc_g", [G, P], U8)
        first_i = sb("first_i", [G, 1], I32)
        part_f = sb("part_f", [P, 1])
        flg = sb("flg", [G, P])
        cum = sb("cum", [G, P])
        starts_g = sb("starts_g", [G, 1])
        same_g = sb("same_g", [G, P], U8)
        fill_all = fill[:, :, :].rearrange("p c a -> p (c a)")
        loc = fill_all.bitcast(U8)[:, 0:(G + 2) * P]
        w0 = sb("w0", [F, H, F]); w0cat = sb("w0cat", [P, F]); fcw = sb("fcw", [F, 2, F]); fcb = sb("fcb", [P, 1])
        bias0 = sb("bias0", [P, F]); wa = sb("wa", [F, 2 * H]); wtmp = sb("wtmp", [F, H, F])
        wkvq = sb("wkvq", [F, 3 * F]); wo = sb("wo", [F, F])
        w3 = sb("w3", [F, 3, H * F]); w3T = sb("w3T", [F, 3, H * F]); wout = sb("wout", [F, F])
        wqk = sb("wqk", [F, H * F]); wvo = sb("wvo", [F, H * F]); wvocat = sb("wvocat", [P, F])
        cw = sb("cw", [P, 16, F]); cr = sb("cr", [F, 3, F]); cb = sb("cb", [F, 9])
        sel = sb("sel", [H, 2, P]); sel_i = sb("sel_i", [H, 2, P], I32)
        mask = sb("mask", [P, P // R, 16]); mask_i = comb[:, 1024:1024 + 2 * P].bitcast(I32).rearrange("p (b k) -> p b k", b=P // R)
        prt_i = sb("prt_i", [P, 1], I32); prt_f = sb("prt_f", [P, 1])
        cpos[0] = 0
        prod = carve2(1024)
        wE = carve2(256)
        out_st = [carve2(132) for _ in range(2)]
        aT = [carve2(512) for _ in range(2)]
        numS = [carve2(P) for _ in range(2)]
        num1 = carve2(P)
        tab = carve2(NT * 64)
        part = carve2(P)
        sc_ = sb("sc_", [P, R, H]); dif = sb("dif", [P, R, H]); ex = sb("ex", [P, R, H])
        stat = sb("stat", [P, 2 * H])
        runmax = sb("runmax", [H, P + 1]); penr = sb("penr", [H, P]); dd = sb("dd", [H, 2, P]); ww = sb("ww", [H, 2, P])
        den1 = sb("den1", [H, P]); denS = [sb(f"denS{u}", [H, P]) for u in range(2)]
        cpos[0] = 0
        tsb = [carve2(16 * P).rearrange("p (k b) -> p k b", b=P) for _ in range(2)]
        xb = [carve2(R * P).rearrange("p (j k c) -> p j k c", j=R, c=F) for _ in range(2)]
        m12 = [fill_all[:, u * 2048:(u + 1) * 2048].rearrange("p (j c) -> p j c", j=R) for u in range(2)]
        b12 = sb("b12", [P, R, 16])
        aggS = [sb(f"aggS{u}", [F, P]) for u in range(2)]
        cout = [sb(f"cout{u}", [P, F]) for u in range(2)]
        hats = work[:, 0:G * R * 12].rearrange("p (s d k) -> p s d k", d=3, k=4)
        attr_c = wide[:, 0:3 * G * R].rearrange("p (d g j) -> p d g j", d=3, j=R)
        ytmp = comb[0:F, 0:NT * P]
        bn = sb("bn", [F, 8])
        NW = 26
        s_yn = sem("s_yn")
        done_of = {0: 1, 1: 2, 4: 3, 5: 4}
        s_xpad = sem("s_xpad"); s_xl = sem("s_xl")

        s_w = sem("s_w"); s_prep = sem("s_prep"); s_off = sem("s_off"); s_nid = sem("s_nid")
        s_win = [sem(f"s_win{u}") for u in range(2)]; s_E = sem("s_E"); s_q = sem("s_q"); s_same = sem("s_same"); s_samew = sem("s_samew"); s_samer = sem("s_samer"); s_slots = sem("s_slots"); s_fslots = sem("s_fslots"); s_clip = sem("s_clip"); s_hats = sem("s_hats")
        s_wT = sem("s_wT"); s_wp = sem("s_wp"); s_vo = sem("s_vo"); s_vod = sem("s_vod")
        s_slT = sem("s_slT"); s_slc = sem("s_slc")
        s_var = sem("s_var"); s_std = sem("s_std"); s_h = sem("s_h"); s_hTp = sem("s_hTp"); s_hTc = sem("s_hTc")
        s_tp = sem("s_tp"); s_tc = sem("s_tc"); s_tabr = sem("s_tabr"); s_tabw = sem("s_tabw")
        s_stage = sem("s_stage"); s_rows = [sem(f"s_rows{b}") for b in range(RING)]
        s_prod = sem("s_prod"); s_raw = sem("s_raw"); s_scored = sem("s_scored"); s_bmax = sem("s_bmax"); s_dif = sem("s_dif")
        s_exp = sem("s_exp"); s_ev = sem("s_ev"); s_den = sem("s_den"); s_wv = sem("s_wv"); s_part = sem("s_part")
        s_partT = sem("s_partT"); s_penr = sem("s_penr"); s_carry = sem("s_carry"); s_runmax = sem("s_runmax")
        s_dd = sem("s_dd"); s_ww = sem("s_ww"); s_w0 = sem("s_w0"); s_wx = sem("s_wx"); s_wE = sem("s_wE")
        s_den1 = sem("s_den1"); s_denS = sem("s_denS"); s_num1 = sem("s_num1"); s_numS = sem("s_numS")
        s_back = sem("s_back"); s_outst = sem("s_outst"); s_outw = [sem(f"s_outw{u}") for u in range(2)]
        s_comb = sem("s_comb"); s_norm = sem("s_norm"); s_aT = sem("s_aT"); s_aTc = sem("s_aTc"); s_fin = sem("s_fin")
        s_xb = sem("s_xb"); s_b12 = sem("s_b12"); s_m12 = sem("s_m12"); s_tb = sem("s_tb"); s_tsb = sem("s_tsb")
        s_msg = sem("s_msg"); s_agg = sem("s_agg"); s_y = sem("s_y"); s_yc = sem("s_yc"); s_bnv = sem("s_bnv"); s_bns = sem("s_bns")
        s_xT = sem("s_xT"); s_xTp = sem("s_xTp"); s_cw = sem("s_cw"); s_mu = sem("s_mu"); s_leaky = sem("s_leaky"); s_hn = sem("s_hn"); s_xout = sem("s_xout"); s_done = sem("s_done")

        CH = [(c, min(4, NT - c)) for c in range(0, NT, 4)]
        NCH = len(CH)
        ATT = {0: 0, 1: 1, 5: 2}
        CONV = {2: 0, 3: 1, 4: 2}
        TABF = {0: 36, 1: 64, 2: F, 3: F, 4: F, 5: F}
        QF = {0: H, 1: F, 5: H * F}
        PF = {0: P, 1: F, 5: P}
        WAYS = {0: 2 * H, 1: 3 * F, 5: H * F}

        tabw = {l: sum(64 if m in ATT else 32 for m in range(l + 1)) for l in range(LAYERS)}

        def per(u):
            return G // 2 + (1 - u)

        def groups(eng, body):
            body(0, 0, 0)
            with eng.Fori(0, (G - 1) // 2) as i:
                body(2 * i + 1, 1, i)
                body(2 * i + 2, 0, i + 1)

        def ring(b):
            return (G - b + RING - 1) // RING

        def quads(eng, body, first=0):
            for g in range(first, 3):
                body(g, g % 2, g, 0)
            assert (G - 3) % RING == 0 and RING == 4
            with eng.Fori(0, (G - 3) // RING) as i:
                body(RING * i + 3, 1, 3, i)
                for b in range(3):
                    body(RING * i + 4 + b, b % 2, b, i + 1)

        def batches(eng, body):
            body(0, 0)
            body(1, 1)
            with eng.Fori(1, SORTS // 2) as i:
                for u in range(2):
                    body(2 * i + u, u)

        block = ctx.enter_context(nc.Block())

        @block.sync
        def _(sp):
            for k, name in enumerate(("src", "dst")):
                if k == 0:
                    sp.wait_ge(s_pad, 3)
                sp.dma_start(key_i[k][0:EP - 1, :], A[name][0:(EP - 1) * ET].rearrange("(p t) -> p t", t=ET)).then_inc(s_keyin[k], 16)
                sp.dma_start(key_i[k][EP - 1:EP, 0:LASTE], A[name][(EP - 1) * ET:EDGES].rearrange("(p t) -> p t", p=1)).then_inc(s_keyin[k], 16)
            with nc.allow_non_contiguous_dma(reason="single columns of a few small vectors"):
                W = []
                W.append(sp.dma_start(x[:, 0:NT - 1, :], A["x"][0:(NT - 1) * P, :].rearrange("(t p) f -> p t f", p=P)))
                W.append(sp.dma_start(w0[:, :, :], A["L0_gnn_w"].rearrange("h f o -> f h o")))
                W.append(sp.dma_start(w0cat[:, :], A["L0_gnn_w"].rearrange("h f o -> (h f) o")))
                W.append(sp.dma_start(fcw[:, :, :], A["L0_gnn_fc_w"].rearrange("a (s o) -> a s o", s=2).to_broadcast([F, 2, F])))
                W.append(sp.dma_start(fcb[:, :], A["L0_gnn_fc_b"].rearrange("(a b) -> a b", b=1).to_broadcast([P, 1])))
                W.append(sp.dma_start(bias0[:, :], A["L0_gnn_bias"].rearrange("(a b) -> a b", a=1).to_broadcast([P, F])))
                for i, name in enumerate(("Wk", "Wv", "Wq")):
                    W.append(sp.dma_start(wkvq[:, i * F:(i + 1) * F], A["L1_gnn_" + name]))
                W.append(sp.dma_start(wo[:, :], A["L1_gnn_Wo"]))
                for i, name in enumerate(("Wq", "Wk", "Wv")):
                    W.append(sp.dma_start(w3[:, i, :].rearrange("f (h o) -> f h o", h=H), A["L3_gnn_" + name].rearrange("h f o -> f h o")))
                W.append(sp.dma_start(wout[:, :], A["L3_gnn_Wout"]))
                for i in range(3):
                    W.append(sp.dma_start(cr[:, i, :], A[f"L2_gnn_R{i + 1}"]))
                    for j, name in enumerate(("b", "g", "be")):
                        W.append(sp.dma_start(cb[:, 3 * i + j:3 * i + j + 1], A[f"L2_gnn_{name}{i + 1}"].rearrange("(c a) -> c a", a=1)))
                for ins in W:
                    ins.then_inc(s_w, 16)
                assert len(W) == NW, len(W)
                sp.wait_ge(s_xpad, 1)
                sp.dma_start(x[0:LASTN, NT - 1, :], A["x"][(NT - 1) * P:NODES, :]).then_inc(s_xl, 16)
            sp.dma_start(attr[0:EP - 1, :], A["edge_attr_3"][0:(EP - 1) * ET, :].rearrange("(p t) c -> p (t c)", t=ET)).then_inc(s_load, 16)
            sp.dma_start(attr[EP - 1:EP, 0:LASTE * 3], A["edge_attr_3"][(EP - 1) * ET:EDGES, :].rearrange("(p t) c -> p (t c)", p=1)).then_inc(s_load, 16)
            sp.wait_ge(s_fill, 4)
            sp.dma_start(D["slots0"][0:NB * R, :].rearrange("(g c) a -> g (c a)", g=G), comb[0:G, 0:1024]).then_inc(s_filled, 16)
            sp.dma_start(D["slots1"][0:NB * R, :].rearrange("(g c) a -> g (c a)", g=G), fill[0:G, :, :].rearrange("p c a -> p (c a)")).then_inc(s_filled, 16)
            for k in range(2):
                sp.dma_start(D[f"flags{k}"].rearrange("(g c) a -> g (c a)", g=G), zero[0:G, 0:P]).then_inc(s_filled, 16)
            for u in range(2):
                sp.wait_ge(s_sc[u], (SORTS // 2) * 2 * EB * 16)
            sp.wait_ge(s_flag, 2 * NT * 16)

            def load_groups(k):
                sp.dma_start(flg[:, :], D[f"flags{k}"].rearrange("(g p) a -> g (p a)", p=P)).then_inc(s_slots, 16)
                w = 4 if k else 1
                sp.dma_start(comb[:, 0:G * R * w].rearrange("p (g c) -> p g c", g=G),
                             D[f"slots{k}"][0:NB * R, :].rearrange("(g p r) a -> p g (r a)", p=P, r=R)).then_inc(s_slots, 16)

            def share_groups(k):
                sp.wait_ge(s_same, 2 * (k + 1))
                sp.dma_start(D[f"same{k}"].rearrange("(g p) -> g p", p=P), same_g[:, :]).then_inc(s_samew, 16)
                sp.dma_start(D[f"loc{k}"].rearrange("(g p) -> g p", p=P), loc_g[:, :]).then_inc(s_samew, 16)
                sp.wait_ge(s_nid, k + 1)
                sp.dma_start(D[f"first{k}"].rearrange("(g a) -> g a", a=1), first_i[:, :]).then_inc(s_samew, 16)
                sp.wait_ge(s_samew, 48 * (k + 1))
                sp.dma_start(same[:, :], D[f"same{k}"].rearrange("(a n) -> a n", a=1).to_broadcast([F, NB])).then_inc(s_samer, 16)
                load_loc(k)

            def load_loc(k):
                sp.dma_start(loc[:, 0:NB], D[f"loc{k}"].rearrange("(a n) -> a n", a=1).to_broadcast([P, NB])).then_inc(s_samer, 16)

            def tables(l):
                sp.wait_ge(s_tabr, l + 1)
                f = TABF[l]
                rowsrc = (tab[:, 0:NT * f].rearrange("p (t c) -> p t c", c=f) if l in (0, 1) else h[:, :, :])
                sp.dma_start(D[f"tab{l}"][0:NT * P, :].rearrange("(t p) c -> p t c", p=P), rowsrc).then_inc(s_tabw, 16)
                sp.dma_start(D[f"tab{l}"][NT * P:NT * P + 1, :], zero[0:1, 0:f]).then_inc(s_tabw, 16)
                if l in QF:
                    q = QF[l]
                    sp.dma_start(D[f"q{l}"][NT * P:, :], zero[:, 0:q]).then_inc(s_tabw, 16)
                    sp.dma_start(D[f"q{l}"][0:NT * P, :].rearrange("(t p) c -> p t c", p=P),
                                 wide[:, 0:NT * q].rearrange("p (t c) -> p t c", c=q)).then_inc(s_tabw, 16)

            def blocks_out(l):
                w = PF[l] + H if l in ATT else F
                src = out_st if l in ATT else cout

                def store(g, u, o):
                    sp.wait_ge(s_outst, l * G + g + 1)
                    sp.dma_start(D[f"blk{l}"].rearrange("(g p) c -> g p c", p=P)[bass.ds(g, 1), :, :].rearrange("a p c -> (a p) c"),
                                 src[u][:, 0:w]).then_inc(s_outw[u], 16)

                def fetch(g, u, o):
                    k = 0 if l == 0 else 1
                    n0 = sp.value_load(D[f"first{k}"].rearrange("(a g) -> a g", a=1)[:, bass.ds(g, 1)], min_val=0, max_val=NODES - 1)
                    if not (isinstance(g, int) and g < 2):
                        sp.wait_ge(s_q, ATT[l] * G + g - 1)
                    sp.dma_start(window[u][:, 0:QF[l]], D[f"q{l}"][bass.ds(n0, P), :]).then_inc(s_win[u], 16)

                if l not in ATT:
                    groups(sp, store)
                    return
                sp.wait_ge(s_tabw, tabw[l])
                for g in range(4):
                    fetch(g, g % 2, g // 2)
                store(0, 0, 0)
                fetch(4, 0, 2)
                store(1, 1, 0)
                with sp.Fori(2, (G - 1) // 2) as i:
                    fetch(2 * i + 1, 1, i)
                    store(2 * i - 2, 0, i - 1)
                    fetch(2 * i + 2, 0, i + 1)
                    store(2 * i - 1, 1, i - 1)
                for g in range(G - 3, G):
                    store(g, g % 2, g // 2)

            sp.wait_ge(s_vo, 1)
            for hh in range(H):
                sp.dma_start(wvocat[hh * F:(hh + 1) * F, :], wvo[:, hh * F:(hh + 1) * F]).then_inc(s_vod, 16)
            for l in range(LAYERS):
                if l < 2:
                    if l:
                        sp.wait_ge(s_done, 1)
                    load_groups(l)
                if l in CONV:
                    if CONV[l]:
                        sp.wait_ge(s_msg, CONV[l] * G)
                    sp.dma_start(cw[:, :, :], A[f"L2_gnn_W{CONV[l] + 1}"].rearrange("(k q) c o -> (q c) k o", q=4)).then_inc(s_cw, 16)
                if l == 5:
                    sp.wait_ge(s_msg, 3 * G)
                    load_loc(1)
                tables(l)
                if l < 2:
                    share_groups(l)
                blocks_out(l)
                if l == 0:
                    sp.wait_ge(s_E, G + 2)
                    sp.dma_start(fill_all[0:G, :], D["slots1"][0:NB * R, :].rearrange("(g c) a -> g (c a)", g=G)).then_inc(s_fslots, 16)
            sp.wait_ge(s_done, LAYERS if LAYERS < 3 else max(2, LAYERS - 2))
            sp.dma_start(out[0:(NT - 1) * P, :].rearrange("(t p) f -> p t f", p=P), x[:, 0:NT - 1, :]).then_inc(s_xout, 16)
            sp.dma_start(out[(NT - 1) * P:NODES, :], x[0:LASTN, NT - 1, :]).then_inc(s_xout, 16)
            sp.wait_ge(s_xout, 32)

        @block.gpsimd
        def _(pool):
            c = Chain(pool, s_pool)
            c.add(nc.gpsimd.memset(ident[:, :], 0.0))
            c.add(nc.gpsimd.memset(below[:, :], 1.0))
            c.add(nc.gpsimd.memset(above[:, :], 1.0))
            c.add(nc.gpsimd.memset(ones[:, :], 1.0))
            c(nc.gpsimd.iota(iota_i[:, :], pattern=[[1, P]], base=0, channel_multiplier=0))
            nc.gpsimd.affine_select(out=ident[:, :], in_=ident[:, :], compare_op=ALU.not_equal, fill=1.0, base=0,
                                    pattern=[[-1, P]], channel_multiplier=1).then_inc(s_const, 1)
            nc.gpsimd.affine_select(out=below[:, :], in_=below[:, :], compare_op=ALU.is_gt, fill=0.0, base=0,
                                    pattern=[[-1, P]], channel_multiplier=1).then_inc(s_const, 1)
            nc.gpsimd.affine_select(out=above[:, :], in_=above[:, :], compare_op=ALU.is_gt, fill=0.0, base=0,
                                    pattern=[[1, P]], channel_multiplier=-1).then_inc(s_const, 1)
            nc.gpsimd.iota(sel_i[:, 0, :].rearrange("p (a b) -> p a b", a=H), pattern=[[1, H], [0, F]], base=0, channel_multiplier=-1).then_inc(s_const, 1)
            nc.gpsimd.iota(sel_i[:, 1, :].rearrange("p (a b) -> p a b", b=R), pattern=[[1, P // R], [0, R]], base=0, channel_multiplier=-1).then_inc(s_const, 1)
            nc.gpsimd.iota(mask_i, pattern=[[1, P // R], [0, 16]], base=0, channel_multiplier=0).then_inc(s_const, 1)
            nc.gpsimd.iota(prt_i[:, :], pattern=[[0, 1]], base=0, channel_multiplier=1).then_inc(s_const, 1)
            nc.gpsimd.memset(fill[:, :, 1:4], 0.0).then_inc(s_fill, 1)
            nc.gpsimd.memset(fill[:, :, 0:1], float(DUMMY)).then_inc(s_fill, 1)
            nc.gpsimd.memset(fill0, float(DUMMY)).then_inc(s_fill, 1)
            pool.wait_ge(s_const, 7)

            def gate(*waits):
                for s, v in waits:
                    pool.wait_ge(s, v)
                pool.sem_inc(s_gate, 1)

            pool.wait_ge(s_filled, 64)
            for k in range(2):
                pool.wait_ge(s_start, k + 1)
                for t in range(NT):
                    n = P if t < NT - 1 else LASTN
                    pool.indirect_dma_start(
                        out=D[f"flags{k}"], out_offset=bass.IndirectOffsetOnAxis(ap=start_i[k][0:n, t:t + 1], axis=0),
                        in_=ones[0:n, 0:1], in_offset=None).then_inc(s_flag, 16)

                def scatter(g, u):
                    gate((s_pos, k * SORTS + g + 1))
                    for j in range(EB):
                        pool.indirect_dma_start(
                            out=D[f"slots{k}"], out_offset=bass.IndirectOffsetOnAxis(ap=pos_st[u][:, j:j + 1], axis=0),
                            in_=pay_st[u][:, j, :] if k else srt_st[u][:, j:j + 1], in_offset=None).then_inc(s_sc[u], 16)
                batches(pool, scatter)
            for l in range(LAYERS):

                def gather(g, u, b, o):
                    need = [(s_stage, l * (G + RING) + g + 1)]
                    if isinstance(g, int) and g == 0:
                        need.append((s_tabw, tabw[l]))
                    gate(*need)
                    f = TABF[l]
                    for r in range(R):
                        pool.indirect_dma_start(
                            out=rows[b][:, r * f:(r + 1) * f], out_offset=None, in_=D[f"tab{l}"],
                            in_offset=bass.IndirectOffsetOnAxis(ap=idx_st[b][:, r:r + 1], axis=0)).then_inc(s_rows[b], 16)
                quads(pool, gather)
                pool.wait_ge(s_outw[0], 16 * (G // 2 + 1) * (l + 1))
                pool.wait_ge(s_outw[1], 16 * (G // 2) * (l + 1))
                w = PF[l] + H if l in ATT else F
                for t in range(NT):
                    pool.indirect_dma_start(
                        out=comb[:, t * w:(t + 1) * w], out_offset=None, in_=D[f"blk{l}"],
                        in_offset=bass.IndirectOffsetOnAxis(ap=last_i[0 if l == 0 else 1][:, t:t + 1], axis=0)).then_inc(s_comb, 16)

        @block.vector
        def _(dve):
            c = Chain(dve, s_dve)
            v = nc.vector
            for k in range(2):
                v.memset(key_i[k][:, LASTE:], PADKEY).then_inc(s_pad, 1)
            v.memset(attr[:, LASTE * 3:], 0.0).then_inc(s_pad, 1)
            v.memset(zero[:, :], 0.0).then_inc(s_fill, 1)
            dve.wait_ge(s_const, 7)
            c.add(v.tensor_copy(identb[:, :], ident[:, :]))
            c.add(v.tensor_copy(iota_b[:, :], iota_i[:, :]))
            c.sync()
            v.memset(x[:, NT - 1, :], 0.0).then_inc(s_xpad, 1)
            c.add(v.memset(eps[:, :], EPS))
            c.add(v.memset(less2[:, :], -2.0))
            c.add(v.memset(idx_a[:, G:, :], 0))
            c(v.memset(idx_c[:, G:, :], 0))
            c.add(v.tensor_single_scalar(sel[:, :, :], sel_i[:, :, :], 0.0, op=ALU.is_equal))
            c(v.tensor_copy(part_f[:, :], prt_i[:, :]))
            c(v.tensor_single_scalar(prt_i[:, :], prt_i[:, :], R.bit_length() - 1, op=ALU.arith_shift_right))
            c(v.tensor_copy(prt_f[:, :], prt_i[:, :]))
            c(v.tensor_scalar(mask[:, :, :], mask_i, prt_f[:, 0:1], None, ALU.is_equal))
            def keys(k):
                c.add(v.tensor_copy(key_f[k], key_i[k]))
                c(v.tensor_single_scalar(tmp_i, key_i[k], 127, op=ALU.bitwise_and))
                c(v.tensor_copy(lo_b[k], tmp_i))
                c(v.tensor_single_scalar(tmp_i, key_i[k], 7, op=ALU.arith_shift_right))
                c(v.tensor_copy(hi_b[k], tmp_i))

            def onehots(g, u, k, done):
                v.tensor_tensor(ohlo[k][u], iota_b[0:EP, None, :].to_broadcast([EP, EB, P]),
                                lo_b[k][:, bass.ds(g * EB, EB)].unsqueeze(2).to_broadcast([EP, EB, P]),
                                ALU.is_equal).then_inc(done, 1)
                v.tensor_tensor(ohhi[k][u], iota_b[0:EP, None, 0:NT].to_broadcast([EP, EB, NT]),
                                hi_b[k][:, bass.ds(g * EB, EB)].unsqueeze(2).to_broadcast([EP, EB, NT]),
                                ALU.is_equal).then_inc(done, 1)

            def count(g, u, k):
                if not (isinstance(g, int) and g < 2):
                    dve.wait_ge(s_hist, k * SORTS + g - 1)
                onehots(g, u, k, s_oh)

            def starts(k):
                dve.wait_ge(s_histall, k + 1)
                c(v.tensor_copy(deg[k][:, :], hist[k]))
                c(v.tensor_scalar(tot[:, :], deg[k][:, :], 1.0, float(R - 1), ALU.max, ALU.add))
                c(v.tensor_copy(nblk_i[:, :], tot[:, :]))
                c(v.tensor_single_scalar(nblk_i[:, :], nblk_i[:, :], R.bit_length() - 1, op=ALU.arith_shift_right))
                v.tensor_copy(nblk[k][:, :], nblk_i[:, :]).then_inc(s_nblk, 1)
                dve.wait_ge(s_prefix, k + 1)
                c(v.tensor_copy(tot[:, :], bank[3][:, NT:2 * NT]))
                c(v.tensor_tensor_scan(start[k][:, :], ones[:, 0:NT], tot[:, :], 0.0, ALU.mult, ALU.add))
                c(v.tensor_tensor(start[k][:, :], start[k][:, :], tot[:, :], ALU.subtract))
                c(v.tensor_tensor(start[k][:, :], start[k][:, :], bank[3][:, 0:NT], ALU.add))
                c(v.tensor_copy(start_i[k][:, :], start[k][:, :]))
                c(v.tensor_tensor(tot[:, :], start[k][:, :], nblk[k][:, :], ALU.add))
                c(v.tensor_scalar(tot[:, :], tot[:, :], -1.0, None, ALU.add))
                c(v.tensor_copy(last_i[k][:, :], tot[:, :]))
                v.tensor_scalar(start[k][:, :], start[k][:, :], float(R), None, ALU.mult).then_inc(s_start, 1)
                dve.wait_ge(s_start, k + 1)

            def columns(g, u, k):
                onehots(g, u, k, s_oh2)
                v.tensor_copy(lo_st[u][:, :], lo_b[k][:, bass.ds(g * EB, EB)]).then_inc(s_oh2, 1)
                v.tensor_scalar(hi_st[u][:, :], hi_b[k][:, bass.ds(g * EB, EB)], 128.0, None, ALU.mult).then_inc(s_oh2, 1)
                v.tensor_copy(keys_st[u][:, :], key_f[k][:, bass.ds(g * EB, EB)]).then_inc(s_oh2, 1)
                if k == 0:
                    count(g, u, 1)

            def positions(g, u, k):
                n = k * SORTS + g + 1
                dve.wait_ge(s_key, n)
                for j in range(EB):
                    v.scalar_tensor_tensor(junk[:, j, :], keyrow[u][j], keys_st[u][:, j:j + 1],
                                           below[0:EP, 0:EP], ALU.is_equal, ALU.mult,
                                           accum_out=rank_in[:, j:j + 1]).then_inc(s_rank, 1)
                dve.wait_ge(s_look, n)
                v.tensor_tensor(picked, look, ohhi[k][u], ALU.mult).then_inc(s_pick, 1)
                dve.wait_ge(s_pick, n)
                v.tensor_reduce(baseline[:, :], picked, AX.X, ALU.add).then_inc(s_bl, 1)
                if not (k == 0 and isinstance(g, int) and g < 2):
                    dve.wait_ge(s_sc[u], (g - u + k * SORTS) * (EB * 8))
                if k:
                    v.tensor_copy(pay_st[u][:, :, :], payload[:, bass.ds(g * EB, EB), :]).then_inc(s_pay, 1)
                else:
                    v.tensor_copy(srt_st[u][:, :], key_f[1][:, bass.ds(g * EB, EB)]).then_inc(s_pay, 1)
                dve.wait_ge(s_pay, n)
                dve.wait_ge(s_bl, n)
                dve.wait_ge(s_rank, EB * n)
                v.tensor_tensor(pos_st[u][:, :], baseline[:, :], rank_in[:, :], ALU.add).then_inc(s_pos, 1)
                dve.wait_ge(s_pos, n)

            def sort(k):
                columns(0, 0, k)
                columns(1, 1, k)
                positions(0, 0, k)
                with dve.Fori(1, SORTS // 2) as i:
                    columns(2 * i, 0, k)
                    positions(2 * i - 1, 1, k)
                    columns(2 * i + 1, 1, k)
                    positions(2 * i, 0, k)
                positions(SORTS - 1, 1, k)

            dve.wait_ge(s_keyin[0], 32)
            keys(0)
            batches(dve, lambda g, u: count(g, u, 0))
            starts(0)
            dve.wait_ge(s_keyin[1], 32)
            keys(1)
            dve.wait_ge(s_load, 32)
            c.add(v.tensor_copy(payload[:, :, 0], key_f[0]))
            c(v.tensor_copy(payload[:, :, 1:4], attr.rearrange("p (t c) -> p t c", c=3)))
            sort(0)
            starts(1)
            sort(1)
            dve.wait_ge(s_w, 16 * NW)
            for i in range(2):
                c(v.tensor_tensor(wtmp[:, :, :], w0[:, :, :], fcw[:, i:i + 1, :].to_broadcast([F, H, F]), ALU.mult))
                c(v.tensor_reduce(wa[:, i * H:(i + 1) * H], wtmp[:, :, :], AX.X, ALU.add))
            for i in range(3):
                v.transpose(w3T[:, i, :], w3[:, i, :]).then_inc(s_wT, 1)
            dve.wait_ge(s_wp, 1)
            c.add(v.tensor_scalar(wqk[:, :], bank[3][0:F, 0:P], INV_F, None, ALU.mult))
            v.tensor_scalar(wvo[:, :], bank[3][0:F, P:2 * P], 1.0 / H, None, ALU.mult).then_inc(s_vo, 1)
            c.add(v.tensor_scalar(w0cat[:, :], w0cat[:, :], 1.0 / H, None, ALU.mult))
            c(v.tensor_scalar(wkvq[:, 2 * F:3 * F], wkvq[:, 2 * F:3 * F], INV_D8, None, ALU.mult))
            c(v.tensor_scalar(rcnt[:, :], deg[1][:, :], 1.0, None, ALU.max))
            c(v.reciprocal(rcnt[:, :], rcnt[:, :]))
            dve.wait_ge(s_xl, 16)

            def prepare(k):
                dve.wait_ge(s_slots, 32 * (k + 1))
                c(v.tensor_tensor_scan(cum[:, :], ones[0:G, :], flg[:, :], 0.0, ALU.mult, ALU.add))
                v.tensor_copy(starts_g[:, :], cum[:, P - 1:P]).then_inc(s_prep, 1)
                v.tensor_scalar(same_g[:, :], flg[:, :], -1.0, 1.0, ALU.mult, ALU.add).then_inc(s_same, 1)
                v.tensor_scalar(loc_g[:, :], cum[:, :], cum[:, 0:1], None, ALU.subtract).then_inc(s_same, 1)
                dve.wait_ge(s_off, k + 1)
                v.tensor_scalar(first_i[:, :], cum[:, 0:1], bank[3][0:G, 0:1], -1.0, ALU.add, ALU.add).then_inc(s_nid, 1)
                w = 4 if k else 1
                slot = comb[:, 0:G * R * w].rearrange("p (g r c) -> p g r c", r=R, c=w)[:, :, :, 0]
                c.add(v.tensor_copy(idx_a[:, 0:G, 0:R], slot))
                c(v.tensor_scalar(valid[:, :, :], slot, float(DUMMY), None, ALU.is_lt))
                c(v.tensor_scalar(pen[:, :, :], valid[:, :, :], -1.0, BIG, ALU.add, ALU.mult))
                dve.wait_ge(s_samer, 32 * (k + 1))

            def conv_slots():
                for n, (j, fld) in enumerate((j, fld) for j in range(R) for fld in range(4)):
                    dve.wait_ge(s_slT, n + 1)
                    dst = idx_c[:, 0:G, j] if fld == 0 else attr_c[:, fld - 1, :, j]
                    v.tensor_copy(dst, bank[4 + n % 2][:, 0:G]).then_inc(s_slc, 1)
                dve.wait_ge(s_slc, 32)
                flat = wide[:, 0:3 * G * R]
                c(v.tensor_scalar(flat, flat, 3.0, 0.0, ALU.mult, ALU.max))
                v.tensor_scalar(flat, flat, 3.0, None, ALU.min).then_inc(s_clip, 1)
                dve.wait_ge(s_clip, 1)
                for kk in (1, 2):
                    for d in range(3):
                        a = wide[:, d * G * R:(d + 1) * G * R]
                        line = tab[:, 0:G * R]
                        c(v.tensor_scalar(line, a, -1.0, 1.0 + kk, ALU.mult, ALU.add))
                        c(v.scalar_tensor_tensor(line, a, 1.0 - kk, line, ALU.add, ALU.min))
                        c(v.tensor_scalar(hats[:, :, d, kk], line, 0.0, None, ALU.max))
                dve.wait_ge(s_hats, 2)

            def layernorm(n):
                cx = tab[:, 0:NT * F].rearrange("p (t f) -> p t f", f=F)
                sq = wide[:, 0:NT * F].rearrange("p (t f) -> p t f", f=F)
                c(v.tensor_reduce(lnm[:, :], x[:, :, :], AX.X, ALU.add))
                c(v.tensor_scalar(lnm[:, :], lnm[:, :], 1.0 / F, None, ALU.mult))
                c(v.tensor_tensor(cx, x[:, :, :], lnm[:, :].unsqueeze(2).to_broadcast([P, NT, F]), ALU.subtract))
                c(v.tensor_tensor(sq, cx, cx, ALU.mult))
                c(v.tensor_reduce(lns[:, :], sq, AX.X, ALU.add))
                v.tensor_scalar(lns[:, :], lns[:, :], 1.0 / F, None, ALU.mult).then_inc(s_var, 1)
                dve.wait_ge(s_std, n + 1)
                c(v.reciprocal(lns[:, :], lns[:, :]))
                c(v.tensor_tensor(cx, cx, lns[:, :].unsqueeze(2).to_broadcast([P, NT, F]), ALU.mult))
                v.tensor_scalar(h[:, :, :], cx, 0.0, None, ALU.max).then_inc(s_h, 1)
                dve.wait_ge(s_h, n + 1)
                for i, (t, m) in enumerate(CH):
                    dve.wait_ge(s_hTp, NCH * n + i + 1)
                    v.tensor_copy(hT[:, t * P:(t + m) * P], bank[4 + i % 2][0:F, 0:m * P]).then_inc(s_hTc, 1)
                dve.wait_ge(s_hTc, NCH * (n + 1))

            def node_tables(l):
                a, f, q, w = ATT[l], TABF[l], QF[l], WAYS[l]
                tb = tab[:, 0:NT * f].rearrange("p (t c) -> p t c", c=f)
                qt = wide[:, 0:NT * q].rearrange("p (t c) -> p t c", c=q)
                if l == 0:
                    c.add(v.tensor_copy(tb[:, :, 0:F], h[:, :, :]))
                for i, (t, m) in enumerate(CH):
                    dve.wait_ge(s_tp, NCH * a + i + 1)
                    ps = bank[6 + i % 2][:, 0:m * w].rearrange("p (t c) -> p t c", c=w)
                    if l == 0:
                        v.tensor_copy(tb[:, t:t + m, F:F + H], ps[:, :, H:2 * H]).then_inc(s_tc, 1)
                        v.tensor_scalar(qt[:, t:t + m, :], ps[:, :, 0:H], fcb[:, 0:1], None, ALU.add).then_inc(s_tc, 1)
                    elif l == 1:
                        v.tensor_copy(tb[:, t:t + m, :], ps[:, :, 0:2 * F]).then_inc(s_tc, 1)
                        v.tensor_copy(qt[:, t:t + m, :], ps[:, :, 2 * F:3 * F]).then_inc(s_tc, 1)
                    else:
                        v.tensor_copy(qt[:, t:t + m, 0:F], ps[:, :, 0:F]).then_inc(s_tc, 1)
                        v.tensor_copy(qt[:, t:t + m, F:], ps[:, :, F:]).then_inc(s_tc, 1)
                dve.wait_ge(s_tc, 2 * NCH * (a + 1))
                c.sync()
                v.memset(runmax[:, P:P + 1], -BIG).then_inc(s_tabr, 1)

            def stage(l, g, b):
                src = idx_a if l in ATT else idx_c
                v.tensor_copy(idx_st[b][:, :], src[:, bass.ds(g, 1), :].rearrange("p a c -> p (a c)")).then_inc(s_stage, 1)

            def place(g, u):
                v.tensor_scalar(spread_q[u][:, :], loc[:, bass.ds(g * P, P)], part_f[:, 0:1], None, ALU.is_equal).then_inc(s_E, 1)

            def attention(l):
                a, f, q, pf = ATT[l], TABF[l], QF[l], PF[l]
                dve.wait_ge(s_tabr, l + 1)
                if l == 5:
                    dve.wait_ge(s_samer, 80)
                c.add(v.memset(loc[:, NB:], 0))
                c.add(v.memset(numS[1][:, P - 1:P], 0.0))
                c(v.memset(denS[1][:, P - 1:P], 0.0))
                if l:
                    dve.wait_ge(s_stage, l * (G + RING))
                for b in range(RING):
                    stage(l, b, b)
                for u in range(2):
                    place(u, u)

                def slots(ap):
                    return ap.rearrange("p a r -> p (a r)").unsqueeze(2).to_broadcast([P, R, H])

                def products(g, u, b, o):
                    n = a * G + g + 1
                    X = rows[b][:, 0:R * f].rearrange("p (r c) -> p r c", c=f)
                    Q = bank[4 + u][:, 0:q]
                    if not (isinstance(g, int) and g == 0 and a == 0):
                        dve.wait_ge(s_part, n - 1)
                    dve.wait_ge(s_q, n)
                    dve.wait_ge(s_rows[b], (o + (l * ring(b) + 1)) * (R * 16))
                    if l == 0:
                        v.tensor_tensor(dif[:, :, :], X[:, :, F:F + H], Q.unsqueeze(1).to_broadcast([P, R, H]), ALU.add).then_inc(s_prod, 1)
                    elif l == 1:
                        v.tensor_tensor(prod[:, 0:R * F].rearrange("p (r c) -> p r c", c=F), X[:, :, 0:F],
                                        Q.unsqueeze(1).to_broadcast([P, R, F]), ALU.mult).then_inc(s_prod, 1)
                    else:
                        v.tensor_tensor(prod[:, :].rearrange("p (r h c) -> p r h c", h=H, c=F), X.unsqueeze(2).to_broadcast([P, R, H, F]),
                                        Q.rearrange("p (h c) -> p h c", h=H).unsqueeze(1).to_broadcast([P, R, H, F]), ALU.mult).then_inc(s_prod, 1)

                def scores(g):
                    dve.wait_ge(s_prod, a * G + g + 1)
                    if l == 0:
                        v.scalar_tensor_tensor(sc_[:, :, :], dif[:, :, :], 0.2, dif[:, :, :], ALU.mult, ALU.max).then_inc(s_raw, 1)
                    else:
                        m = R * F if l == 1 else R * H * F
                        v.tensor_reduce(sc_[:, :, :].rearrange("p r h -> p (r h)"),
                                        prod[:, 0:m].rearrange("p (a c) -> p a c", a=R * H), AX.X, ALU.add).then_inc(s_raw, 1)

                def penalty(g):
                    dve.wait_ge(s_raw, a * G + g + 1)
                    v.tensor_tensor(sc_[:, :, :], sc_[:, :, :], slots(pen[:, bass.ds(g, 1), :]), ALU.add).then_inc(s_scored, 1)

                def block_max(g):
                    n = a * G + g + 1
                    dve.wait_ge(s_scored, n)
                    if not (isinstance(g, int) and g == 0 and a == 0):
                        dve.wait_ge(s_partT, n - 1)
                    v.tensor_reduce(stat[:, H:2 * H], sc_[:, :, :].rearrange("p r h -> p h r"), AX.X, ALU.max).then_inc(s_bmax, 1)

                def less_max(g):
                    dve.wait_ge(s_bmax, a * G + g + 1)
                    v.tensor_tensor(dif[:, :, :], sc_[:, :, :], stat[:, H:2 * H].unsqueeze(1).to_broadcast([P, R, H]), ALU.subtract).then_inc(s_dif, 1)

                def filled(g):
                    dve.wait_ge(s_exp, a * G + g + 1)
                    v.tensor_tensor(ex[:, :, :], ex[:, :, :], slots(valid[:, bass.ds(g, 1), :]), ALU.mult).then_inc(s_ev, 1)

                def block_den(g):
                    dve.wait_ge(s_ev, a * G + g + 1)
                    v.tensor_reduce(stat[:, 0:H], ex[:, :, :].rearrange("p r h -> p h r"), AX.X, ALU.add).then_inc(s_den, 1)

                def weighted(g, b):
                    X = rows[b][:, 0:R * f].rearrange("p (r c) -> p r c", c=f)
                    if l == 1:
                        v.tensor_tensor(prod[:, 0:R * F].rearrange("p (r h c) -> p r h c", h=H, c=F // H),
                                        X[:, :, F:2 * F].rearrange("p r (h c) -> p r h c", h=H),
                                        ex[:, :, :].unsqueeze(3).to_broadcast([P, R, H, F // H]), ALU.mult).then_inc(s_wv, 1)
                    else:
                        v.tensor_tensor(prod[:, :].rearrange("p (r h c) -> p r h c", h=H, c=F), X[:, :, 0:F].unsqueeze(2).to_broadcast([P, R, H, F]),
                                        ex[:, :, :].unsqueeze(3).to_broadcast([P, R, H, F]), ALU.mult).then_inc(s_wv, 1)

                def block_sums(g, b):
                    dve.wait_ge(s_wv, a * G + g + 1)
                    v.tensor_reduce(part[:, 0:pf], prod[:, 0:R * pf].rearrange("p (r c) -> p c r", c=pf), AX.X, ALU.add).then_inc(s_part, 1)
                    stage(l, g + RING, b)

                def carry_in(g):
                    v.tensor_scalar(penr[:, :], same[0:H, bass.ds(g * P, P)], -1.0, BIG, ALU.add, ALU.mult).then_inc(s_penr, 1)
                    v.tensor_copy(runmax[:, 0:1], runmax[:, P:P + 1]).then_inc(s_carry, 1)

                def carry_max(g):
                    n = a * G + g + 1
                    dve.wait_ge(s_penr, n)
                    dve.wait_ge(s_carry, n)
                    dve.wait_ge(s_partT, n)
                    v.tensor_tensor_scan(runmax[:, 1:P + 1], penr[:, :], bank[1][0:H, P:2 * P], runmax[:, 0:1], ALU.add, ALU.max).then_inc(s_runmax, 1)

                def carry_diff(g):
                    dve.wait_ge(s_runmax, a * G + g + 1)
                    v.tensor_tensor(dd[:, 0, :], bank[1][0:H, P:2 * P], runmax[:, 1:P + 1], ALU.subtract).then_inc(s_dd, 1)
                    v.tensor_tensor(dd[:, 1, :], runmax[:, 0:P], runmax[:, 1:P + 1], ALU.subtract).then_inc(s_dd, 1)

                def carry_clip(g):
                    n = a * G + g + 1
                    dve.wait_ge(s_dd, 3 * n - 1)
                    if not (isinstance(g, int) and g == 0 and a == 0):
                        dve.wait_ge(s_numS, n - 1)
                        dve.wait_ge(s_denS, n - 1)
                    v.tensor_scalar(dd[:, 1, :], dd[:, 1, :], 0.0, None, ALU.min).then_inc(s_dd, 1)

                def carry_same(g):
                    dve.wait_ge(s_ww, a * G + g + 1)
                    v.tensor_tensor(ww[:, 1, :], ww[:, 1, :], same[0:H, bass.ds(g * P, P)], ALU.mult).then_inc(s_w0, 1)

                def carry_den1(g):
                    dve.wait_ge(s_w0, a * G + g + 1)
                    v.tensor_tensor(den1[:, :], bank[1][0:H, 0:P], ww[:, 0, :], ALU.mult).then_inc(s_den1, 1)

                def carry_den(g, u):
                    dve.wait_ge(s_den1, a * G + g + 1)
                    v.tensor_tensor_scan(denS[u][:, :], ww[:, 1, :], den1[:, :], denS[1 - u][:, P - 1:P], ALU.mult, ALU.add).then_inc(s_denS, 1)

                def carry_num1(g):
                    dve.wait_ge(s_wE, a * G + g + 1)
                    v.tensor_tensor(num1[0:pf, :], bank[0][0:pf, 0:P], wE[0:pf, 0:P], ALU.mult).then_inc(s_num1, 1)

                def carry_num(g, u):
                    dve.wait_ge(s_num1, a * G + g + 1)
                    v.tensor_tensor_scan(numS[u][0:pf, :], wE[0:pf, P:2 * P], num1[0:pf, :], numS[1 - u][0:pf, P - 1:P], ALU.mult, ALU.add).then_inc(s_numS, 1)

                def body(g, u, b, o):
                    carry_in(g - 1)
                    products(g, u, b, o)
                    scores(g)
                    carry_max(g - 1)
                    penalty(g)
                    carry_diff(g - 1)
                    block_max(g)
                    carry_clip(g - 1)
                    less_max(g)
                    place(g + 2, u)
                    filled(g)
                    carry_same(g - 1)
                    block_den(g)
                    carry_den1(g - 1)
                    weighted(g, b)
                    carry_den(g - 1, 1 - u)
                    block_sums(g, b)
                    carry_num1(g - 1)
                    carry_num(g - 1, 1 - u)

                products(0, 0, 0, 0)
                scores(0)
                penalty(0)
                block_max(0)
                less_max(0)
                place(2, 0)
                filled(0)
                block_den(0)
                weighted(0, 0)
                block_sums(0, 0)
                quads(dve, body, 1)
                carry_in(G - 1)
                carry_max(G - 1)
                carry_diff(G - 1)
                carry_clip(G - 1)
                carry_same(G - 1)
                carry_den1(G - 1)
                carry_den(G - 1, 0)
                carry_num1(G - 1)
                carry_num(G - 1, 0)

            def attention_nodes(l):
                a, pf = ATT[l], PF[l]
                w = pf + H
                dve.wait_ge(s_comb, 16 * NT * (l + 1))
                cm = comb[:, 0:NT * w].rearrange("p (t c) -> p t c", c=w)
                d = cm[:, :, pf:w]
                c(v.tensor_scalar(d, d, 1e-16, None, ALU.max))
                c(v.reciprocal(d, d))
                for hh in range(H):
                    m = pf // H
                    v.tensor_tensor(cm[:, :, hh * m:(hh + 1) * m], cm[:, :, hh * m:(hh + 1) * m],
                                    cm[:, :, pf + hh:pf + hh + 1].to_broadcast([P, NT, m]), ALU.mult).then_inc(s_norm, 1)
                dve.wait_ge(s_norm, 4 * (a + 1))
                dve.wait_ge(s_fin, a + 1)
                for i, (t, m) in enumerate(((0, 16), (16, NT - 16))):
                    ps = bank[6 + i][:, 0:m * F].rearrange("p (t c) -> p t c", c=F)
                    c(v.tensor_tensor(x[:, t:t + m, :], x[:, t:t + m, :], ps, ALU.add))
                if l == 0:
                    v.tensor_tensor(x[:, :, :], x[:, :, :], bias0[:, None, :].to_broadcast([P, NT, F]), ALU.add).then_inc(s_done, 1)
                else:
                    v.tensor_tensor(x[:, :, :], x[:, :, :], h[:, :, :], ALU.add).then_inc(s_done, 1)
                dve.wait_ge(s_done, done_of[l])

            def convolution(l):
                q = CONV[l]
                dve.wait_ge(s_stage, l * (G + RING))
                c(v.memset(aggS[1][:, P - 1:P], 0.0))
                for b in range(RING):
                    stage(l, b, b)

                def body(g, u, b, o):
                    n = q * G + g + 1
                    X = rows[b][:, 0:R * F].rearrange("p (j c) -> p j c", c=F)
                    hat = hats[:, bass.ds(g * R, R), :, :]
                    if not (isinstance(g, int) and g < 2 and q == 0):
                        dve.wait_ge(s_tb, n - 2)
                    v.tensor_tensor(b12[:, :, :].rearrange("p j (b a) -> p j b a", b=4),
                                    hat[:, :, 2, :].unsqueeze(3).to_broadcast([P, R, 4, 4]),
                                    hat[:, :, 1, :].unsqueeze(2).to_broadcast([P, R, 4, 4]), ALU.mult).then_inc(s_b12, 1)
                    dve.wait_ge(s_b12, n)
                    v.tensor_tensor(m12[u].rearrange("p j (b k) -> p j b k", k=16), b12[:, :, :].unsqueeze(2).to_broadcast([P, R, P // R, 16]),
                                    mask[:, :, :].unsqueeze(1).to_broadcast([P, R, P // R, 16]), ALU.mult).then_inc(s_m12, 1)
                    dve.wait_ge(s_rows[b], (o + (l * ring(b) + 1)) * (R * 16))
                    v.tensor_tensor(xb[u], X.unsqueeze(2).to_broadcast([P, R, 4, F]),
                                    hat[:, :, 0, :].unsqueeze(3).to_broadcast([P, R, 4, F]), ALU.mult).then_inc(s_xb, 1)
                    dve.wait_ge(s_xb, n)
                    stage(l, g + RING, b)
                    if not (isinstance(g, int) and g < 2):
                        scan(g - 2, u)

                def scan(g, u):
                    n = q * G + g + 1
                    dve.wait_ge(s_msg, n)
                    if isinstance(g, int) and g == 0:
                        dve.wait_ge(s_m12, n)
                    else:
                        dve.wait_ge(s_agg, n - 1)
                    v.tensor_tensor_scan(aggS[u][:, :], same[:, bass.ds(g * P, P)], bank[2][0:F, 0:P],
                                         aggS[1 - u][:, P - 1:P], ALU.mult, ALU.add).then_inc(s_agg, 1)
                quads(dve, body)
                scan(G - 2, (G - 2) % 2)
                scan(G - 1, (G - 1) % 2)

            def conv_nodes(l):
                q = CONV[l]
                y = wide[0:F, 0:NT * P]
                dve.wait_ge(s_comb, 16 * NT * (l + 1))
                cm = comb[:, 0:NT * F].rearrange("p (t c) -> p t c", c=F)
                v.tensor_tensor(cm, cm, rcnt[:, :].unsqueeze(2).to_broadcast([P, NT, F]), ALU.mult).then_inc(s_yn, 1)
                for i, (t, m) in enumerate(CH):
                    dve.wait_ge(s_yc, NCH * q + i + 1)
                    if q < 2:
                        part_y = y[:, t * P:(t + m) * P]
                        v.scalar_tensor_tensor(part_y, part_y, 0.01, part_y, ALU.mult, ALU.max).then_inc(s_leaky, 1)
                if q < 2:
                    dve.wait_ge(s_leaky, NCH * (q + 1))
                mu, var, scale, shift, less_mu = (bn[:, i:i + 1] for i in range(5))
                c(v.scalar_tensor_tensor(y[:, 0:NODES], y[:, 0:NODES], 1.0, hT[:, 0:NODES], ALU.mult, ALU.add, accum_out=mu))
                v.tensor_scalar(less_mu, mu, -1.0 / NODES, None, ALU.mult).then_inc(s_mu, 1)
                dve.wait_ge(s_bns, q + 1)
                c(v.reciprocal(scale, var))
                c(v.tensor_tensor(scale, scale, cb[:, 3 * q + 1:3 * q + 2], ALU.mult))
                c(v.scalar_tensor_tensor(shift, less_mu, scale, cb[:, 3 * q + 2:3 * q + 3], ALU.mult, ALU.add))
                for i, (t, m) in enumerate(((0, 16), (16, NT - 16))):
                    v.tensor_scalar(hT[:, t * P:(t + m) * P], y[:, t * P:(t + m) * P], scale, shift, ALU.mult, ALU.add).then_inc(s_xT, 1)
                for i, (t, m) in enumerate(((0, 16), (16, NT - 16))):
                    dve.wait_ge(s_xTp, 2 * q + i + 1)
                    v.tensor_copy(h[:, t:t + m, :], bank[6 + i][:, 0:m * F].rearrange("p (t c) -> p t c", c=F)).then_inc(s_hn, 1)
                dve.wait_ge(s_hn, 2 * q + 2)
                if q < 2:
                    v.memset(bn[:, 5:6], 0.0).then_inc(s_tabr, 1)
                else:
                    v.tensor_tensor(x[:, :, :], x[:, :, :], h[:, :, :], ALU.add).then_inc(s_done, 1)
                    dve.wait_ge(s_done, done_of[l])

            for l in range(LAYERS):
                if l in (0, 1, 2, 5):
                    layernorm((0, 1, 2, 5).index(l))
                if l == 2:
                    v.memset(bn[:, 5:6], 0.0).then_inc(s_tabr, 1)
                if l in ATT:
                    node_tables(l)
                if l < 2:
                    prepare(l)
                if l in ATT:
                    attention(l)
                    if l == 0:
                        conv_slots()
                    attention_nodes(l)
                else:
                    convolution(l)
                    conv_nodes(l)

        @block.tensor
        def _(pe):
            mm = nc.tensor.matmul
            pe.wait_ge(s_fill, 4)
            def count(g, u, k):
                pe.wait_ge(s_oh, k * 2 * SORTS + 2 * g + 2)
                for j in range(EB):
                    last = mm(hist[k], ohlo[k][u][:, j, :], ohhi[k][u][:, j, :], start=False, stop=False,
                              skip_group_check=True)
                last.then_inc(s_hist, 1)

            def starts(k):
                mm(hist[k], zero[:, 0:P], zero[:, 0:NT], start=False, stop=True, skip_group_check=True).then_inc(s_histall, 1)
                pe.wait_ge(s_nblk, k + 1)
                mm(bank[3][:, 0:NT], above[:, :], nblk[k][:, :], start=True, stop=True)
                mm(bank[3][:, NT:2 * NT], ones[:, :], nblk[k][:, :], start=True, stop=True).then_inc(s_prefix, 1)
                pe.wait_ge(s_start, k + 1)
                mm(hist[k], ident[:, :], start[k][:, :], start=True, stop=True).then_inc(s_acc[k], 1)

            def rank(g, u, k):
                first = isinstance(g, int) and g == 0 and k == 0
                early = isinstance(g, int) and g < 2 and k == 0
                n = k * SORTS + g + 1
                pe.wait_ge(s_oh2, 5 * n)
                if not first:
                    pe.wait_ge(s_ohT, n - 1)
                for j in range(EB):
                    last = nc.tensor.transpose(trb[:, j * P:j * P + EP], ohlo[k][u][:, j, :], identb[0:EP, 0:EP])
                last.then_inc(s_T, 1)
                if k == 0:
                    count(g, u, 1)
                if not early:
                    pe.wait_ge(s_rank, EB * (n - 2))
                for j in range(EB):
                    lo = lo_st[u][:, j:j + 1].to_broadcast([EP, EP])
                    hi = hi_st[u][:, j:j + 1].to_broadcast([EP, EP])
                    mm(keyrow[u][j], lo, identb[0:EP, 0:EP], start=True, stop=False)
                    last = mm(keyrow[u][j], hi, identb[0:EP, 0:EP], start=False, stop=True)
                last.then_inc(s_key, 1)
                if not first:
                    pe.wait_ge(s_pick, n - 1)
                pe.wait_ge(s_ohT, n)
                for j in range(EB):
                    pe.wait_ge(s_cp[k], EB * g + j + 1)
                    mm(hist[k], ohlo[k][u][:, j, :], ohhi[k][u][:, j, :], start=False, stop=True,
                       skip_group_check=True).then_inc(s_acc[k], 1)
                    last = mm(look[:, j, :], ohloT[k][:, j, :], base_sb[k][:, j, :], start=True, stop=True)
                last.then_inc(s_look, 1)

            for k in range(2):
                mm(hist[k], zero[:, 0:P], zero[:, 0:NT], start=True, stop=False, skip_group_check=True)
            batches(pe, lambda g, u: count(g, u, 0))
            for k in range(2):
                if k:
                    pe.wait_ge(s_rank, EB * SORTS)
                starts(k)
                batches(pe, lambda g, u: rank(g, u, k))

            tr = nc.tensor.transpose

            def bank_ours(i):
                mm(bank[i][0:F, 0:1], zero[:, 0:F], zero[:, 0:1], start=True, stop=True)

            pe.wait_ge(s_wT, 3)
            pe.wait_ge(s_rank, 2 * EB * SORTS)
            for hh in range(H):
                one = slice(hh * F, (hh + 1) * F)
                mm(bank[3][0:F, hh * F:(hh + 1) * F], w3T[:, 0, one], w3T[:, 1, one], start=True, stop=True)
                last = mm(bank[3][0:F, P + hh * F:P + (hh + 1) * F], w3T[:, 2, one], wout[:, :], start=True, stop=True)
            last.then_inc(s_wp, 1)

            def prepare(k):
                pe.wait_ge(s_prep, k + 1)
                if k == 0:
                    pe.wait_ge(s_vo, 1)
                mm(bank[3][0:G, 0:1], above[0:G, 0:G], starts_g[:, :], start=True, stop=True).then_inc(s_off, 1)

            def conv_slots():
                pe.wait_ge(s_fslots, 16)
                for n, (j, fld) in enumerate((j, fld) for j in range(R) for fld in range(4)):
                    if n >= 2:
                        pe.wait_ge(s_slc, n - 1)
                    view = fill_all[0:G, j * 512:(j + 1) * 512].rearrange("g (s c) -> g s c", c=4)
                    tr(bank[4 + n % 2][:, 0:G], view[:, :, fld], ident[0:G, 0:G]).then_inc(s_slT, 1)
                pe.wait_ge(s_slc, 32)

            def h_transposed(n):
                pe.wait_ge(s_h, n + 1)
                for i, (t, m) in enumerate(CH):
                    if i >= 2:
                        pe.wait_ge(s_hTc, NCH * n + i - 1)
                    for k in range(m):
                        last = tr(bank[4 + i % 2][0:F, k * P:(k + 1) * P], h[:, t + k, :], ident[:, :])
                    last.then_inc(s_hTp, 1)

            def node_tables(l):
                a, w = ATT[l], WAYS[l]
                wt = {0: wa, 1: wkvq, 5: wqk}[l]
                pe.wait_ge(s_hTc, NCH * ((0, 1, 2, 5).index(l) + 1))
                for i, (t, m) in enumerate(CH):
                    if i >= 2:
                        pe.wait_ge(s_tc, 2 * NCH * a + 2 * (i - 1))
                    for k in range(m):
                        last = mm(bank[6 + i % 2][:, k * w:(k + 1) * w], hT[:, (t + k) * P:(t + k + 1) * P], wt[:, :], start=True, stop=True)
                    last.then_inc(s_tp, 1)

            def attention(l):
                a, pf = ATT[l], PF[l]

                def query(g, u, o):
                    pe.wait_ge(s_win[u], 16 * (a * per(u) + o + 1))
                    pe.wait_ge(s_E, a * (G + 2) + g + 1)
                    mm(bank[4 + u][:, 0:QF[l]], spread_q[u][:, :], window[u][:, 0:QF[l]], start=True, stop=True).then_inc(s_q, 1)

                def inward(g):
                    n = a * G + g + 1
                    pe.wait_ge(s_den, n)
                    pe.wait_ge(s_part, n)
                    tr(bank[0][0:pf, 0:P], part[:, 0:pf], ident[:, :])
                    tr(bank[1][0:H, 0:P], stat[:, 0:H], ident[:, :])
                    tr(bank[1][0:H, P:2 * P], stat[:, H:2 * H], ident[:, :]).then_inc(s_partT, 1)

                def outward(g, u):
                    n = a * G + g + 1
                    pe.wait_ge(s_w0, n)
                    mm(bank[2][:, 0:2 * P], sel[:, 0 if pf == P else 1, :], ww[:, :, :].rearrange("p a b -> p (a b)"),
                       start=True, stop=True).then_inc(s_wx, 1)
                    pe.wait_ge(s_denS, n)
                    pe.wait_ge(s_numS, n)
                    if not (isinstance(g, int) and g == 0):
                        pe.wait_ge(s_outst, l * G + g)
                    if pf < P:
                        bank_ours(3)
                    tr(bank[3][:, 0:pf], numS[u][0:pf, :], ident[0:pf, 0:pf])
                    tr(bank[3][:, pf:pf + H], denS[u][:, :], ident[0:H, 0:H]).then_inc(s_back, 1)

                def body(g, u):
                    outward(g - 1, 1 - u)
                    inward(g)
                query(0, 0, 0)
                query(1, 1, 0)
                inward(0)
                query(2, 0, 1)
                body(1, 1)
                with pe.Fori(1, (G - 1) // 2) as i:
                    query(2 * i + 1, 1, i)
                    body(2 * i, 0)
                    query(2 * i + 2, 0, i + 1)
                    body(2 * i + 1, 1)
                body(G - 1, 0)
                outward(G - 1, 0)

            def attention_nodes(l):
                a, pf = ATT[l], PF[l]
                w = pf + H
                wt = {0: w0cat, 1: wo, 5: wvocat}[l]
                cm = comb[:, 0:NT * w].rearrange("p (t c) -> p t c", c=w)
                pe.wait_ge(s_norm, 4 * (a + 1))
                pe.wait_ge(s_vod, 64)

                def products(i):
                    t, m = CH[i]
                    pe.wait_ge(s_aTc, NCH * a + i + 1)
                    for k in range(m):
                        n = t + k
                        last = mm(bank[6 + n // 16][:, (n % 16) * F:(n % 16 + 1) * F], aT[i % 2][0:pf, k * P:(k + 1) * P], wt[:, :], start=True, stop=True)
                    return last
                for i, (t, m) in enumerate(CH):
                    for k in range(m):
                        last = tr(bank[4 + i % 2][0:pf, k * P:(k + 1) * P], cm[:, t + k, 0:pf], ident[:, :])
                    last.then_inc(s_aT, 1)
                    if i:
                        products(i - 1)
                products(NCH - 1).then_inc(s_fin, 1)

            def convolution(l):
                q = CONV[l]
                pe.wait_ge(s_cw, 16 * (q + 1))

                def outer(g, u):
                    n = q * G + g + 1
                    pe.wait_ge(s_m12, n)
                    pe.wait_ge(s_xb, n)
                    if not (isinstance(g, int) and g == 0):
                        pe.wait_ge(s_tsb, n - 1)
                    for j in range(R):
                        last = mm(bank[4 + j // 2][:, (j % 2) * 2 * P:(j % 2 + 1) * 2 * P], xb[u][:, j, :, :].rearrange("p k c -> p (k c)"),
                                  m12[u][:, j, :], start=True, stop=True)
                    last.then_inc(s_tb, 1)

                def weights(g, u):
                    n = q * G + g + 1
                    pe.wait_ge(s_tsb, n)
                    if not (isinstance(g, int) and g == 0):
                        pe.wait_ge(s_agg, n - 1)
                    for k in range(16):
                        last = mm(bank[2][0:F, 0:P], cw[:, k, :], tsb[u][:, k, :], start=(k == 0), stop=(k == 15))
                    last.then_inc(s_msg, 1)

                def back(g, u):
                    n = q * G + g + 1
                    pe.wait_ge(s_agg, n)
                    if not (isinstance(g, int) and g == 0):
                        pe.wait_ge(s_outst, l * G + g)
                    bank_ours(3)
                    tr(bank[3][:, 0:F], aggS[u][:, :], ident[0:F, 0:F]).then_inc(s_back, 1)

                def body(g, u, o):
                    outer(g, u)
                    if not (isinstance(g, int) and g == 0):
                        weights(g - 1, 1 - u)
                        if not (isinstance(g, int) and g == 1):
                            back(g - 2, u)
                body(0, 0, 0)
                body(1, 1, 0)
                body(2, 0, 0)
                with pe.Fori(1, (G - 1) // 2) as i:
                    body(2 * i + 1, 1, i)
                    body(2 * i + 2, 0, i + 1)
                back(G - 2, (G - 2) % 2)
                weights(G - 1, (G - 1) % 2)
                back(G - 1, (G - 1) % 2)

            def conv_nodes(l):
                q = CONV[l]
                cm = comb[:, 0:NT * F].rearrange("p (t c) -> p t c", c=F)
                pe.wait_ge(s_yn, q + 1)
                for i, (t, m) in enumerate(CH):
                    if i >= 2:
                        pe.wait_ge(s_yc, NCH * q + i - 1)
                    last = mm(bank[4 + i % 2][0:F, 0:m * P], cr[:, q, :], hT[:, t * P:(t + m) * P], start=True, stop=False)
                    for k in range(m):
                        last = mm(bank[4 + i % 2][0:F, k * P:(k + 1) * P], cm[:, t + k, :], ident[:, :], start=False, stop=(k == m - 1))
                    last.then_inc(s_y, 1)
                for i, (t, m) in enumerate(((0, 16), (16, NT - 16))):
                    pe.wait_ge(s_xT, 2 * q + i + 1)
                    for k in range(m):
                        last = tr(bank[6 + i][:, k * F:(k + 1) * F], hT[:, (t + k) * P:(t + k + 1) * P], ident[0:F, 0:F])
                    last.then_inc(s_xTp, 1)

            for l in range(LAYERS):
                if l in (0, 1, 2, 5):
                    h_transposed((0, 1, 2, 5).index(l))
                if l in ATT:
                    node_tables(l)
                if l < 2:
                    prepare(l)
                if l in ATT:
                    attention(l)
                    if l == 0:
                        conv_slots()
                    attention_nodes(l)
                else:
                    convolution(l)
                    conv_nodes(l)

        @block.scalar
        def _(act):
            def rank(g, u, k):
                n = k * SORTS + g + 1
                if not (isinstance(g, int) and g == 0 and k == 0):
                    act.wait_ge(s_look, n - 1)
                act.wait_ge(s_T, n)
                nc.scalar.activation(ohloT[k], trb.rearrange("p (j c) -> p j c", c=P)[:, :, 0:EP],
                                     ACT.Copy).then_inc(s_ohT, 1)
                for j in range(EB):
                    act.wait_ge(s_acc[k], EB * g + j + 1)
                    nc.scalar.activation(base_sb[k][:, j, :], hist[k], ACT.Copy).then_inc(s_cp[k], 1)
            for k in range(2):
                batches(act, lambda g, u: rank(g, u, k))
            cp = nc.scalar.activation

            def layernorm(n):
                act.wait_ge(s_var, n + 1)
                cp(lns[:, :], lns[:, :], ACT.Sqrt, bias=eps[:, 0:1]).then_inc(s_std, 1)

            def attention(l):
                a, pf = ATT[l], PF[l]

                def exps(g):
                    n = a * G + g + 1
                    act.wait_ge(s_dif, n)
                    cp(ex[:, :, :], dif[:, :, :], ACT.Exp).then_inc(s_exp, 1)

                def carries(g):
                    n = a * G + g + 1
                    act.wait_ge(s_dd, 3 * n)
                    cp(ww[:, :, :], dd[:, :, :], ACT.Exp).then_inc(s_ww, 1)

                def spread(g):
                    n = a * G + g + 1
                    act.wait_ge(s_wx, n)
                    cp(wE[0:pf, :], bank[2][0:pf, 0:2 * P], ACT.Copy).then_inc(s_wE, 1)

                def outs(g, u, o):
                    act.wait_ge(s_back, l * G + g + 1)
                    if not (isinstance(g, int) and g < 2):
                        act.wait_ge(s_outw[u], 16 * (per(u) * l + o))
                    elif l:
                        act.wait_ge(s_outw[u], 16 * per(u) * l)
                    cp(out_st[u][:, 0:pf + H], bank[3][:, 0:pf + H], ACT.Copy).then_inc(s_outst, 1)

                def body(g, u, o):
                    exps(g)
                    carries(g - 1)
                    outs(g - 2, u, o - 1)
                    spread(g - 1)
                exps(0)
                exps(1)
                carries(0)
                spread(0)
                body(2, 0, 1)
                body(3, 1, 1)
                with act.Fori(2, (G - 1) // 2) as i:
                    body(2 * i, 0, i)
                    body(2 * i + 1, 1, i)
                body(G - 1, 0, (G - 1) // 2)
                carries(G - 1)
                outs(G - 2, 1, (G - 2) // 2)
                spread(G - 1)
                outs(G - 1, 0, (G - 1) // 2)

            def conv_slots():
                act.wait_ge(s_clip, 1)
                src = wide[:, 0:3 * G * R].rearrange("p (d s) -> p s d", d=3)
                cp(hats[:, :, :, 0], src, ACT.Relu, bias=ones[:, 0:1], scale=-1.0).then_inc(s_hats, 1)
                cp(hats[:, :, :, 3], src, ACT.Relu, bias=less2[:, 0:1]).then_inc(s_hats, 1)

            def attention_nodes(l):
                a, pf = ATT[l], PF[l]
                for i, (t, m) in enumerate(CH):
                    act.wait_ge(s_aT, NCH * a + i + 1)
                    cp(aT[i % 2][0:pf, 0:m * P], bank[4 + i % 2][0:pf, 0:m * P], ACT.Copy).then_inc(s_aTc, 1)

            def convolution(l):
                q = CONV[l]

                def body(g, u, o):
                    n = q * G + g + 1
                    act.wait_ge(s_tb, n)
                    if not (isinstance(g, int) and g < 2):
                        act.wait_ge(s_msg, n - 2)
                    view = tsb[u].rearrange("p k n -> p n k")
                    for b in range(4):
                        last = cp(view[:, 32 * b:32 * b + 32, :], bank[4 + b][:, :].rearrange("p (n k) -> p n k", k=16), ACT.Copy)
                    last.then_inc(s_tsb, 1)
                    if not (isinstance(g, int) and g < 2):
                        outs(g - 2, u, o - 1)

                def outs(g, u, o):
                    act.wait_ge(s_back, l * G + g + 1)
                    if isinstance(g, int) and g < 2:
                        act.wait_ge(s_outw[u], 16 * per(u) * l)
                    else:
                        act.wait_ge(s_outw[u], 16 * (per(u) * l + o))
                    cp(cout[u][:, :], bank[3][:, 0:F], ACT.Copy).then_inc(s_outst, 1)
                body(0, 0, 0)
                body(1, 1, 0)
                body(2, 0, 1)
                body(3, 1, 1)
                with act.Fori(2, (G - 1) // 2) as i:
                    body(2 * i, 0, i)
                    body(2 * i + 1, 1, i)
                body(G - 1, 0, (G - 1) // 2)
                outs(G - 2, 1, (G - 2) // 2)
                outs(G - 1, 0, (G - 1) // 2)

            def conv_nodes(l):
                q = CONV[l]
                for i, (t, m) in enumerate(CH):
                    act.wait_ge(s_y, NCH * q + i + 1)
                    cp(wide[0:F, t * P:(t + m) * P], bank[4 + i % 2][0:F, 0:m * P], ACT.Identity,
                       bias=cb[:, 3 * q:3 * q + 1]).then_inc(s_yc, 1)
                act.wait_ge(s_mu, q + 1)
                cp(ytmp[:, 0:NODES], wide[0:F, 0:NODES], ACT.Square, bias=bn[:, 4:5], accum_out=bn[:, 1:2]).then_inc(s_bnv, 1)
                act.wait_ge(s_bnv, q + 1)
                cp(bn[:, 1:2], bn[:, 1:2], ACT.Sqrt, bias=eps[0:F, 0:1], scale=1.0 / NODES).then_inc(s_bns, 1)

            for l in range(LAYERS):
                if l in (0, 1, 2, 5):
                    layernorm((0, 1, 2, 5).index(l))
                if l in ATT:
                    attention(l)
                    if l == 0:
                        conv_slots()
                    attention_nodes(l)
                else:
                    convolution(l)
                    conv_nodes(l)


_SCRATCH = {
    "slots0": (SLOTS, 1), "slots1": (SLOTS, 4), "flags0": (NB, 1), "flags1": (NB, 1),
    "tab0": (DUMMY + 1, 36), "tab1": (DUMMY + 1, 64), "tab2": (DUMMY + 1, F), "tab3": (DUMMY + 1, F),
    "tab4": (DUMMY + 1, F), "tab5": (DUMMY + 1, F),
    "q0": ((NT + 1) * P, H), "q1": ((NT + 1) * P, F), "q5": ((NT + 1) * P, P),
    "blk0": (NB, P + H), "blk1": (NB, F + H), "blk2": (NB, F), "blk3": (NB, F), "blk4": (NB, F), "blk5": (NB, P + H),
}


def kernel(**inputs):
    import numpy as np
    import concourse.bacc as bacc
    from concourse.bass_utils import run_bass_kernel_spmd as run

    nc = bacc.Bacc("TRN2", target_bir_lowering=False, num_devices=1)
    arrays, A = {}, {}
    for n, v in inputs.items():
        a = np.ascontiguousarray(v)
        arrays["in_" + n] = a
        A[n] = nc.dram_tensor("in_" + n, a.shape, mybir.dt.from_np(a.dtype), kind="ExternalInput").ap()
    D = {n: nc.dram_tensor("d_" + n, s, FP, kind="Internal").ap() for n, s in _SCRATCH.items()}
    for k in range(2):
        D[f"same{k}"] = nc.dram_tensor(f"d_same{k}", (NB,), U8, kind="Internal").ap()
        D[f"loc{k}"] = nc.dram_tensor(f"d_loc{k}", (NB,), U8, kind="Internal").ap()
        D[f"first{k}"] = nc.dram_tensor(f"d_first{k}", (G,), I32, kind="Internal").ap()
    o = nc.dram_tensor("out", (NODES, F), FP, kind="ExternalOutput").ap()
    build(nc, A, o, D)
    return run(nc, [arrays], core_ids=[0]).results[0]["out"]
```
